# Optimizing a Trainium2 kernel written in Bass

```python
import numpy as np
import jax
import jax.numpy as jnp

def _softmax(x, axis=-1):
    return jax.nn.softmax(x, axis=axis)

def _gelu(x):
    return jax.nn.gelu(x, approximate=True)

def _silu(x):
    return jax.nn.silu(x)

def _sigmoid(x):
    return jax.nn.sigmoid(x)

def _layernorm(x, axis=-1, eps=1e-05):
    m = jnp.mean(x, axis=axis, keepdims=True)
    v = jnp.var(x, axis=axis, keepdims=True)
    return (x - m) / jnp.sqrt(v + eps)

def _scatter_add(tgt, idx, src, axis=0):
    return tgt.at[idx].add(src)

def _segment_sum(src, seg, n):
    return jax.ops.segment_sum(src, seg, n)
kernel_name = 'mk_prb_d2_jaxref_r8_184e05'

def setup_inputs(seed: int=0):
    np.random.seed(seed)
    _w = jnp.asarray

    def _L0_attn_setup():
        import jax, jax.numpy as jnp
        import numpy as np
        import math
        D_MODEL, N_HEADS, D_K, D_C, D_HR = (128, 8, 128, 32, 32)
        B, S = (4, 256)
        key = jax.random.key(seed)
        ks = jax.random.split(key, 17)

        def lin(k, fan_in, fan_out):
            lim = 1.0 / math.sqrt(fan_in)
            kw, kb = jax.random.split(k)
            W = jax.random.uniform(kw, (fan_in, fan_out), jnp.float32, -lim, lim)
            b = jax.random.uniform(kb, (fan_out,), jnp.float32, -lim, lim)
            return (W, b)
        W_DQ, b_DQ = lin(ks[0], D_MODEL, D_C)
        W_UQ, b_UQ = lin(ks[1], D_C, N_HEADS * D_K)
        W_DKV, b_DKV = lin(ks[2], D_MODEL, D_C)
        W_UK, b_UK = lin(ks[3], D_C, N_HEADS * D_K)
        W_UV, b_UV = lin(ks[4], D_C, N_HEADS * D_K)
        W_QR, b_QR = lin(ks[5], D_C, N_HEADS * D_HR)
        W_KR, b_KR = lin(ks[6], D_MODEL, D_HR)
        W_O, b_O = lin(ks[7], N_HEADS * D_K, D_MODEL)
        h_t = jax.random.normal(ks[8], (B, S, D_MODEL), jnp.float32)
        return {'h_t': h_t, 'W_DQ': W_DQ, 'b_DQ': b_DQ, 'W_UQ': W_UQ, 'b_UQ': b_UQ, 'W_DKV': W_DKV, 'b_DKV': b_DKV, 'W_UK': W_UK, 'b_UK': b_UK, 'W_UV': W_UV, 'b_UV': b_UV, 'W_QR': W_QR, 'b_QR': b_QR, 'W_KR': W_KR, 'b_KR': b_KR, 'W_O': W_O, 'b_O': b_O}
    _L0_attn_in = _L0_attn_setup()

    def _L0_ffn_setup():
        import jax, jax.numpy as jnp
        import numpy as np
        JITTER_EPS = 0.01
        NEG_INF = -jnp.inf

        def sparsemixer_eval(scores, jitter_eps):
            m1 = jnp.max(scores, axis=-1, keepdims=True)
            ind1 = jnp.argmax(scores, axis=-1)
            factor1 = jnp.maximum(jnp.abs(scores), m1)
            mask1 = jax.lax.stop_gradient((m1 - scores) / factor1 > 2.0 * jitter_eps)
            gates1 = jax.nn.softmax(jnp.where(mask1, NEG_INF, scores), axis=-1)
            mult1 = jnp.take_along_axis(gates1, ind1[:, None], axis=-1)[:, 0]
            E = scores.shape[-1]
            onehot1 = ind1[:, None] == jnp.arange(E)[None, :]
            masked_scores = jnp.where(onehot1, NEG_INF, scores)
            m2 = jnp.max(masked_scores, axis=-1, keepdims=True)
            ind2 = jnp.argmax(masked_scores, axis=-1)
            factor2 = jnp.maximum(jnp.abs(scores), m2)
            mask2 = jax.lax.stop_gradient((m2 - scores) / factor2 > 2.0 * jitter_eps)
            gates2 = jax.nn.softmax(jnp.where(mask2, NEG_INF, masked_scores), axis=-1)
            mult2 = jnp.take_along_axis(gates2, ind2[:, None], axis=-1)[:, 0]
            multiplier = jnp.stack([mult1, mult2], axis=-1)
            selected = jnp.stack([ind1, ind2], axis=-1)
            return (multiplier, selected)
        key = jax.random.key(seed)
        k0, k1, k2, k3, k4 = jax.random.split(key, 5)
        B, S, H, F, E = (2, 128, 128, 256, 8)
        scale = 0.02
        return {'hidden_states': jax.random.normal(k0, (B, S, H), dtype=jnp.float32), 'router_w': jax.random.normal(k1, (E, H), dtype=jnp.float32) * scale, 'w_gate': jax.random.normal(k2, (E, F, H), dtype=jnp.float32) * scale, 'w_up': jax.random.normal(k3, (E, F, H), dtype=jnp.float32) * scale, 'w_down': jax.random.normal(k4, (E, H, F), dtype=jnp.float32) * scale}
    _L0_ffn_in = _L0_ffn_setup()

    def _L1_attn_setup():
        import jax, jax.numpy as jnp
        import numpy as np
        B, N, C, H = (4, 512, 128, 16)
        EPS = 1e-06
        key = jax.random.key(seed)
        k1, k2, k3 = jax.random.split(key, 3)
        x = jax.random.normal(k1, (B, N, C), dtype=jnp.float32)
        qkv_w = jax.random.normal(k2, (3 * C, C), dtype=jnp.float32) * 0.02
        qkv_b = jnp.zeros((3 * C,), dtype=jnp.float32)
        proj_w = jax.random.normal(k3, (C, C), dtype=jnp.float32) * 0.02
        proj_b = jnp.zeros((C,), dtype=jnp.float32)
        return {'x': x, 'qkv_w': qkv_w, 'qkv_b': qkv_b, 'proj_w': proj_w, 'proj_b': proj_b}
    _L1_attn_in = _L1_attn_setup()

    def _L1_ffn_setup():
        import jax, jax.numpy as jnp
        import numpy as np
        SWIGLU_ALPHA = 1.702
        SWIGLU_LIMIT = 7.0
        TOP_K = 4
        key = jax.random.key(seed)
        k = jax.random.split(key, 5)
        B, S, D, E, I = (2, 128, 128, 8, 256)
        return {'hidden_states': jax.random.normal(k[0], (B, S, D), dtype=jnp.float32), 'router_weight': jax.random.normal(k[1], (E, D), dtype=jnp.float32) * 0.02, 'router_bias': jnp.zeros((E,), dtype=jnp.float32), 'gate_up_proj': jax.random.normal(k[2], (E, 2 * I, D), dtype=jnp.float32) * 0.02, 'gate_up_proj_bias': jnp.zeros((E, 2 * I), dtype=jnp.float32), 'down_proj': jax.random.normal(k[3], (E, D, I), dtype=jnp.float32) * 0.02, 'down_proj_bias': jnp.zeros((E, D), dtype=jnp.float32)}
    _L1_ffn_in = _L1_ffn_setup()
    _d = {'L0_attn_h_t': _L0_attn_in['h_t'], 'L0_attn_W_DQ': _L0_attn_in['W_DQ'], 'L0_attn_b_DQ': _L0_attn_in['b_DQ'], 'L0_attn_W_UQ': _L0_attn_in['W_UQ'], 'L0_attn_b_UQ': _L0_attn_in['b_UQ'], 'L0_attn_W_DKV': _L0_attn_in['W_DKV'], 'L0_attn_b_DKV': _L0_attn_in['b_DKV'], 'L0_attn_W_UK': _L0_attn_in['W_UK'], 'L0_attn_b_UK': _L0_attn_in['b_UK'], 'L0_attn_W_UV': _L0_attn_in['W_UV'], 'L0_attn_b_UV': _L0_attn_in['b_UV'], 'L0_attn_W_QR': _L0_attn_in['W_QR'], 'L0_attn_b_QR': _L0_attn_in['b_QR'], 'L0_attn_W_KR': _L0_attn_in['W_KR'], 'L0_attn_b_KR': _L0_attn_in['b_KR'], 'L0_attn_W_O': _L0_attn_in['W_O'], 'L0_attn_b_O': _L0_attn_in['b_O'], 'L0_ffn_router_w': _L0_ffn_in['router_w'], 'L0_ffn_w_gate': _L0_ffn_in['w_gate'], 'L0_ffn_w_up': _L0_ffn_in['w_up'], 'L0_ffn_w_down': _L0_ffn_in['w_down'], 'L1_attn_qkv_w': _L1_attn_in['qkv_w'], 'L1_attn_qkv_b': _L1_attn_in['qkv_b'], 'L1_attn_proj_w': _L1_attn_in['proj_w'], 'L1_attn_proj_b': _L1_attn_in['proj_b'], 'L1_ffn_router_weight': _L1_ffn_in['router_weight'], 'L1_ffn_router_bias': _L1_ffn_in['router_bias'], 'L1_ffn_gate_up_proj': _L1_ffn_in['gate_up_proj'], 'L1_ffn_gate_up_proj_bias': _L1_ffn_in['gate_up_proj_bias'], 'L1_ffn_down_proj': _L1_ffn_in['down_proj'], 'L1_ffn_down_proj_bias': _L1_ffn_in['down_proj_bias']}
    _x0 = _d['L0_attn_h_t']
    _d['L0_attn_h_t'] = jax.random.normal(jax.random.fold_in(jax.random.key(seed), 1), (8, 1024, 128), dtype=_x0.dtype)
    del _x0
    return _d

def reference(L0_attn_h_t, L0_attn_W_DQ, L0_attn_b_DQ, L0_attn_W_UQ, L0_attn_b_UQ, L0_attn_W_DKV, L0_attn_b_DKV, L0_attn_W_UK, L0_attn_b_UK, L0_attn_W_UV, L0_attn_b_UV, L0_attn_W_QR, L0_attn_b_QR, L0_attn_W_KR, L0_attn_b_KR, L0_attn_W_O, L0_attn_b_O, L0_ffn_router_w, L0_ffn_w_gate, L0_ffn_w_up, L0_ffn_w_down, L1_attn_qkv_w, L1_attn_qkv_b, L1_attn_proj_w, L1_attn_proj_b, L1_ffn_router_weight, L1_ffn_router_bias, L1_ffn_gate_up_proj, L1_ffn_gate_up_proj_bias, L1_ffn_down_proj, L1_ffn_down_proj_bias):

    def _L0_attn_ref(h_t, W_DQ, b_DQ, W_UQ, b_UQ, W_DKV, b_DKV, W_UK, b_UK, W_UV, b_UV, W_QR, b_QR, W_KR, b_KR, W_O, b_O):
        import jax, jax.numpy as jnp
        import numpy as np
        import math
        D_MODEL, N_HEADS, D_K, D_C, D_HR = (128, 8, 128, 32, 32)
        B, S = (4, 256)
        b, s, _ = h_t.shape
        c_q = h_t @ W_DQ + b_DQ
        c_kv = h_t @ W_DKV + b_DKV
        q_c = (c_q @ W_UQ + b_UQ).reshape(b, s, N_HEADS, D_K).transpose(0, 2, 1, 3)
        k_c = (c_kv @ W_UK + b_UK).reshape(b, s, N_HEADS, D_K).transpose(0, 2, 1, 3)
        v_c = (c_kv @ W_UV + b_UV).reshape(b, s, N_HEADS, D_K).transpose(0, 2, 1, 3)
        q_r = (c_q @ W_QR + b_QR).reshape(b, s, N_HEADS, D_HR).transpose(0, 2, 1, 3)
        k_r = (h_t @ W_KR + b_KR)[:, None, :, :]
        k_r = jnp.broadcast_to(k_r, (b, N_HEADS, s, D_HR))
        q = jnp.concatenate([q_c, q_r], axis=-1)
        k = jnp.concatenate([k_c, k_r], axis=-1)
        scale = 1.0 / math.sqrt(D_K + D_HR)
        scores = jnp.einsum('bhsd,bhtd->bhst', q, k) * scale
        attn = jax.nn.softmax(scores, axis=-1)
        o = jnp.einsum('bhst,bhtd->bhsd', attn, v_c)
        o = o.transpose(0, 2, 1, 3).reshape(b, s, N_HEADS * D_K)
        return o @ W_O + b_O

    def _L0_ffn_ref(hidden_states, router_w, w_gate, w_up, w_down):
        import jax, jax.numpy as jnp
        import numpy as np
        JITTER_EPS = 0.01
        NEG_INF = -jnp.inf

        def sparsemixer_eval(scores, jitter_eps):
            m1 = jnp.max(scores, axis=-1, keepdims=True)
            ind1 = jnp.argmax(scores, axis=-1)
            factor1 = jnp.maximum(jnp.abs(scores), m1)
            mask1 = jax.lax.stop_gradient((m1 - scores) / factor1 > 2.0 * jitter_eps)
            gates1 = jax.nn.softmax(jnp.where(mask1, NEG_INF, scores), axis=-1)
            mult1 = jnp.take_along_axis(gates1, ind1[:, None], axis=-1)[:, 0]
            E = scores.shape[-1]
            onehot1 = ind1[:, None] == jnp.arange(E)[None, :]
            masked_scores = jnp.where(onehot1, NEG_INF, scores)
            m2 = jnp.max(masked_scores, axis=-1, keepdims=True)
            ind2 = jnp.argmax(masked_scores, axis=-1)
            factor2 = jnp.maximum(jnp.abs(scores), m2)
            mask2 = jax.lax.stop_gradient((m2 - scores) / factor2 > 2.0 * jitter_eps)
            gates2 = jax.nn.softmax(jnp.where(mask2, NEG_INF, masked_scores), axis=-1)
            mult2 = jnp.take_along_axis(gates2, ind2[:, None], axis=-1)[:, 0]
            multiplier = jnp.stack([mult1, mult2], axis=-1)
            selected = jnp.stack([ind1, ind2], axis=-1)
            return (multiplier, selected)
        B, S, H = hidden_states.shape
        E = router_w.shape[0]
        x = hidden_states.reshape(-1, H)
        T = x.shape[0]
        logits = x @ router_w.T
        routing_weights, selected = sparsemixer_eval(logits, JITTER_EPS)
        tok = jnp.arange(T)
        dense_w = jnp.zeros((T, E), dtype=x.dtype)
        dense_w = dense_w.at[tok, selected[:, 0]].add(routing_weights[:, 0])
        dense_w = dense_w.at[tok, selected[:, 1]].add(routing_weights[:, 1])
        out = jnp.zeros_like(x)
        for e in range(E):
            h = jax.nn.silu(x @ w_gate[e].T) * (x @ w_up[e].T)
            out = out + dense_w[:, e:e + 1] * (h @ w_down[e].T)
        return out.reshape(B, S, H)

    def _L1_attn_ref(x, qkv_w, qkv_b, proj_w, proj_b):
        import jax, jax.numpy as jnp
        import numpy as np
        B, N, C, H = (4, 512, 128, 16)
        EPS = 1e-06
        b, n, c = x.shape
        d = c // H
        qkv = x @ qkv_w.T + qkv_b
        qkv = qkv.reshape(b, n, 3, H, d).transpose(2, 0, 3, 1, 4)
        q, k, v = (qkv[0], qkv[1], qkv[2])
        q = jax.nn.sigmoid(q)
        k = jax.nn.sigmoid(k)
        k_sum = k.sum(axis=2)
        sink_incoming = 1.0 / jnp.sum((q + EPS) * (k_sum[:, :, None, :] + EPS), axis=-1)
        q_sum = q.sum(axis=2)
        source_outgoing = 1.0 / jnp.sum((k + EPS) * (q_sum[:, :, None, :] + EPS), axis=-1)
        k_so_sum = (k * source_outgoing[..., None]).sum(axis=2, keepdims=True)
        conserved_sink = jnp.sum((q + EPS) * (k_so_sum + EPS), axis=-1) + EPS
        q_si_sum = (q * sink_incoming[..., None]).sum(axis=2, keepdims=True)
        conserved_source = jnp.sum((k + EPS) * (q_si_sum + EPS), axis=-1) + EPS
        conserved_source = jnp.clip(conserved_source, -1.0, 1.0)
        ratio = float(n) / float(n)
        sink_allocation = jax.nn.sigmoid(conserved_sink * ratio)
        source_competition = jax.nn.softmax(conserved_source, axis=-1) * float(n)
        q_norm = q * sink_incoming[..., None]
        v_comp = v * source_competition[..., None]
        kv = jnp.einsum('bhnd,bhnm->bhdm', k, v_comp)
        out = jnp.einsum('bhnd,bhdm->bhnm', q_norm, kv)
        out = out * sink_allocation[..., None]
        out = out.transpose(0, 2, 1, 3).reshape(b, n, c)
        out = out @ proj_w.T + proj_b
        return out

    def _L1_ffn_ref(hidden_states, router_weight, router_bias, gate_up_proj, gate_up_proj_bias, down_proj, down_proj_bias):
        import jax, jax.numpy as jnp
        import numpy as np
        SWIGLU_ALPHA = 1.702
        SWIGLU_LIMIT = 7.0
        TOP_K = 4
        B, S, D = hidden_states.shape
        E = router_weight.shape[0]
        x = hidden_states.reshape(-1, D)
        N = x.shape[0]
        logits = x @ router_weight.T + router_bias
        topk_logits, topk_idx = jax.lax.top_k(logits, TOP_K)
        topk_w = jax.nn.softmax(topk_logits.astype(jnp.float32), axis=-1)
        combine = jnp.zeros((N, E), dtype=jnp.float32)
        combine = combine.at[jnp.arange(N)[:, None], topk_idx].set(topk_w)
        gate_up = jnp.einsum('nd,ejd->nej', x, gate_up_proj) + gate_up_proj_bias
        gate, up = jnp.split(gate_up, 2, axis=-1)
        gate = jnp.minimum(gate, SWIGLU_LIMIT)
        up = jnp.clip(up, -SWIGLU_LIMIT, SWIGLU_LIMIT)
        act = (up + 1.0) * gate * jax.nn.sigmoid(SWIGLU_ALPHA * gate)
        out = jnp.einsum('nei,edi->ned', act, down_proj) + down_proj_bias
        y = jnp.einsum('ned,ne->nd', out, combine.astype(out.dtype))
        return y.reshape(B, S, D)
    x = L0_attn_h_t
    xn = _layernorm(x, axis=-1)
    x = x + _L0_attn_ref(xn, L0_attn_W_DQ, L0_attn_b_DQ, L0_attn_W_UQ, L0_attn_b_UQ, L0_attn_W_DKV, L0_attn_b_DKV, L0_attn_W_UK, L0_attn_b_UK, L0_attn_W_UV, L0_attn_b_UV, L0_attn_W_QR, L0_attn_b_QR, L0_attn_W_KR, L0_attn_b_KR, L0_attn_W_O, L0_attn_b_O) + _L0_ffn_ref(xn, L0_ffn_router_w, L0_ffn_w_gate, L0_ffn_w_up, L0_ffn_w_down)
    xn = _layernorm(x, axis=-1)
    x = x + _L1_attn_ref(xn, L1_attn_qkv_w, L1_attn_qkv_b, L1_attn_proj_w, L1_attn_proj_b) + _L1_ffn_ref(xn, L1_ffn_router_weight, L1_ffn_router_bias, L1_ffn_gate_up_proj, L1_ffn_gate_up_proj_bias, L1_ffn_down_proj, L1_ffn_down_proj_bias)
    return x

_drawn_inputs = setup_inputs


def setup_inputs(seed=0):
    import zlib

    import numpy as np

    out = dict(_drawn_inputs(seed))
    spreads = {'L1_attn_qkv_b': (0.0, 0.519),
     'L1_attn_proj_b': (0.0, 0.433),
     'L1_ffn_router_bias': (0.0, 1.35),
     'L1_ffn_gate_up_proj_bias': (0.0, 2.0),
     'L1_ffn_down_proj_bias': (0.0, 0.8)}
    factors = {'L0_attn_W_DQ': 8.0,
     'L0_attn_b_DQ': 8.0,
     'L0_attn_W_UQ': 8.0,
     'L0_attn_b_UQ': 8.0,
     'L0_attn_W_DKV': 7.698,
     'L0_attn_b_DKV': 4.113,
     'L0_attn_W_UK': 8.0,
     'L0_attn_b_UK': 64.0,
     'L0_attn_W_UV': 3.182,
     'L0_attn_W_QR': 8.0,
     'L0_attn_b_QR': 8.0,
     'L0_attn_W_KR': 8.0,
     'L0_attn_b_KR': 64.0,
     'L0_attn_b_O': 16.408,
     'L0_ffn_router_w': 5.291,
     'L0_ffn_w_gate': 4.667,
     'L0_ffn_w_up': 4.678,
     'L0_ffn_w_down': 4.661,
     'L1_attn_qkv_w': 22.108,
     'L1_attn_proj_w': 3.561,
     'L1_ffn_gate_up_proj': 8.1,
     'L0_attn_b_UV': 5.099,
     'L1_ffn_router_weight': 3.237}
    for name, (base, spread) in spreads.items():
        noise = np.random.default_rng([zlib.crc32(name.encode()), seed]).standard_normal(out[name].shape)
        drawn = base * np.exp(spread * noise) if base else spread * noise
        out[name] = jnp.asarray(drawn.astype(out[name].dtype))
    for name, factor in factors.items():
        out[name] = (out[name] * factor).astype(out[name].dtype)
    return out
```

```python
from contextlib import ExitStack

import numpy as np

import concourse.bass as bass
from concourse import mybir

F32 = mybir.dt.float32
F32R = mybir.dt.float32r
ALU = mybir.AluOpType
ACT = mybir.ActivationFunctionType
X = mybir.AxisListType.X

P = 128
BATCH = 8
SEQ = 1024
NT = SEQ // P
D = 128
BANK = 512
HALVES = SEQ // BANK
LN_EPS = 1e-5

H0, DK, DC, DR = 8, 128, 32, 32
KD = DC + DR
SCALE = 1.0 / float(np.sqrt(DK + DR))
QUAD = P // DC
QUADS = H0 // QUAD
GROUPS = QUADS * NT
TILES = GROUPS * QUAD

H1, D1 = 16, 8
EPS1 = 1e-6

E, F = 8, 256
FH = F // P
UNITS = E * FH * HALVES
JITTER2 = 0.02
TOP_K = 4
ALPHA, LIMIT = 1.702, 7.0
MINUS_INF = -3.0e38

DVE_STEPS = 62
POOL_STEPS = 16


class Signal:

    def __init__(self, sem, per, start):
        self.sem, self.per, self.start = sem, per, start

    def at(self, b, k):
        return b.times(self.per) + (self.start + k)


class Sequence:

    def __init__(self, engine, index):
        self.engine, self.index, self.products = engine, index, {}

    def times(self, n):
        if n not in self.products:
            self.products[n] = self.engine.snap(self.index * n)
        return self.products[n]


def two_layer_kernel(nc, ins, out):
    with ExitStack() as ctx:
        def sb(name, shape, dt=F32):
            return ctx.enter_context(nc.sbuf_tensor(name, shape, dt))

        def signal(name, per=0, start=0):
            return Signal(ctx.enter_context(nc.semaphore(name)), per, start)

        x_in = sb("x_in", [P, NT, D])
        x_mid = sb("x_mid", [P, NT, D])
        x_norm = sb("x_norm", [P, NT, D])
        xT = sb("xT", [P, SEQ])
        stats = sb("stats", [P, NT, 6])
        mean_var = sb("mean_var", [P, NT, 2])
        var_eps = sb("var_eps", [P, NT])
        rstd = sb("rstd", [P, NT])
        spare = sb("spare", [P, 2])
        minus_half = sb("minus_half", [P, NT])

        keys = sb("keys", [P, SEQ], F32R)
        q_parts = sb("q_parts", [P, QUAD, 2, SEQ], F32R)
        probs = sb("probs", [P, 2, SEQ])
        probsT = sb("probsT", [P, 2 * QUAD, SEQ])
        latent = sb("latent", [P, NT, DC])
        neg_max = sb("neg_max", [P, 4])
        row_sum = sb("row_sum", [P, 2, QUAD])
        inv_sum = sb("inv_sum", [P, 2, QUAD])
        scale_sb = sb("scale_sb", [P, 2, P])
        o_latent = sb("o_latent", [P, 2, P])

        room = probsT[:, :, :].rearrange("p a b -> p (a b)")
        qkv = room[:, 0:NT * 3 * D].rearrange("p (n c) -> p n c", n=NT)
        weighted = room[:, 3 * SEQ:5 * SEQ].rearrange("p (n c) -> p n c", n=NT)
        tmp = room[:, 5 * SEQ:6 * SEQ].rearrange("p (n c) -> p n c", n=NT)
        v_comp = room[:, 6 * SEQ:7 * SEQ].rearrange("p (n c) -> p n c", n=NT)
        q_normT = room[:, 7 * SEQ:8 * SEQ]
        heads_out, heads_outT = tmp, room[:, 6 * SEQ:7 * SEQ]
        sums_eps = sb("sums_eps", [P, 2 * D])
        sums2_eps = sb("sums2_eps", [P, 2 * D])
        inv_flow = sb("inv_flow", [P, 2, NT * H1])
        conserved = sb("conserved", [P, 2, NT * H1])
        sink_alloc = sb("sink_alloc", [P, NT * H1])
        source_exp = sb("source_exp", [P, NT * H1])
        source_inv = sb("source_inv", [P, H1])
        kv = sb("kv", [P, D])

        logits = sb("logits", [P, NT, E])
        gate_w = sb("gate_w", [P, NT, E])
        r_a, r_b, r_c, r_d, r_e = (sb(f"r_{c}", [P, NT, E]) for c in "abcde")
        rank = sb("rank", [P, NT, E])
        top1, top2, r_s1, r_s2 = (sb(f"top_{c}", [P, NT]) for c in "abcd")
        pair_a, pair_b = (probs[:, 1, c * BANK:(c + 1) * BANK].rearrange("p (n e j) -> p n e j", n=NT, e=E)
                          for c in range(2))
        r_exp = sb("r_exp", [P, 2, NT, E])
        gate_wT = sb("gate_wT", [E, SEQ])
        gate_rows = sb("gate_rows", [P, E // 4, SEQ])
        gate_bc = sb("gate_bc", [P, 2, SEQ])
        ffn_t = sb("ffn_t", [P, 2, BANK])
        ffn_g = sb("ffn_g", [P, 2, BANK])
        ffn_u = sb("ffn_u", [P, 2, BANK])
        ffn_gu = sb("ffn_gu", [P, 2, BANK])
        ffn_h = sb("ffn_h", [P, 2, BANK])
        y_T = probs[:, 0, :]

        ident = sb("ident", [P, P])
        ones = sb("ones", [P, P])
        same_head = sb("same_head", [P, H1, D1])
        earlier = sb("earlier", [P, E, E])
        w_q = sb("w_q", [P, H0, P])
        b_q = sb("b_q", [P, H0])
        w_k = sb("w_k", [P, P])
        b_k = sb("b_k", [P, 1])
        w_dkv = sb("w_dkv", [P, DC])
        b_dkv = sb("b_dkv", [P, DC])
        w_o = sb("w_o", [P, QUADS, D])
        b_o = sb("b_o", [P, D])
        w_gate = [sb(f"w_gate{l}", [P, E * F]) for l in range(2)]
        w_up = [sb(f"w_up{l}", [P, E * F]) for l in range(2)]
        w_down = [sb(f"w_down{l}", [P, E * FH, D]) for l in range(2)]
        w_router = [sb(f"w_router{l}", [P, E]) for l in range(2)]
        b_router = sb("b_router", [P, E])
        b_gate = sb("b_gate", [P, E * FH])
        b_up = sb("b_up", [P, E * FH])
        b_down = sb("b_down", [E, D])
        w_qkv = sb("w_qkv", [P, 3 * D])
        b_qkv = sb("b_qkv", [P, 3 * D])
        w_proj = sb("w_proj", [P, D])
        b_proj = sb("b_proj", [P, D])

        take = [0]

        def prep(parts, *shape):
            n = int(np.prod(shape))
            v = room[0:parts, take[0]:take[0] + n]
            take[0] += n
            return v.rearrange("p (a b) -> p a b", a=shape[0]) if len(shape) > 1 else v

        uq_T = prep(P, H0, DC + 1)
        uk_T = prep(P, H0, DC)
        uv_T = prep(P, H0, DC)
        wo_heads = prep(P, H0, D)
        b_uv = prep(P, H0)
        dq_T = prep(DC, D)
        b_dq1 = prep(DC + 1, 1)
        q_rope = prep(DC + 1, H0, DR)
        absorbed = prep(DC + 1, H0, P)
        b_o_in = prep(P, D)

        ps = ctx.enter_context(nc.psum_tensor("ps", [P, 8, BANK], F32))

        def banks(a, n=2):
            return ps[:, a:a + n, :].rearrange("p a b -> p (a b)")

        weights_in = signal("weights_in")
        pool_consts = signal("pool_consts")
        prep_mm = signal("prep_mm")
        prep_sb = signal("prep_sb")
        prep_act = signal("prep_act")
        x_loaded = signal("x_loaded", 16)
        x_taken = signal("x_taken", 1, start=1)
        y_stored = signal("y_stored", 16, start=1)
        y_done = signal("y_done", 1)
        dve_step = signal("dve_step", DVE_STEPS)
        pool_step = signal("pool_step", POOL_STEPS)
        pool_carrier = signal("pool_carrier")
        var_ready = signal("var_ready", 2)
        rstd_ready = signal("rstd_ready", 2)
        norm_ready = signal("norm_ready", 2 * NT)
        normT_ready = signal("normT_ready", 4)
        xT_ready = signal("xT_ready", 4)
        k_proj = signal("k_proj", 1)
        keys_ready = signal("keys_ready", 1)
        latent_mm = signal("latent_mm", 1)
        latent_ready = signal("latent_ready", 1)
        q_proj = signal("q_proj", H0)
        q_high = signal("q_high", H0)
        q_ready = signal("q_ready", H0)
        scores_ready = signal("scores_ready", TILES)
        max_ready = signal("max_ready", TILES)
        exp_done = signal("exp_done", TILES)
        pT_low = signal("pT_low", TILES)
        pT_high = signal("pT_high", TILES)
        low_copied = signal("low_copied", TILES)
        high_copied = signal("high_copied", TILES)
        inv_ready = signal("inv_ready", GROUPS)
        u_ready = signal("u_ready", GROUPS)
        scale_ready = signal("scale_ready", GROUPS)
        u_scaled = signal("u_scaled", GROUPS)
        o_ready = signal("o_ready", GROUPS)
        o_added = signal("o_added", GROUPS)
        logits_mm = signal("logits_mm", 2)
        shift_ready = signal("shift_ready", 3)
        r_exp_done = signal("r_exp_done", 3)
        gate_ready = signal("gate_ready", 2)
        gateT_mm = signal("gateT_mm", 2)
        gateT_ready = signal("gateT_ready", 2)
        rows_ready = signal("rows_ready", 64)
        gu_ready = signal("gu_ready", 2 * UNITS)
        gate_lim = signal("gate_lim", UNITS)
        tanh_done = signal("tanh_done", 2 * UNITS)
        up_copied = signal("up_copied", UNITS)
        g_free = signal("g_free", 2 * UNITS)
        gu_done = signal("gu_done", 2 * UNITS)
        h_ready = signal("h_ready", 2 * UNITS)
        down_done = signal("down_done", 2 * UNITS)
        yT_ready = signal("yT_ready", 4)
        y_mm = signal("y_mm", 4)
        y_added = signal("y_added", 2)
        qkv_mm = signal("qkv_mm", NT)
        z_ready = signal("z_ready", NT)
        sig_tanh = signal("sig_tanh", 1)
        qk_ready = signal("qk_ready", 1)
        sums_mm = signal("sums_mm", 2)
        weighted_ready = signal("weighted_ready", 1)
        qnT_mm = signal("qnT_mm", 2)
        qnT_ready = signal("qnT_ready", 2)
        conserved_ready = signal("conserved_ready", 1)
        flow_act = signal("flow_act", 2)
        v_ready = signal("v_ready", 1)
        kv_mm = signal("kv_mm", 1)
        kv_ready = signal("kv_ready", 1)
        heads_mm = signal("heads_mm", 2)
        heads_ready = signal("heads_ready", 2)
        headsT_mm = signal("headsT_mm", 2)
        headsT_ready = signal("headsT_ready", 2)
        proj_mm = signal("proj_mm", 2)
        proj_added = signal("proj_added", 2)

        loads = [
            (uq_T, "UQ_T"), (uk_T, "UK_T"), (uv_T, "UV_T"), (wo_heads, "W_O"), (b_uv, "b_UV"), (dq_T, "DQ_T"),
            (b_dq1, "b_DQ1"), (q_rope, "Q_rope"), (w_k[:, :], "W_K"), (b_k[:, :], "b_K"), (w_dkv[:, :], "W_DKV"),
            (w_gate[0][:, :], "gate0"), (w_up[0][:, :], "up0"), (w_down[0][:, :, :], "down0"),
            (w_router[0][:, :], "router0"), (w_qkv[:, :], "W_QKV"), (w_proj[:, :], "W_PROJ"),
            (w_gate[1][:, :], "gate1"), (w_up[1][:, :], "up1"), (w_down[1][:, :, :], "down1"),
            (w_router[1][:, :], "router1"), (b_gate[:, :], "b_gate"), (b_up[:, :], "b_up"), (b_down[:, :], "b_down"),
        ]
        rows = [(b_dkv, "b_DKV", DC), (b_o_in, "b_O", D), (b_qkv, "b_QKV", 3 * D), (b_proj, "b_PROJ", D),
                (b_router, "b_ROUTER", E)]
        ALL_WEIGHTS = 16 * (len(loads) + len(rows))

        block = ctx.enter_context(nc.Block())

        @block.sync
        def _(sp):
            for dst, name in loads:
                sp.dma_start(dst, ins[name]).then_inc(weights_in.sem, 16)
            for dst, name, n in rows:
                sp.dma_start(dst[:, 0:n], ins[name].partition_broadcast(P)).then_inc(weights_in.sem, 16)
            sp.sem_inc(x_taken.sem, 1)
            sp.sem_inc(y_stored.sem, 1)
            with sp.Fori(0, BATCH) as index:
                b = Sequence(sp, index)
                sp.wait_ge(x_taken.sem, x_taken.at(b, 0))
                sp.dma_start(x_in[:, :, :], ins["x"][bass.ds(index, 1), :, :].rearrange("a (n p) d -> p (a n) d", p=P)
                             ).then_inc(x_loaded.sem, 16)
                for l in range(2):
                    sp.wait_ge(gateT_ready.sem, gateT_ready.at(b, l + 1))
                    for g in range(E // 4):
                        sp.dma_start(gate_rows[0:97:32, g, :], gate_wT[4 * g:4 * g + 4, :]).then_inc(rows_ready.sem, 16)
                sp.wait_ge(y_done.sem, y_done.at(b, 1))
                sp.dma_start(out[bass.ds(index, 1), :, :].rearrange("a (n p) d -> p (a n) d", p=P), x_mid[:, :, :]
                             ).then_inc(y_stored.sem, 16)
            sp.wait_ge(y_stored.sem, y_stored.per * BATCH + 1)

        @block.gpsimd
        def _(pool):
            nc.gpsimd.memset(minus_half[:, :], -0.5).then_inc(pool_consts.sem, 1)
            nc.gpsimd.memset(ident[:, :], 0.0).then_inc(pool_consts.sem, 1)
            nc.gpsimd.memset(ones[:, :], 1.0).then_inc(pool_consts.sem, 1)
            nc.gpsimd.memset(same_head[:, :, :], 1.0).then_inc(pool_consts.sem, 1)
            nc.gpsimd.memset(earlier[:, :, :], 1.0).then_inc(pool_consts.sem, 1)
            pool.wait_ge(pool_consts.sem, 5)
            nc.gpsimd.affine_select(out=ident[:, :], in_=ident[:, :], compare_op=ALU.not_equal, fill=1.0, base=0,
                                    pattern=[[-1, P]], channel_multiplier=1).then_inc(pool_consts.sem, 1)
            nc.gpsimd.affine_select(out=same_head[:, :, :], in_=same_head[:, :, :], compare_op=ALU.is_ge, fill=0.0,
                                    base=0, pattern=[[-D1, H1], [0, D1]], channel_multiplier=1
                                    ).then_inc(pool_consts.sem, 1)
            pool.wait_ge(pool_consts.sem, 7)
            nc.gpsimd.affine_select(out=same_head[:, :, :], in_=same_head[:, :, :], compare_op=ALU.is_ge, fill=0.0,
                                    base=D1 - 1, pattern=[[D1, H1], [0, D1]], channel_multiplier=-1
                                    ).then_inc(pool_consts.sem, 1)
            nc.gpsimd.affine_select(out=earlier[:, :, :], in_=earlier[:, :, :], compare_op=ALU.is_ge, fill=0.0,
                                    base=-1, pattern=[[1, E], [-1, E]], channel_multiplier=0
                                    ).then_inc(pool_consts.sem, 1)

            with pool.Fori(0, BATCH) as index:
                b = Sequence(pool, index)
                steps = 0
                for l in range(2):
                    pool.wait_ge(var_ready.sem, var_ready.at(b, l + 1))
                    nc.gpsimd.tensor_tensor(rstd[:, :], var_eps[:, :], minus_half[:, :], ALU.pow
                                            ).then_inc(rstd_ready.sem, 1)
                    for u in range(UNITS):
                        e, c = u // (FH * HALVES), u % HALVES
                        if u % (FH * HALVES) == 0:
                            if e == 0:
                                pool.wait_ge(rows_ready.sem, rows_ready.at(b, 32 * (l + 1)))
                            if e >= 1:
                                pool.wait_ge(h_ready.sem, h_ready.at(b, l * UNITS + e * FH * HALVES))
                            pool.sem_inc(pool_carrier.sem, 1)
                            nc.gpsimd.partition_broadcast(
                                gate_bc[:, e % 2, :], gate_rows[32 * (e % 4):32 * (e % 4) + 1, e // 4, :]
                            ).then_inc(pool_step.sem, 1)
                            steps += 1
                            pool.wait_ge(pool_step.sem, pool_step.at(b, steps))
                        pool.wait_ge(gu_done.sem, gu_done.at(b, l * UNITS + u + 1))
                        if l * UNITS + u >= 2:
                            pool.wait_ge(down_done.sem, down_done.at(b, l * UNITS + u - 1))
                        nc.gpsimd.tensor_tensor(ffn_h[:, u % 2, :], ffn_gu[:, u % 2, :],
                                                gate_bc[:, e % 2, c * BANK:(c + 1) * BANK], ALU.mult
                                                ).then_inc(h_ready.sem, 1)
                assert steps == POOL_STEPS, steps

        @block.scalar
        def _(act):
            act.wait_ge(weights_in.sem, ALL_WEIGHTS)
            for l in range(2):
                nc.scalar.mul(w_down[l][:, :, :], w_down[l][:, :, :], 0.5).then_inc(prep_act.sem, 1)

            def copy_xT(b, l):
                for c in range(2):
                    act.wait_ge(normT_ready.sem, normT_ready.at(b, 2 * l + c + 1))
                    nc.scalar.copy(xT[:, c * BANK:(c + 1) * BANK], ps[:, 4 + c, :]).then_inc(xT_ready.sem, 1)

            def gates(b, l):
                for k in range([0, 2][l], [2, 3][l]):
                    act.wait_ge(shift_ready.sem, shift_ready.at(b, k + 1))
                    src = r_c if k == 1 else r_a
                    nc.scalar.activation(r_exp[:, k % 2, :, :], src[:, :, :], ACT.Exp).then_inc(r_exp_done.sem, 1)
                act.wait_ge(gateT_mm.sem, gateT_mm.at(b, l + 1))
                nc.scalar.copy(gate_wT[:, :], banks(4)[0:E, :]).then_inc(gateT_ready.sem, 1)

            def experts_out(b, l):
                for c in range(HALVES):
                    act.wait_ge(down_done.sem, down_done.at(b, (l + 1) * UNITS))
                    nc.scalar.copy(y_T[:, c * BANK:(c + 1) * BANK], ps[:, 4 + c, :]).then_inc(yT_ready.sem, 1)

            with act.Fori(0, BATCH) as index:
                b = Sequence(act, index)
                copy_xT(b, 0)

                def query_high(h):
                    act.wait_ge(q_proj.sem, q_proj.at(b, h + 1))
                    nc.scalar.activation(q_parts[:, h % QUAD, 0, :], banks(2 * (h % 2)), ACT.Identity,
                                         bias=b_q[:, h:h + 1]).then_inc(q_high.sem, 1)

                for quad in range(QUADS):
                    for j in range(QUAD):
                        query_high(quad * QUAD + j)
                    for s in range(NT * QUAD + 3):
                        if s < NT * QUAD:
                            t = quad * NT * QUAD + s
                            act.wait_ge(max_ready.sem, max_ready.at(b, t + 1))
                            if t >= 2:
                                act.wait_ge(pT_high.sem, pT_high.at(b, t - 1))
                            g = t // QUAD
                            if g >= 2 and t % QUAD == 0:
                                act.wait_ge(inv_ready.sem, inv_ready.at(b, g - 1))
                            nc.scalar.activation(probs[:, t % 2, :], banks(2 * (t % 2)), ACT.Exp,
                                                 bias=neg_max[:, t % 4:t % 4 + 1],
                                                 accum_out=row_sum[:, g % 2, t % QUAD:t % QUAD + 1]
                                                 ).then_inc(exp_done.sem, 1)
                        if 1 <= s <= NT * QUAD:
                            t = quad * NT * QUAD + s - 1
                            act.wait_ge(pT_low.sem, pT_low.at(b, t + 1))
                            if t >= 2 * QUAD:
                                act.wait_ge(u_ready.sem, u_ready.at(b, t // QUAD - 1))
                            nc.scalar.copy(probsT[:, t % (2 * QUAD), 0:BANK], ps[:, 4, :]).then_inc(low_copied.sem, 1)
                        if s >= QUAD + 2 and (s - 2) % QUAD == 0:
                            g = quad * NT + (s - 2) // QUAD - 1
                            act.wait_ge(u_ready.sem, u_ready.at(b, g + 1))
                            if g >= 2:
                                act.wait_ge(u_scaled.sem, u_scaled.at(b, g - 1))
                            nc.scalar.copy(scale_sb[:, g % 2, :], ps[:, 6, 256 + 128 * (g % 2):384 + 128 * (g % 2)]
                                           ).then_inc(scale_ready.sem, 1)

                gates(b, 0)
                for u in range(UNITS):
                    act.wait_ge(gu_ready.sem, gu_ready.at(b, u + 1))
                    if u >= 2:
                        act.wait_ge(g_free.sem, g_free.at(b, u - 1))
                    nc.scalar.activation(ffn_t[:, u % 2, :], ps[:, u % 2, :], ACT.Tanh, scale=0.5
                                         ).then_inc(tanh_done.sem, 1)
                experts_out(b, 0)

                copy_xT(b, 1)
                act.wait_ge(z_ready.sem, z_ready.at(b, NT))
                nc.scalar.activation(qkv[:, :, 0:2 * D], qkv[:, :, 0:2 * D], ACT.Tanh, scale=0.5
                                     ).then_inc(sig_tanh.sem, 1)
                for c in range(2):
                    act.wait_ge(qnT_mm.sem, qnT_mm.at(b, c + 1))
                    nc.scalar.copy(q_normT[:, c * BANK:(c + 1) * BANK], ps[:, [6, 2][c], :]).then_inc(qnT_ready.sem, 1)
                act.wait_ge(conserved_ready.sem, conserved_ready.at(b, 1))
                nc.scalar.activation(sink_alloc[:, :], conserved[:, 0, :], ACT.Tanh, scale=0.5
                                     ).then_inc(flow_act.sem, 1)
                nc.scalar.activation(source_exp[:, :], conserved[:, 1, :], ACT.Exp).then_inc(flow_act.sem, 1)
                for c in range(2):
                    act.wait_ge(headsT_mm.sem, headsT_mm.at(b, c + 1))
                    nc.scalar.copy(heads_outT[:, c * BANK:(c + 1) * BANK], ps[:, 4 + c, :]
                                   ).then_inc(headsT_ready.sem, 1)
                gates(b, 1)
                for u in range(UNITS):
                    if u >= 2:
                        act.wait_ge(gu_done.sem, gu_done.at(b, UNITS + u - 1))
                    act.wait_ge(gu_ready.sem, gu_ready.at(b, UNITS + u + 1))
                    f = u // HALVES
                    nc.scalar.activation(ffn_u[:, u % 2, :], ps[:, 2 + u % 2, :], ACT.Identity,
                                         bias=b_up[:, f:f + 1]).then_inc(up_copied.sem, 1)
                    act.wait_ge(gate_lim.sem, gate_lim.at(b, u + 1))
                    nc.scalar.activation(ffn_t[:, u % 2, :], ffn_g[:, u % 2, :], ACT.Tanh, scale=0.5 * ALPHA
                                         ).then_inc(tanh_done.sem, 1)
                experts_out(b, 1)

        @block.vector
        def _(dve):
            dve.wait_ge(weights_in.sem, ALL_WEIGHTS)
            dve.wait_ge(prep_mm.sem, 1)
            for h in range(H0):
                for half in range(2):
                    nc.vector.tensor_scalar(absorbed[:, h, half * KD:half * KD + DC],
                                            ps[0:DC + 1, 0, h * DC:(h + 1) * DC], SCALE, None, ALU.mult)
                    last = nc.vector.tensor_scalar(absorbed[:, h, half * KD + DC:(half + 1) * KD], q_rope[:, h, :],
                                                   SCALE, None, ALU.mult)
                last.then_inc(prep_sb.sem, 1)
            dve.wait_ge(prep_mm.sem, 2)
            nc.vector.tensor_copy(w_q[:, :, :].rearrange("p a b -> p (a b)"), banks(2)).then_inc(prep_sb.sem, 1)
            nc.vector.tensor_copy(b_q[:, :], ps[:, 1, 0:H0]).then_inc(prep_sb.sem, 1)
            nc.vector.tensor_copy(w_o[:, :, :].rearrange("p a b -> p (a b)"), ps[:, 4, 0:QUADS * D]
                                  ).then_inc(prep_sb.sem, 1)
            nc.vector.tensor_tensor(b_o[:, :], ps[:, 5, 0:D], b_o_in, ALU.add).then_inc(prep_sb.sem, 1)
            nc.vector.tensor_scalar(b_up[:, :], b_up[:, :], 1.0, None, ALU.add).then_inc(prep_sb.sem, 1)
            dve.wait_ge(prep_sb.sem, H0 + 5)

            with dve.Fori(0, BATCH) as index:
                b = Sequence(dve, index)
                count = [0]

                def link(ins, aggregates_next=False):
                    count[0] += 1
                    ins.then_inc(dve_step.sem, 1)
                    dve.wait_ge(dve_step.sem, dve_step.at(b, count[0]))
                    if aggregates_next:
                        nc.vector.memset(spare[:, 0:1], 0.0)

                def layer_norm(l, x):
                    for n in range(NT):
                        last = nc.vector.bn_stats(stats[:, n, :], x[:, n, :])
                    link(last, aggregates_next=True)
                    for n in range(NT):
                        last = nc.vector.bn_aggr(mean_var[:, n, :], stats[:, n, :])
                    link(last)
                    nc.vector.tensor_scalar(var_eps[:, :], mean_var[:, :, 1], LN_EPS, None, ALU.add
                                            ).then_inc(var_ready.sem, 1)
                    dve.wait_ge(rstd_ready.sem, rstd_ready.at(b, l + 1))
                    for n in range(NT):
                        nc.vector.tensor_scalar(x_norm[:, n, :], x[:, n, :], mean_var[:, n, 0:1], rstd[:, n:n + 1],
                                                ALU.subtract, ALU.mult).then_inc(norm_ready.sem, 1)

                def wide(v):
                    return v.unsqueeze(2).to_broadcast([P, NT, E])

                def ranks():
                    by_j = logits[:, :, :].unsqueeze(2).to_broadcast([P, NT, E, E])
                    by_e = logits[:, :, :].unsqueeze(3).to_broadcast([P, NT, E, E])
                    nc.vector.tensor_tensor(pair_a, by_j, by_e, ALU.is_gt)
                    link(nc.vector.tensor_tensor(pair_b, by_j, by_e, ALU.is_equal))
                    link(nc.vector.tensor_tensor(pair_b, pair_b,
                                                 earlier[:, :, :].unsqueeze(1).to_broadcast([P, NT, E, E]), ALU.mult))
                    link(nc.vector.tensor_tensor(pair_a, pair_a, pair_b, ALU.add))
                    link(nc.vector.tensor_reduce(rank[:, :, :], pair_a, X, ALU.add))

                def route_two():
                    dve.wait_ge(logits_mm.sem, logits_mm.at(b, 1))
                    link(nc.vector.tensor_copy(logits[:, :, :].rearrange("p n e -> p (n e)"), ps[:, 7, 0:NT * E]))
                    link(nc.vector.tensor_reduce(top1[:, :], logits[:, :, :], X, ALU.max))
                    nc.vector.tensor_tensor(r_a[:, :, :], logits[:, :, :], wide(top1[:, :]), ALU.subtract
                                            ).then_inc(shift_ready.sem, 1)
                    ranks()
                    link(nc.vector.tensor_scalar(r_b[:, :, :], rank[:, :, :], 0.0, MINUS_INF, ALU.is_equal, ALU.mult))
                    link(nc.vector.tensor_tensor(r_b[:, :, :], r_b[:, :, :], logits[:, :, :], ALU.add))
                    link(nc.vector.tensor_reduce(top2[:, :], r_b[:, :, :], X, ALU.max))
                    nc.vector.tensor_tensor(r_c[:, :, :], r_b[:, :, :], wide(top2[:, :]), ALU.subtract
                                            ).then_inc(shift_ready.sem, 1)
                    link(nc.vector.scalar_tensor_tensor(r_d[:, :, :], logits[:, :, :], -1.0, logits[:, :, :],
                                                        ALU.mult, ALU.max))
                    for k, (top, total) in enumerate(((top1, r_s1), (top2, r_s2))):
                        link(nc.vector.tensor_tensor(r_e[:, :, :], r_d[:, :, :], wide(top[:, :]), ALU.max))
                        link(nc.vector.tensor_tensor(gate_w[:, :, :], logits[:, :, :], wide(top[:, :]), ALU.subtract))
                        link(nc.vector.scalar_tensor_tensor(r_e[:, :, :], r_e[:, :, :], JITTER2, gate_w[:, :, :],
                                                            ALU.mult, ALU.add))
                        dve.wait_ge(r_exp_done.sem, r_exp_done.at(b, k + 1))
                        link(nc.vector.scalar_tensor_tensor(r_e[:, :, :], r_e[:, :, :], 0.0, r_exp[:, k, :, :],
                                                            ALU.is_ge, ALU.mult))
                        link(nc.vector.tensor_reduce(total[:, :], r_e[:, :, :], X, ALU.add))
                        link(nc.vector.reciprocal(total[:, :], total[:, :]))
                    link(nc.vector.scalar_tensor_tensor(r_e[:, :, :], rank[:, :, :], 0.0, wide(r_s1[:, :]),
                                                        ALU.is_equal, ALU.mult))
                    link(nc.vector.scalar_tensor_tensor(r_d[:, :, :], rank[:, :, :], 1.0, wide(r_s2[:, :]),
                                                        ALU.is_equal, ALU.mult))
                    nc.vector.tensor_tensor(gate_w[:, :, :], r_e[:, :, :], r_d[:, :, :], ALU.add
                                            ).then_inc(gate_ready.sem, 1)

                def route_four():
                    dve.wait_ge(logits_mm.sem, logits_mm.at(b, 2))
                    link(nc.vector.tensor_tensor(
                        logits[:, :, :], ps[:, 7, 0:NT * E].rearrange("p (n e) -> p n e", e=E),
                        b_router[:, :].unsqueeze(1).to_broadcast([P, NT, E]), ALU.add))
                    link(nc.vector.tensor_reduce(top1[:, :], logits[:, :, :], X, ALU.max))
                    nc.vector.tensor_tensor(r_a[:, :, :], logits[:, :, :], wide(top1[:, :]), ALU.subtract
                                            ).then_inc(shift_ready.sem, 1)
                    ranks()
                    dve.wait_ge(r_exp_done.sem, r_exp_done.at(b, 3))
                    link(nc.vector.scalar_tensor_tensor(r_e[:, :, :], rank[:, :, :], TOP_K - 0.5, r_exp[:, 0, :, :],
                                                        ALU.is_lt, ALU.mult))
                    link(nc.vector.tensor_reduce(r_s1[:, :], r_e[:, :, :], X, ALU.add))
                    link(nc.vector.reciprocal(r_s1[:, :], r_s1[:, :]))
                    nc.vector.tensor_tensor(gate_w[:, :, :], r_e[:, :, :], wide(r_s1[:, :]), ALU.mult
                                            ).then_inc(gate_ready.sem, 1)

                def experts_add(l):
                    for c in range(2):
                        dve.wait_ge(y_mm.sem, y_mm.at(b, 2 * l + c + 1))
                        link(nc.vector.tensor_tensor(
                            x_mid[:, 4 * c:4 * c + 4, :], x_mid[:, 4 * c:4 * c + 4, :],
                            ps[:, c, :].rearrange("p (n d) -> p n d", d=D), ALU.add))

                dve.wait_ge(x_loaded.sem, x_loaded.at(b, 16))
                layer_norm(0, x_in)
                dve.wait_ge(y_stored.sem, y_stored.at(b, 0))
                count[0] += 1
                nc.vector.tensor_tensor(x_mid[:, :, :], x_in[:, :, :],
                                        b_o[:, :].unsqueeze(1).to_broadcast([P, NT, D]), ALU.add
                                        ).then_inc(dve_step.sem, 1)
                dve.wait_ge(dve_step.sem, dve_step.at(b, count[0]))
                dve.wait_ge(norm_ready.sem, norm_ready.at(b, NT))
                nc.vector.tensor_copy(var_eps[:, 0:1], var_eps[:, 0:1]).then_inc(x_taken.sem, 1)

                dve.wait_ge(k_proj.sem, k_proj.at(b, 1))
                nc.vector.tensor_scalar(keys[0:KD, :], banks(0)[0:KD, :], b_k[0:KD, :], None, ALU.add)
                high = probs[KD:P, 1, :]
                link(nc.vector.tensor_scalar(high.bitcast(F32R), banks(0)[KD:P, :], b_k[KD:P, :], None, ALU.add))
                nc.vector.scalar_tensor_tensor(keys[KD:P, :], banks(0)[KD:P, :], b_k[KD:P, :], high,
                                               ALU.add, ALU.subtract).then_inc(keys_ready.sem, 1)
                dve.wait_ge(latent_mm.sem, latent_mm.at(b, 1))
                nc.vector.tensor_tensor(latent[:, :, :], ps[:, 7, 0:NT * DC].rearrange("p (n c) -> p n c", c=DC),
                                        b_dkv[:, :].unsqueeze(1).to_broadcast([P, NT, DC]), ALU.add
                                        ).then_inc(latent_ready.sem, 1)

                for quad in range(QUADS):
                    for j in range(QUAD):
                        h = quad * QUAD + j
                        dve.wait_ge(q_high.sem, q_high.at(b, h + 1))
                        nc.vector.scalar_tensor_tensor(
                            q_parts[:, j, 1, :], banks(2 * (h % 2)), b_q[:, h:h + 1],
                            q_parts[:, j, 0, :].bitcast(F32), ALU.add, ALU.subtract).then_inc(q_ready.sem, 1)
                    for s in range(NT * QUAD + 4):
                        if s < NT * QUAD:
                            t = quad * NT * QUAD + s
                            dve.wait_ge(scores_ready.sem, scores_ready.at(b, t + 1))
                            if t >= 4:
                                dve.wait_ge(exp_done.sem, exp_done.at(b, t - 3))
                            nc.vector.tensor_reduce(neg_max[:, t % 4:t % 4 + 1], banks(2 * (t % 2)), X, ALU.max,
                                                    negate=True).then_inc(max_ready.sem, 1)
                        if 1 <= s <= NT * QUAD:
                            t = quad * NT * QUAD + s - 1
                            dve.wait_ge(pT_high.sem, pT_high.at(b, t + 1))
                            if t >= 2 * QUAD:
                                dve.wait_ge(u_ready.sem, u_ready.at(b, t // QUAD - 1))
                            nc.vector.tensor_copy(probsT[:, t % (2 * QUAD), BANK:SEQ], ps[:, 5, :]
                                                  ).then_inc(high_copied.sem, 1)
                        if s >= QUAD and s % QUAD == 0:
                            g = quad * NT + s // QUAD - 1
                            dve.wait_ge(exp_done.sem, exp_done.at(b, (g + 1) * QUAD))
                            if g >= 2:
                                dve.wait_ge(u_ready.sem, u_ready.at(b, g - 1))
                            nc.vector.reciprocal(inv_sum[:, g % 2, :], row_sum[:, g % 2, :]).then_inc(inv_ready.sem, 1)
                        if s >= QUAD + 2 and (s - 2) % QUAD == 0:
                            g = quad * NT + (s - 2) // QUAD - 1
                            dve.wait_ge(scale_ready.sem, scale_ready.at(b, g + 1))
                            if g >= 2:
                                dve.wait_ge(o_ready.sem, o_ready.at(b, g - 1))
                            nc.vector.tensor_tensor(o_latent[:, g % 2, :], ps[:, 6, 128 * (g % 2):128 * (g % 2) + 128],
                                                    scale_sb[:, g % 2, :], ALU.mult).then_inc(u_scaled.sem, 1)
                        if s >= QUAD + 3 and (s - 3) % QUAD == 0:
                            g = quad * NT + (s - 3) // QUAD - 1
                            n = g % NT
                            dve.wait_ge(o_ready.sem, o_ready.at(b, g + 1))
                            if g >= NT:
                                dve.wait_ge(o_added.sem, o_added.at(b, g - NT + 1))
                            nc.vector.tensor_tensor(x_mid[:, n, :], x_mid[:, n, :],
                                                    ps[:, 7, 128 * (g % 2):128 * (g % 2) + 128], ALU.add
                                                    ).then_inc(o_added.sem, 1)

                route_two()
                for u in range(UNITS):
                    dve.wait_ge(tanh_done.sem, tanh_done.at(b, u + 1))
                    nc.vector.scalar_tensor_tensor(ffn_g[:, u % 2, :], ffn_t[:, u % 2, :], 1.0, ps[:, u % 2, :],
                                                   ALU.add, ALU.mult).then_inc(g_free.sem, 1)
                    dve.wait_ge(g_free.sem, g_free.at(b, u + 1))
                    if u >= 2:
                        dve.wait_ge(h_ready.sem, h_ready.at(b, u - 1))
                    nc.vector.tensor_tensor(ffn_gu[:, u % 2, :], ffn_g[:, u % 2, :], ps[:, 2 + u % 2, :], ALU.mult
                                            ).then_inc(gu_done.sem, 1)
                dve.wait_ge(o_added.sem, o_added.at(b, GROUPS))
                experts_add(0)
                layer_norm(1, x_mid)
                for n in range(NT):
                    dve.wait_ge(qkv_mm.sem, qkv_mm.at(b, n + 1))
                    nc.vector.tensor_tensor(qkv[:, n, :], ps[:, n % 4, 0:3 * D], b_qkv[:, :], ALU.add
                                            ).then_inc(z_ready.sem, 1)
                dve.wait_ge(norm_ready.sem, norm_ready.at(b, 2 * NT))
                link(nc.vector.tensor_tensor(x_mid[:, :, :], x_mid[:, :, :],
                                             b_proj[:, :].unsqueeze(1).to_broadcast([P, NT, D]), ALU.add))
                dve.wait_ge(sig_tanh.sem, sig_tanh.at(b, 1))
                nc.vector.tensor_scalar(qkv[:, :, 0:2 * D], qkv[:, :, 0:2 * D], 0.5, 0.5, ALU.mult, ALU.add
                                        ).then_inc(qk_ready.sem, 1)
                q, k, v = qkv[:, :, 0:D], qkv[:, :, D:2 * D], qkv[:, :, 2 * D:3 * D]

                def heads(x):
                    return x.rearrange("p n (h d) -> p n h d", d=D1)

                def per_head(x):
                    return x.rearrange("p (n h) -> p n h", n=NT).unsqueeze(3).to_broadcast([P, NT, H1, D1])

                def flow(dst, x, total):
                    link(nc.vector.scalar_tensor_tensor(tmp, x, EPS1, total.unsqueeze(1).to_broadcast([P, NT, D]),
                                                        ALU.add, ALU.mult))
                    link(nc.vector.tensor_reduce(dst, tmp.rearrange("p n (h d) -> p (n h) d", d=D1), X, ALU.add))

                dve.wait_ge(sums_mm.sem, sums_mm.at(b, 1))
                link(nc.vector.tensor_scalar(sums_eps[:, :], ps[:, 4, 0:2 * D], EPS1, None, ALU.add))
                flow(inv_flow[:, 0, :], q, sums_eps[:, D:2 * D])
                flow(inv_flow[:, 1, :], k, sums_eps[:, 0:D])
                link(nc.vector.reciprocal(inv_flow[:, :, :], inv_flow[:, :, :]))
                nc.vector.tensor_tensor(heads(weighted[:, :, 0:D]), heads(q), per_head(inv_flow[:, 0, :]), ALU.mult)
                nc.vector.tensor_tensor(heads(weighted[:, :, D:2 * D]), heads(k), per_head(inv_flow[:, 1, :]),
                                        ALU.mult).then_inc(weighted_ready.sem, 1)
                dve.wait_ge(sums_mm.sem, sums_mm.at(b, 2))
                link(nc.vector.tensor_scalar(sums2_eps[:, :], ps[:, 5, 0:2 * D], EPS1, None, ALU.add))
                flow(conserved[:, 0, :], q, sums2_eps[:, D:2 * D])
                flow(conserved[:, 1, :], k, sums2_eps[:, 0:D])
                link(nc.vector.tensor_scalar(conserved[:, :, :], conserved[:, :, :], EPS1, None, ALU.add))
                link(nc.vector.tensor_scalar(conserved[:, 1, :], conserved[:, 1, :], 1.0, -1.0, ALU.min, ALU.max))
                nc.vector.tensor_copy(var_eps[:, 0:1], var_eps[:, 0:1]).then_inc(conserved_ready.sem, 1)
                dve.wait_ge(flow_act.sem, flow_act.at(b, 1))
                link(nc.vector.tensor_scalar(sink_alloc[:, :], sink_alloc[:, :], 0.5, 0.5, ALU.mult, ALU.add))
                dve.wait_ge(flow_act.sem, flow_act.at(b, 2))
                nc.vector.tensor_tensor(heads(v_comp), heads(v), per_head(source_exp[:, :]), ALU.mult
                                        ).then_inc(v_ready.sem, 1)
                dve.wait_ge(kv_mm.sem, kv_mm.at(b, 1))
                link(nc.vector.tensor_reduce(source_inv[:, :], ps[:, 1, 0:NT * H1].rearrange("p (n h) -> p h n", n=NT),
                                             X, ALU.add))
                nc.vector.reciprocal(source_inv[:, :], source_inv[:, :])
                link(nc.vector.scalar_tensor_tensor(kv[:, :], ps[:, 0, 0:D], float(SEQ),
                                                    same_head[:, :, :].rearrange("p h d -> p (h d)"),
                                                    ALU.mult, ALU.mult))
                nc.vector.tensor_tensor(kv[:, :].rearrange("p (h d) -> p h d", d=D1),
                                        kv[:, :].rearrange("p (h d) -> p h d", d=D1),
                                        source_inv[:, :].unsqueeze(2).to_broadcast([P, H1, D1]), ALU.mult
                                        ).then_inc(kv_ready.sem, 1)
                for c in range(2):
                    dve.wait_ge(heads_mm.sem, heads_mm.at(b, c + 1))
                    half = slice(4 * c, 4 * c + 4)
                    nc.vector.tensor_tensor(heads(heads_out[:, half, :]),
                                            ps[:, 2 + c, :].rearrange("p (n h d) -> p n h d", n=4, d=D1),
                                            per_head(sink_alloc[:, :])[:, half, :, :], ALU.mult
                                            ).then_inc(heads_ready.sem, 1)
                for c in range(2):
                    dve.wait_ge(proj_mm.sem, proj_mm.at(b, c + 1))
                    link(nc.vector.tensor_tensor(
                        x_mid[:, 4 * c:4 * c + 4, :], x_mid[:, 4 * c:4 * c + 4, :],
                        ps[:, [6, 0][c], :].rearrange("p (n d) -> p n d", d=D), ALU.add))
                route_four()
                for u in range(UNITS):
                    f = u // HALVES
                    dve.wait_ge(gu_ready.sem, gu_ready.at(b, UNITS + u + 1))
                    nc.vector.tensor_scalar(ffn_g[:, u % 2, :], ps[:, u % 2, :], b_gate[:, f:f + 1], LIMIT,
                                            ALU.add, ALU.min).then_inc(gate_lim.sem, 1)
                    dve.wait_ge(up_copied.sem, up_copied.at(b, u + 1))
                    nc.vector.tensor_scalar(ffn_u[:, u % 2, :], ffn_u[:, u % 2, :], 1.0 + LIMIT, 1.0 - LIMIT,
                                            ALU.min, ALU.max)
                    dve.wait_ge(tanh_done.sem, tanh_done.at(b, UNITS + u + 1))
                    nc.vector.scalar_tensor_tensor(ffn_g[:, u % 2, :], ffn_t[:, u % 2, :], 1.0, ffn_g[:, u % 2, :],
                                                   ALU.add, ALU.mult).then_inc(g_free.sem, 1)
                    dve.wait_ge(g_free.sem, g_free.at(b, UNITS + u + 1))
                    if u >= 2:
                        dve.wait_ge(h_ready.sem, h_ready.at(b, UNITS + u - 1))
                    nc.vector.tensor_tensor(ffn_gu[:, u % 2, :], ffn_g[:, u % 2, :], ffn_u[:, u % 2, :], ALU.mult
                                            ).then_inc(gu_done.sem, 1)
                experts_add(1)
                nc.vector.tensor_copy(var_eps[:, 0:1], var_eps[:, 0:1]).then_inc(y_done.sem, 1)
                assert count[0] == DVE_STEPS, count[0]

        @block.tensor
        def _(pe):
            pe.wait_ge(weights_in.sem, ALL_WEIGHTS)
            pe.wait_ge(pool_consts.sem, 9)
            for h in range(H0):
                mm = nc.tensor.matmul(ps[0:DC + 1, 0, h * DC:(h + 1) * DC], uq_T[:, h, :], uk_T[:, h, :],
                                      start=True, stop=True)
            mm.then_inc(prep_mm.sem, 1)
            for h in range(H0):
                nc.tensor.matmul(ps[DC * (h % QUAD):DC * (h % QUAD + 1), 4, (h // QUAD) * D:(h // QUAD + 1) * D],
                                 uv_T[:, h, :], wo_heads[:, h, :], start=True, stop=True)
            for h in range(H0):
                nc.tensor.matmul(ps[:, 5, 0:D], b_uv[:, h:h + 1].to_broadcast([P, P]), wo_heads[:, h, :],
                                 start=(h == 0), stop=(h == H0 - 1))
            pe.wait_ge(prep_sb.sem, H0)
            for h in range(H0):
                nc.tensor.matmul(ps[:, 1, h:h + 1], absorbed[:, h, :], b_dq1, start=True, stop=True)
            for c in range(2):
                last = nc.tensor.matmul(ps[:, 2 + c, :], dq_T,
                                        absorbed[0:DC, 4 * c:4 * c + 4, :].rearrange("p a b -> p (a b)"),
                                        start=True, stop=True)
            last.then_inc(prep_mm.sem, 1)
            pe.wait_ge(prep_sb.sem, H0 + 5)
            pe.wait_ge(prep_act.sem, 2)

            def transpose_norm(b, l):
                for n in range(NT):
                    pe.wait_ge(norm_ready.sem, norm_ready.at(b, l * NT + n + 1))
                    mm = nc.tensor.transpose(ps[:, 4 + n // 4, (n % 4) * P:(n % 4 + 1) * P], x_norm[:, n, :],
                                             ident[:, :])
                    if n % 4 == 3:
                        mm.then_inc(normT_ready.sem, 1)

            def router(b, l):
                for n in range(NT):
                    mm = nc.tensor.matmul(ps[:, 7, n * E:(n + 1) * E], xT[:, n * P:(n + 1) * P], w_router[l][:, :],
                                          start=True, stop=True)
                mm.then_inc(logits_mm.sem, 1)

            def gates_transpose(b, l):
                pe.wait_ge(gate_ready.sem, gate_ready.at(b, l + 1))
                for n in range(NT):
                    mm = nc.tensor.transpose(ps[0:E, 4 + n // 4, (n % 4) * P:(n % 4 + 1) * P], gate_w[:, n, :],
                                             ident[:, :])
                mm.then_inc(gateT_mm.sem, 1)

            def experts(b, l):
                def gate_up(u):
                    f, c = u // HALVES, u % HALVES
                    if u >= 2:
                        pe.wait_ge(gu_done.sem, gu_done.at(b, l * UNITS + u - 1))
                    tokens = xT[:, c * BANK:(c + 1) * BANK]
                    nc.tensor.matmul(ps[:, u % 2, :], w_gate[l][:, f * P:(f + 1) * P], tokens, start=True, stop=True)
                    nc.tensor.matmul(ps[:, 2 + u % 2, :], w_up[l][:, f * P:(f + 1) * P], tokens, start=True, stop=True
                                     ).then_inc(gu_ready.sem, 1)

                def down(u):
                    f, c = u // HALVES, u % HALVES
                    pe.wait_ge(h_ready.sem, h_ready.at(b, l * UNITS + u + 1))
                    nc.tensor.matmul(ps[:, 4 + c, :], w_down[l][:, f, :], ffn_h[:, u % 2, :], start=(l == 0 and f == 0),
                                     stop=(f == E * FH - 1)).then_inc(down_done.sem, 1)

                pe.wait_ge(gateT_ready.sem, gateT_ready.at(b, l + 1))
                if l == 1:
                    for c in range(HALVES):
                        nc.tensor.matmul(ps[:, 4 + c, :], b_down[:, :], gate_wT[:, c * BANK:(c + 1) * BANK],
                                         start=True, stop=False)
                for u in range(UNITS + 2):
                    if u < UNITS:
                        gate_up(u)
                    if u >= 2:
                        down(u - 2)
                for n in range(NT):
                    if n % 4 == 0:
                        pe.wait_ge(yT_ready.sem, yT_ready.at(b, 2 * l + n // 4 + 1))
                    mm = nc.tensor.transpose(ps[:, n // 4, (n % 4) * P:(n % 4 + 1) * P], y_T[:, n * P:(n + 1) * P],
                                             ident[:, :])
                    if n % 4 == 3:
                        mm.then_inc(y_mm.sem, 1)

            with pe.Fori(0, BATCH) as index:
                b = Sequence(pe, index)
                transpose_norm(b, 0)
                pe.wait_ge(xT_ready.sem, xT_ready.at(b, 2))
                for c in range(HALVES):
                    mm = nc.tensor.matmul(ps[:, c, :], w_k[:, :], xT[:, c * BANK:(c + 1) * BANK], start=True, stop=True)
                mm.then_inc(k_proj.sem, 1)
                for n in range(NT):
                    mm = nc.tensor.matmul(ps[:, 7, n * DC:(n + 1) * DC], xT[:, n * P:(n + 1) * P], w_dkv[:, :],
                                          start=True, stop=True)
                mm.then_inc(latent_mm.sem, 1)

                def scores(t):
                    j, n = t % QUAD, (t // QUAD) % NT
                    if t % (NT * QUAD) >= 2:
                        pe.wait_ge(exp_done.sem, exp_done.at(b, t - 1))
                    else:
                        quad = t // (NT * QUAD)
                        pe.wait_ge(q_ready.sem, q_ready.at(b, (quad + 1) * QUAD))
                        pe.wait_ge(keys_ready.sem, keys_ready.at(b, 1))
                    for c in range(HALVES):
                        for part in range(2):
                            mm = nc.tensor.matmul(ps[:, 2 * (t % 2) + c, :], q_parts[:, j, part, n * P:(n + 1) * P],
                                                  keys[:, c * BANK:(c + 1) * BANK], start=(part == 0),
                                                  stop=(part == 1))
                    mm.then_inc(scores_ready.sem, 1)

                def transpose_probs(t):
                    pe.wait_ge(exp_done.sem, exp_done.at(b, t + 1))
                    for c, (copied, done) in enumerate(((low_copied, pT_low), (high_copied, pT_high))):
                        if t >= 1:
                            pe.wait_ge(copied.sem, copied.at(b, t))
                        for i in range(4):
                            k = 4 * c + i
                            mm = nc.tensor.transpose(ps[:, 4 + c, i * P:(i + 1) * P],
                                                     probs[:, t % 2, k * P:(k + 1) * P], ident[:, :])
                        mm.then_inc(done.sem, 1)

                def values(g):
                    pe.wait_ge(low_copied.sem, low_copied.at(b, (g + 1) * QUAD))
                    pe.wait_ge(high_copied.sem, high_copied.at(b, (g + 1) * QUAD))
                    pe.wait_ge(inv_ready.sem, inv_ready.at(b, g + 1))
                    if g == 0:
                        pe.wait_ge(latent_ready.sem, latent_ready.at(b, 1))
                    if g >= 1:
                        pe.wait_ge(u_scaled.sem, u_scaled.at(b, g))
                    at = 128 * (g % 2)
                    for k in range(NT):
                        for j in range(QUAD):
                            nc.tensor.matmul(ps[DC * j:DC * (j + 1), 6, at:at + P], latent[:, k, :],
                                             probsT[:, (g % 2) * QUAD + j, k * P:(k + 1) * P],
                                             start=(k == 0), stop=(k == NT - 1))
                    for j in range(QUAD):
                        mm = nc.tensor.matmul(ps[DC * j:DC * (j + 1), 6, 256 + at:256 + at + P],
                                              inv_sum[:, g % 2, j:j + 1].to_broadcast([P, DC]), ident[:, :],
                                              start=True, stop=True)
                    mm.then_inc(u_ready.sem, 1)

                def output(g):
                    pe.wait_ge(u_scaled.sem, u_scaled.at(b, g + 1))
                    if g >= 1:
                        pe.wait_ge(o_added.sem, o_added.at(b, g))
                    at = 128 * (g % 2)
                    nc.tensor.matmul(ps[:, 7, at:at + P], o_latent[:, g % 2, :], w_o[:, g // NT, :],
                                     start=True, stop=True).then_inc(o_ready.sem, 1)

                for quad in range(QUADS):
                    for j in range(QUAD):
                        h = quad * QUAD + j
                        if j >= 2:
                            pe.wait_ge(q_ready.sem, q_ready.at(b, h - 1))
                        elif quad == 0:
                            pe.wait_ge(keys_ready.sem, keys_ready.at(b, 1))
                        else:
                            pe.wait_ge(exp_done.sem, exp_done.at(b, quad * NT * QUAD))
                        for c in range(HALVES):
                            mm = nc.tensor.matmul(ps[:, 2 * (h % 2) + c, :], w_q[:, h, :],
                                                  xT[:, c * BANK:(c + 1) * BANK], start=True, stop=True)
                        mm.then_inc(q_proj.sem, 1)
                    for s in range(NT * QUAD + 3):
                        t = quad * NT * QUAD + s
                        if s < NT * QUAD:
                            scores(t)
                        if 1 <= s <= NT * QUAD:
                            transpose_probs(t - 1)
                        if s >= QUAD + 1 and (s - 1) % QUAD == 0:
                            values(quad * NT + (s - 1) // QUAD - 1)
                        if s >= QUAD + 2 and (s - 2) % QUAD == 0:
                            output(quad * NT + (s - 2) // QUAD - 1)

                pe.wait_ge(o_added.sem, o_added.at(b, GROUPS))
                router(b, 0)
                pe.wait_ge(low_copied.sem, low_copied.at(b, TILES))
                pe.wait_ge(high_copied.sem, high_copied.at(b, TILES))
                gates_transpose(b, 0)
                experts(b, 0)

                transpose_norm(b, 1)
                pe.wait_ge(xT_ready.sem, xT_ready.at(b, 4))
                for n in range(NT):
                    if n >= 4:
                        pe.wait_ge(z_ready.sem, z_ready.at(b, n - 3))
                    nc.tensor.matmul(ps[:, n % 4, 0:3 * D], xT[:, n * P:(n + 1) * P], w_qkv[:, :],
                                     start=True, stop=True).then_inc(qkv_mm.sem, 1)
                router(b, 1)
                pe.wait_ge(qk_ready.sem, qk_ready.at(b, 1))
                for n in range(NT):
                    mm = nc.tensor.matmul(ps[:, 4, 0:2 * D], ones[:, :], qkv[:, n, 0:2 * D], start=(n == 0),
                                          stop=(n == NT - 1))
                mm.then_inc(sums_mm.sem, 1)
                pe.wait_ge(weighted_ready.sem, weighted_ready.at(b, 1))
                for n in range(NT):
                    mm = nc.tensor.matmul(ps[:, 5, 0:2 * D], ones[:, :], weighted[:, n, :], start=(n == 0),
                                          stop=(n == NT - 1))
                mm.then_inc(sums_mm.sem, 1)
                for n in range(NT):
                    mm = nc.tensor.transpose(ps[:, [6, 2][n // 4], (n % 4) * P:(n % 4 + 1) * P], weighted[:, n, 0:D],
                                             ident[:, :])
                    if n % 4 == 3:
                        mm.then_inc(qnT_mm.sem, 1)
                pe.wait_ge(v_ready.sem, v_ready.at(b, 1))
                for n in range(NT):
                    nc.tensor.matmul(ps[:, 0, 0:D], qkv[:, n, D:2 * D], v_comp[:, n, :], start=(n == 0),
                                     stop=(n == NT - 1))
                nc.tensor.matmul(ps[:, 1, 0:NT * H1], ones[:, :], source_exp[:, :], start=True, stop=True
                                 ).then_inc(kv_mm.sem, 1)
                pe.wait_ge(kv_ready.sem, kv_ready.at(b, 1))
                pe.wait_ge(qnT_ready.sem, qnT_ready.at(b, 2))
                for n in range(NT):
                    mm = nc.tensor.matmul(ps[:, 2 + n // 4, (n % 4) * D:(n % 4 + 1) * D], q_normT[:, n * P:(n + 1) * P],
                                          kv[:, :], start=True, stop=True)
                    if n % 4 == 3:
                        mm.then_inc(heads_mm.sem, 1)
                for n in range(NT):
                    if n % 4 == 0:
                        pe.wait_ge(heads_ready.sem, heads_ready.at(b, n // 4 + 1))
                    mm = nc.tensor.transpose(ps[:, 4 + n // 4, (n % 4) * P:(n % 4 + 1) * P], heads_out[:, n, :],
                                             ident[:, :])
                    if n % 4 == 3:
                        mm.then_inc(headsT_mm.sem, 1)
                for n in range(NT):
                    if n % 4 == 0:
                        pe.wait_ge(headsT_ready.sem, headsT_ready.at(b, n // 4 + 1))
                    mm = nc.tensor.matmul(ps[:, [6, 0][n // 4], (n % 4) * D:(n % 4 + 1) * D],
                                          heads_outT[:, n * P:(n + 1) * P], w_proj[:, :], start=True, stop=True)
                    if n % 4 == 3:
                        mm.then_inc(proj_mm.sem, 1)
                gates_transpose(b, 1)
                experts(b, 1)


def kernel(**inputs):
    import concourse.bacc as _bacc
    from concourse.bass_utils import run_bass_kernel_spmd as _run

    def get(name):
        return np.asarray(inputs[name])

    def head_T(w, heads):
        return w.reshape(w.shape[0], heads, -1).transpose(2, 1, 0)

    def stack(w, bias):
        return np.concatenate([w, bias[None, :]], axis=0)

    a0, a1, f0, f1 = "L0_attn_", "L1_attn_", "L0_ffn_", "L1_ffn_"
    key_w = np.concatenate([get(a0 + "W_DKV"), get(a0 + "W_KR")], axis=1)
    key_b = np.concatenate([get(a0 + "b_DKV"), get(a0 + "b_KR")])
    gu = get(f1 + "gate_up_proj")
    gu_b = get(f1 + "gate_up_proj_bias")

    def up(w):
        return w.transpose(2, 0, 1).reshape(D, E * F)

    def down(w):
        return w.transpose(2, 0, 1).reshape(FH, P, E, D).transpose(1, 2, 0, 3).reshape(P, E * FH, D)

    def column(bias):
        return bias.reshape(E * FH, P).T

    arrays = {
        "x": get(a0 + "h_t"),
        "UQ_T": head_T(stack(get(a0 + "W_UQ"), get(a0 + "b_UQ")), H0),
        "UK_T": head_T(get(a0 + "W_UK"), H0),
        "UV_T": head_T(get(a0 + "W_UV"), H0),
        "W_O": get(a0 + "W_O").reshape(H0, DK, D).transpose(1, 0, 2),
        "b_UV": get(a0 + "b_UV").reshape(H0, DK).T,
        "DQ_T": get(a0 + "W_DQ").T,
        "b_DQ1": np.concatenate([get(a0 + "b_DQ"), np.ones(1, np.float32)])[:, None],
        "Q_rope": stack(get(a0 + "W_QR"), get(a0 + "b_QR")).reshape(DC + 1, H0, DR),
        "W_K": np.concatenate([key_w, key_w], axis=1),
        "b_K": np.concatenate([key_b, key_b])[:, None],
        "W_DKV": get(a0 + "W_DKV"),
        "gate0": up(get(f0 + "w_gate")),
        "up0": up(get(f0 + "w_up")),
        "down0": down(get(f0 + "w_down")),
        "router0": get(f0 + "router_w").T,
        "W_QKV": get(a1 + "qkv_w").T,
        "W_PROJ": get(a1 + "proj_w").T,
        "gate1": up(gu[:, 0:F, :]),
        "up1": up(gu[:, F:2 * F, :]),
        "down1": down(get(f1 + "down_proj")),
        "router1": get(f1 + "router_weight").T,
        "b_gate": column(gu_b[:, 0:F]),
        "b_up": column(gu_b[:, F:2 * F]),
        "b_down": get(f1 + "down_proj_bias"),
        "b_DKV": get(a0 + "b_DKV"),
        "b_O": get(a0 + "b_O"),
        "b_QKV": get(a1 + "qkv_b"),
        "b_PROJ": get(a1 + "proj_b"),
        "b_ROUTER": get(f1 + "router_bias"),
    }
    nc = _bacc.Bacc("TRN2", target_bir_lowering=False, num_devices=1)
    arrays = {f"in_{k}": np.ascontiguousarray(v) for k, v in arrays.items()}
    ins = {k[3:]: nc.dram_tensor(k, v.shape, mybir.dt.from_np(v.dtype), kind="ExternalInput").ap()
           for k, v in arrays.items()}
    out = nc.dram_tensor("out", (BATCH, SEQ, D), F32, kind="ExternalOutput").ap()
    nc.disable_value_cache = True
    two_layer_kernel(nc, ins, out)
    r = _run(nc, [arrays], core_ids=[0])
    return r.results[0]["out"]
```

```python
from contextlib import ExitStack

import numpy as np

import concourse.bass as bass
from concourse import mybir

F32 = mybir.dt.float32
F32R = mybir.dt.float32r
ALU = mybir.AluOpType
ACT = mybir.ActivationFunctionType
X = mybir.AxisListType.X

P = 128
BATCH = 8
SEQ = 1024
NT = SEQ // P
D = 128
BANK = 512
HALVES = SEQ // BANK
LN_EPS = 1e-5

H0, DK, DC, DR = 8, 128, 32, 32
KD = DC + DR
SCALE = 1.0 / float(np.sqrt(DK + DR))
QUAD = P // DC
QUADS = H0 // QUAD
GROUPS = QUADS * NT
TILES = GROUPS * QUAD

STEPS = H0 + TILES
T_LAG = 2
INV_LAG = 1
VALUES_LAG = 3
SCALES_LAG = 7
SCALED_LAG = 8
OUTPUT_LAG = 9
ADDED_LAG = 10
ROUTER_STEP = 8
ROUTER_EXP_STEPS = (18, 20)
GATES_STEP = QUAD + NT * QUAD + 3
UNIT_STEP = STEPS + T_LAG

H1, D1 = 16, 8
EPS1 = 1e-6

E, F = 8, 256
FH = F // P
UNITS = E * FH * HALVES
JITTER2 = 0.02
TOP_K = 4
ALPHA, LIMIT = 1.702, 7.0
MINUS_INF = -3.0e38

FLOW_TANH = 4
FLOW_SUMS = 6
FLOW_WEIGHTS = 7
FLOW_SUMS2 = 11
FLOW_CONSERVED = 12
FLOW_ALLOC = 14
FLOW_VALUES = 15
FLOW_KV = 16
FLOW_OUT = 18
FLOW_PROJ = 22

DVE_STEPS = 61
POOL_STEPS = 16


def step_of(t):
    return t + (t // (NT * QUAD) + 1) * QUAD


def use_of(w):
    quad, s = divmod(w, QUAD + NT * QUAD)
    if not 0 <= w < STEPS:
        return None, None
    return (quad * QUAD + s, None) if s < QUAD else (None, quad * NT * QUAD + s - QUAD)


def group_at(w, lag):
    t = use_of(w - lag)[1]
    return t // QUAD if t is not None and t % QUAD == QUAD - 1 else None


class Signal:

    def __init__(self, sem, per, start):
        self.sem, self.per, self.start = sem, per, start

    def at(self, b, k):
        return b.times(self.per) + (self.start + k)


class Sequence:

    def __init__(self, engine, index):
        self.engine, self.index, self.products = engine, index, {}

    def times(self, n):
        if n not in self.products:
            self.products[n] = self.engine.snap(self.index * n)
        return self.products[n]


def two_layer_kernel(nc, ins, out):
    with ExitStack() as ctx:
        def sb(name, shape, dt=F32):
            return ctx.enter_context(nc.sbuf_tensor(name, shape, dt))

        def signal(name, per=0, start=0):
            return Signal(ctx.enter_context(nc.semaphore(name)), per, start)

        x_in = sb("x_in", [P, NT, D])
        x_mid = sb("x_mid", [P, NT, D])
        xT = sb("xT", [P, SEQ])
        stats = sb("stats", [P, NT, 6])
        mean_var = sb("mean_var", [P, NT, 2])
        var_eps = sb("var_eps", [P, NT])
        rstd = sb("rstd", [P, NT])
        spare = sb("spare", [P, 2])
        minus_half = sb("minus_half", [P, NT])

        keys = sb("keys", [P, SEQ], F32R)
        q_parts = sb("q_parts", [P, QUAD, 2, SEQ], F32R)
        probs = sb("probs", [P, 3, SEQ])
        probsT = sb("probsT", [P, 2 * QUAD, SEQ])
        latent = sb("latent", [P, NT, DC])
        neg_max = sb("neg_max", [P, 4])
        row_sum = sb("row_sum", [P, 2, QUAD])
        inv_sum = sb("inv_sum", [P, 2, QUAD])
        scale_sb = sb("scale_sb", [P, 2, P])
        o_latent = sb("o_latent", [P, 2, P])

        room = probsT[:, :, :].rearrange("p a b -> p (a b)")
        qkv = room[:, 0:NT * 3 * D].rearrange("p (n c) -> p n c", n=NT)
        weighted = room[:, 3 * SEQ:5 * SEQ].rearrange("p (n c) -> p n c", n=NT)
        tmp = room[:, 5 * SEQ:6 * SEQ].rearrange("p (n c) -> p n c", n=NT)
        v_comp = room[:, 6 * SEQ:7 * SEQ].rearrange("p (n c) -> p n c", n=NT)
        q_normT = room[:, 7 * SEQ:8 * SEQ]
        heads_out, heads_outT = tmp, room[:, 6 * SEQ:7 * SEQ]
        sums_eps = sb("sums_eps", [P, 2 * D])
        sums2_eps = sb("sums2_eps", [P, 2 * D])
        inv_flow = sb("inv_flow", [P, 2, NT * H1])
        conserved = sb("conserved", [P, 2, NT * H1])
        sink_alloc = sb("sink_alloc", [P, NT * H1])
        source_exp = sb("source_exp", [P, NT * H1])
        source_inv = sb("source_inv", [P, H1])
        kv = sb("kv", [P, D])

        logits = sb("logits", [P, NT, E])
        gate_w = sb("gate_w", [P, NT, E])
        r_a, r_b, r_c, r_d, r_e = (sb(f"r_{c}", [P, NT, E]) for c in "abcde")
        rank = sb("rank", [P, NT, E])
        top1, top2, r_s1, r_s2 = (sb(f"top_{c}", [P, NT]) for c in "abcd")
        r_exp = sb("r_exp", [P, 2, NT, E])
        gate_wT = sb("gate_wT", [E, SEQ])
        gate_rows = sb("gate_rows", [P, E // 4, SEQ])
        gate_bc = sb("gate_bc", [P, 2, SEQ])
        ffn_t = sb("ffn_t", [P, 2, BANK])
        ffn_g = sb("ffn_g", [P, 2, BANK])
        ffn_u = sb("ffn_u", [P, 2, BANK])
        ffn_gu = sb("ffn_gu", [P, 2, BANK])
        ffn_h = sb("ffn_h", [P, 2, BANK])
        pair_a, pair_b = (t[:, 0, :].rearrange("p (n e j) -> p n e j", n=NT, e=E) for t in (ffn_t, ffn_gu))
        y_T = probs[:, 0, :]
        x_norm = probs[:, 2, :].rearrange("p (n d) -> p n d", d=D)

        ident = sb("ident", [P, P])
        ones = sb("ones", [P, P])
        same_head = sb("same_head", [P, H1, D1])
        earlier = sb("earlier", [P, E, E])
        w_q = sb("w_q", [P, H0, P])
        b_q = sb("b_q", [P, H0])
        w_k = sb("w_k", [P, P])
        b_k = sb("b_k", [P, 1])
        w_dkv = sb("w_dkv", [P, DC])
        b_dkv = sb("b_dkv", [P, DC])
        w_o = sb("w_o", [P, QUADS, D])
        b_o = sb("b_o", [P, D])
        w_gate = [sb(f"w_gate{l}", [P, E * F]) for l in range(2)]
        w_up = [sb(f"w_up{l}", [P, E * F]) for l in range(2)]
        w_down = [sb(f"w_down{l}", [P, E * FH, D]) for l in range(2)]
        w_router = [sb(f"w_router{l}", [P, E]) for l in range(2)]
        b_router = sb("b_router", [P, E])
        b_gate = sb("b_gate", [P, E * FH])
        b_up = sb("b_up", [P, E * FH])
        b_down = sb("b_down", [E, D])
        w_qkv = sb("w_qkv", [P, 3 * D])
        b_qkv = sb("b_qkv", [P, 3 * D])
        w_proj = sb("w_proj", [P, D])
        b_proj = sb("b_proj", [P, D])

        take = [0]

        def prep(parts, *shape):
            n = int(np.prod(shape))
            v = room[0:parts, take[0]:take[0] + n]
            take[0] += n
            return v.rearrange("p (a b) -> p a b", a=shape[0]) if len(shape) > 1 else v

        uq_T = prep(P, H0, DC + 1)
        uk_T = prep(P, H0, DC)
        uv_T = prep(P, H0, DC)
        wo_heads = prep(P, H0, D)
        b_uv = prep(P, H0)
        dq_T = prep(DC, D)
        b_dq1 = prep(DC + 1, 1)
        q_rope = prep(DC + 1, H0, DR)
        absorbed = prep(DC + 1, H0, P)
        b_o_in = prep(P, D)

        ps = ctx.enter_context(nc.psum_tensor("ps", [P, 8, BANK], F32))

        def banks(a, n=2):
            return ps[:, a:a + n, :].rearrange("p a b -> p (a b)")

        weights_in = signal("weights_in")
        pool_consts = signal("pool_consts")
        prep_mm = signal("prep_mm")
        prep_sb = signal("prep_sb")
        prep_act = signal("prep_act")
        x_loaded = signal("x_loaded", 16)
        x_taken = signal("x_taken", 1, start=1)
        y_stored = signal("y_stored", 16, start=1)
        y_done = signal("y_done", 1)
        dve_step = signal("dve_step", DVE_STEPS)
        pool_step = signal("pool_step", POOL_STEPS)
        pool_carrier = signal("pool_carrier")
        var_ready = signal("var_ready", 2)
        rstd_ready = signal("rstd_ready", 2)
        norm_ready = signal("norm_ready", 2 * NT)
        normT_ready = signal("normT_ready", 4)
        xT_ready = signal("xT_ready", 4)
        k_proj = signal("k_proj", 1)
        keys_ready = signal("keys_ready", 1)
        latent_mm = signal("latent_mm", 1)
        latent_ready = signal("latent_ready", 1)
        q_proj = signal("q_proj", H0)
        q_high = signal("q_high", H0)
        q_ready = signal("q_ready", H0)
        scores_ready = signal("scores_ready", TILES)
        max_ready = signal("max_ready", TILES)
        exp_done = signal("exp_done", TILES)
        pT_low = signal("pT_low", TILES)
        pT_high = signal("pT_high", TILES)
        low_copied = signal("low_copied", TILES)
        high_copied = signal("high_copied", TILES)
        inv_ready = signal("inv_ready", GROUPS)
        u_ready = signal("u_ready", GROUPS)
        scale_ready = signal("scale_ready", GROUPS)
        u_scaled = signal("u_scaled", GROUPS)
        o_ready = signal("o_ready", GROUPS)
        o_added = signal("o_added", GROUPS)
        logits_mm = signal("logits_mm", 2)
        shift_ready = signal("shift_ready", 3)
        r_exp_done = signal("r_exp_done", 3)
        gate_ready = signal("gate_ready", 2)
        gateT_mm = signal("gateT_mm", 2)
        gateT_ready = signal("gateT_ready", 2)
        rows_ready = signal("rows_ready", 64)
        gu_ready = signal("gu_ready", 2 * UNITS)
        gate_lim = signal("gate_lim", UNITS)
        tanh_done = signal("tanh_done", 2 * UNITS)
        up_copied = signal("up_copied", UNITS)
        g_free = signal("g_free", 2 * UNITS)
        gu_done = signal("gu_done", 2 * UNITS)
        h_ready = signal("h_ready", 2 * UNITS)
        down_done = signal("down_done", 2 * UNITS)
        yT_ready = signal("yT_ready", 4)
        y_mm = signal("y_mm", 4)
        y_added = signal("y_added", 2)
        qkv_mm = signal("qkv_mm", NT)
        z_ready = signal("z_ready", NT)
        sig_tanh = signal("sig_tanh", 1)
        qk_ready = signal("qk_ready", 1)
        sums_mm = signal("sums_mm", 2)
        weighted_ready = signal("weighted_ready", 1)
        qnT_mm = signal("qnT_mm", 2)
        qnT_ready = signal("qnT_ready", 2)
        conserved_ready = signal("conserved_ready", 1)
        flow_act = signal("flow_act", 2)
        v_ready = signal("v_ready", 1)
        kv_mm = signal("kv_mm", 1)
        kv_ready = signal("kv_ready", 1)
        heads_mm = signal("heads_mm", 2)
        heads_ready = signal("heads_ready", 2)
        headsT_mm = signal("headsT_mm", 2)
        headsT_ready = signal("headsT_ready", 2)
        proj_mm = signal("proj_mm", 2)
        proj_added = signal("proj_added", 2)

        loads = [
            (uq_T, "UQ_T"), (uk_T, "UK_T"), (uv_T, "UV_T"), (wo_heads, "W_O"), (b_uv, "b_UV"), (dq_T, "DQ_T"),
            (b_dq1, "b_DQ1"), (q_rope, "Q_rope"), (w_k[:, :], "W_K"), (b_k[:, :], "b_K"), (w_dkv[:, :], "W_DKV"),
            (w_gate[0][:, :], "gate0"), (w_up[0][:, :], "up0"), (w_down[0][:, :, :], "down0"),
            (w_router[0][:, :], "router0"), (w_qkv[:, :], "W_QKV"), (w_proj[:, :], "W_PROJ"),
            (w_gate[1][:, :], "gate1"), (w_up[1][:, :], "up1"), (w_down[1][:, :, :], "down1"),
            (w_router[1][:, :], "router1"), (b_gate[:, :], "b_gate"), (b_up[:, :], "b_up"), (b_down[:, :], "b_down"),
        ]
        rows = [(b_dkv, "b_DKV", DC), (b_o_in, "b_O", D), (b_qkv, "b_QKV", 3 * D), (b_proj, "b_PROJ", D),
                (b_router, "b_ROUTER", E)]
        ALL_WEIGHTS = 16 * (len(loads) + len(rows))

        block = ctx.enter_context(nc.Block())

        @block.sync
        def _(sp):
            for dst, name in loads:
                sp.dma_start(dst, ins[name]).then_inc(weights_in.sem, 16)
            for dst, name, n in rows:
                sp.dma_start(dst[:, 0:n], ins[name].partition_broadcast(P)).then_inc(weights_in.sem, 16)
            sp.sem_inc(x_taken.sem, 1)
            sp.sem_inc(y_stored.sem, 1)
            with sp.Fori(0, BATCH) as index:
                b = Sequence(sp, index)
                sp.wait_ge(x_taken.sem, x_taken.at(b, 0))
                sp.dma_start(x_in[:, :, :], ins["x"][bass.ds(index, 1), :, :].rearrange("a (n p) d -> p (a n) d", p=P)
                             ).then_inc(x_loaded.sem, 16)
                for l in range(2):
                    sp.wait_ge(gateT_ready.sem, gateT_ready.at(b, l + 1))
                    for g in range(E // 4):
                        sp.dma_start(gate_rows[0:97:32, g, :], gate_wT[4 * g:4 * g + 4, :]).then_inc(rows_ready.sem, 16)
                sp.wait_ge(y_done.sem, y_done.at(b, 1))
                sp.dma_start(out[bass.ds(index, 1), :, :].rearrange("a (n p) d -> p (a n) d", p=P), x_mid[:, :, :]
                             ).then_inc(y_stored.sem, 16)
            sp.wait_ge(y_stored.sem, y_stored.per * BATCH + 1)

        @block.gpsimd
        def _(pool):
            nc.gpsimd.memset(minus_half[:, :], -0.5).then_inc(pool_consts.sem, 1)
            nc.gpsimd.memset(ident[:, :], 0.0).then_inc(pool_consts.sem, 1)
            nc.gpsimd.memset(ones[:, :], 1.0).then_inc(pool_consts.sem, 1)
            nc.gpsimd.memset(same_head[:, :, :], 1.0).then_inc(pool_consts.sem, 1)
            nc.gpsimd.memset(earlier[:, :, :], 1.0).then_inc(pool_consts.sem, 1)
            pool.wait_ge(pool_consts.sem, 5)
            nc.gpsimd.affine_select(out=ident[:, :], in_=ident[:, :], compare_op=ALU.not_equal, fill=1.0, base=0,
                                    pattern=[[-1, P]], channel_multiplier=1).then_inc(pool_consts.sem, 1)
            nc.gpsimd.affine_select(out=same_head[:, :, :], in_=same_head[:, :, :], compare_op=ALU.is_ge, fill=0.0,
                                    base=0, pattern=[[-D1, H1], [0, D1]], channel_multiplier=1
                                    ).then_inc(pool_consts.sem, 1)
            pool.wait_ge(pool_consts.sem, 7)
            nc.gpsimd.affine_select(out=same_head[:, :, :], in_=same_head[:, :, :], compare_op=ALU.is_ge, fill=0.0,
                                    base=D1 - 1, pattern=[[D1, H1], [0, D1]], channel_multiplier=-1
                                    ).then_inc(pool_consts.sem, 1)
            nc.gpsimd.affine_select(out=earlier[:, :, :], in_=earlier[:, :, :], compare_op=ALU.is_ge, fill=0.0,
                                    base=-1, pattern=[[1, E], [-1, E]], channel_multiplier=0
                                    ).then_inc(pool_consts.sem, 1)

            with pool.Fori(0, BATCH) as index:
                b = Sequence(pool, index)
                steps = 0
                for l in range(2):
                    pool.wait_ge(var_ready.sem, var_ready.at(b, l + 1))
                    nc.gpsimd.tensor_tensor(rstd[:, :], var_eps[:, :], minus_half[:, :], ALU.pow
                                            ).then_inc(rstd_ready.sem, 1)
                    for u in range(UNITS):
                        e, c = u // (FH * HALVES), u % HALVES
                        if u == 0 or (u % (FH * HALVES) == 2 and e + 1 < E):
                            to = 0 if u == 0 else e + 1
                            if u == 0:
                                pool.wait_ge(rows_ready.sem, rows_ready.at(b, 32 * (l + 1)))
                            else:
                                pool.wait_ge(h_ready.sem, h_ready.at(b, l * UNITS + u))
                            pool.sem_inc(pool_carrier.sem, 1)
                            nc.gpsimd.partition_broadcast(
                                gate_bc[:, to % 2, :], gate_rows[32 * (to % 4):32 * (to % 4) + 1, to // 4, :]
                            ).then_inc(pool_step.sem, 1)
                            steps += 1
                            pool.wait_ge(pool_step.sem, pool_step.at(b, steps))
                        pool.wait_ge(gu_done.sem, gu_done.at(b, l * UNITS + u + 1))
                        if l * UNITS + u >= 2:
                            pool.wait_ge(down_done.sem, down_done.at(b, l * UNITS + u - 1))
                        nc.gpsimd.tensor_tensor(ffn_h[:, u % 2, :], ffn_gu[:, u % 2, :],
                                                gate_bc[:, e % 2, c * BANK:(c + 1) * BANK], ALU.mult
                                                ).then_inc(h_ready.sem, 1)
                assert steps == POOL_STEPS, steps

        @block.scalar
        def _(act):
            act.wait_ge(weights_in.sem, ALL_WEIGHTS)
            for l in range(2):
                nc.scalar.mul(w_down[l][:, :, :], w_down[l][:, :, :], 0.5).then_inc(prep_act.sem, 1)

            def copy_xT(b, l):
                for c in range(2):
                    act.wait_ge(normT_ready.sem, normT_ready.at(b, 2 * l + c + 1))
                    nc.scalar.copy(xT[:, c * BANK:(c + 1) * BANK], ps[:, 4 + c, :]).then_inc(xT_ready.sem, 1)

            def router_exp(b, k):
                act.wait_ge(shift_ready.sem, shift_ready.at(b, k + 1))
                src = r_c if k == 1 else r_a
                nc.scalar.activation(r_exp[:, k % 2, :, :], src[:, :, :], ACT.Exp).then_inc(r_exp_done.sem, 1)

            def copy_gatesT(b, l):
                act.wait_ge(gateT_mm.sem, gateT_mm.at(b, l + 1))
                nc.scalar.copy(gate_wT[:, :], banks(4)[0:E, :]).then_inc(gateT_ready.sem, 1)

            def experts_out(b, l):
                for c in range(HALVES):
                    act.wait_ge(down_done.sem, down_done.at(b, (l + 1) * UNITS))
                    nc.scalar.copy(y_T[:, c * BANK:(c + 1) * BANK], ps[:, 4 + c, :]).then_inc(yT_ready.sem, 1)

            with act.Fori(0, BATCH) as index:
                b = Sequence(act, index)
                copy_xT(b, 0)

                def query_high(h):
                    act.wait_ge(q_proj.sem, q_proj.at(b, h + 1))
                    nc.scalar.activation(q_parts[:, h % QUAD, 0, :], banks(2 * (h % 2)), ACT.Identity,
                                         bias=b_q[:, h:h + 1]).then_inc(q_high.sem, 1)

                def attention_step(w):
                    h, t = use_of(w)
                    if h is not None:
                        query_high(h)
                    if t is not None:
                        act.wait_ge(max_ready.sem, max_ready.at(b, t + 1))
                        if t >= 3:
                            act.wait_ge(pT_high.sem, pT_high.at(b, t - 2))
                        g = t // QUAD
                        if g >= 2 and t % QUAD == 0:
                            act.wait_ge(inv_ready.sem, inv_ready.at(b, g - 1))
                        nc.scalar.activation(probs[:, t % 3, :], banks(2 * (t % 2)), ACT.Exp,
                                             bias=neg_max[:, t % 4:t % 4 + 1],
                                             accum_out=row_sum[:, g % 2, t % QUAD:t % QUAD + 1]
                                             ).then_inc(exp_done.sem, 1)
                    t = use_of(w - T_LAG)[1]
                    if t is not None:
                        act.wait_ge(pT_low.sem, pT_low.at(b, t + 1))
                        if t >= 2 * QUAD:
                            act.wait_ge(u_ready.sem, u_ready.at(b, t // QUAD - 1))
                        nc.scalar.copy(probsT[:, t % (2 * QUAD), 0:BANK], ps[:, 4, :]).then_inc(low_copied.sem, 1)
                    if w in ROUTER_EXP_STEPS:
                        router_exp(b, ROUTER_EXP_STEPS.index(w))
                    if w == GATES_STEP + 1:
                        copy_gatesT(b, 0)
                    g = group_at(w, SCALES_LAG)
                    if g is not None:
                        act.wait_ge(u_ready.sem, u_ready.at(b, g + 1))
                        if g >= 2:
                            act.wait_ge(u_scaled.sem, u_scaled.at(b, g - 1))
                        nc.scalar.copy(scale_sb[:, g % 2, :], ps[:, 6 + g % 2, P:2 * P]).then_inc(scale_ready.sem, 1)

                for w in range(UNIT_STEP):
                    attention_step(w)

                for u in range(UNITS):
                    act.wait_ge(gu_ready.sem, gu_ready.at(b, u + 1))
                    if u >= 2:
                        act.wait_ge(g_free.sem, g_free.at(b, u - 1))
                    nc.scalar.activation(ffn_t[:, u % 2, :], ps[:, u % 2, :], ACT.Tanh, scale=0.5
                                         ).then_inc(tanh_done.sem, 1)
                    attention_step(UNIT_STEP + u)
                experts_out(b, 0)

                copy_xT(b, 1)
                router_exp(b, 2)
                copy_gatesT(b, 1)
                for u in range(UNITS):
                    if u >= 2:
                        act.wait_ge(gu_done.sem, gu_done.at(b, UNITS + u - 1))
                    act.wait_ge(gu_ready.sem, gu_ready.at(b, UNITS + u + 1))
                    f = u // HALVES
                    nc.scalar.activation(ffn_u[:, u % 2, :], ps[:, 2 + u % 2, :], ACT.Identity,
                                         bias=b_up[:, f:f + 1]).then_inc(up_copied.sem, 1)
                    act.wait_ge(gate_lim.sem, gate_lim.at(b, u + 1))
                    nc.scalar.activation(ffn_t[:, u % 2, :], ffn_g[:, u % 2, :], ACT.Tanh, scale=0.5 * ALPHA
                                         ).then_inc(tanh_done.sem, 1)
                    if u == FLOW_TANH:
                        act.wait_ge(z_ready.sem, z_ready.at(b, NT))
                        nc.scalar.activation(qkv[:, :, 0:2 * D], qkv[:, :, 0:2 * D], ACT.Tanh, scale=0.5
                                             ).then_inc(sig_tanh.sem, 1)
                    if u in (FLOW_SUMS2, FLOW_SUMS2 + 1):
                        c = u - FLOW_SUMS2
                        act.wait_ge(qnT_mm.sem, qnT_mm.at(b, c + 1))
                        nc.scalar.copy(q_normT[:, c * BANK:(c + 1) * BANK], ps[:, 6, :]).then_inc(qnT_ready.sem, 1)
                    if u == FLOW_ALLOC:
                        act.wait_ge(conserved_ready.sem, conserved_ready.at(b, 1))
                        nc.scalar.activation(sink_alloc[:, :], conserved[:, 0, :], ACT.Tanh, scale=0.5
                                             ).then_inc(flow_act.sem, 1)
                        nc.scalar.activation(source_exp[:, :], conserved[:, 1, :], ACT.Exp).then_inc(flow_act.sem, 1)
                    if u == FLOW_OUT + 2:
                        for c in range(2):
                            act.wait_ge(headsT_mm.sem, headsT_mm.at(b, c + 1))
                            nc.scalar.copy(heads_outT[:, c * BANK:(c + 1) * BANK], ps[:, 6 + c, :]
                                           ).then_inc(headsT_ready.sem, 1)
                experts_out(b, 1)

        @block.vector
        def _(dve):
            dve.wait_ge(weights_in.sem, ALL_WEIGHTS)
            dve.wait_ge(prep_mm.sem, 1)
            for h in range(H0):
                for half in range(2):
                    nc.vector.tensor_scalar(absorbed[:, h, half * KD:half * KD + DC],
                                            ps[0:DC + 1, 0, h * DC:(h + 1) * DC], SCALE, None, ALU.mult)
                    last = nc.vector.tensor_scalar(absorbed[:, h, half * KD + DC:(half + 1) * KD], q_rope[:, h, :],
                                                   SCALE, None, ALU.mult)
                last.then_inc(prep_sb.sem, 1)
            dve.wait_ge(prep_mm.sem, 2)
            nc.vector.tensor_copy(w_q[:, :, :].rearrange("p a b -> p (a b)"), banks(2)).then_inc(prep_sb.sem, 1)
            nc.vector.tensor_copy(b_q[:, :], ps[:, 1, 0:H0]).then_inc(prep_sb.sem, 1)
            nc.vector.tensor_copy(w_o[:, :, :].rearrange("p a b -> p (a b)"), ps[:, 4, 0:QUADS * D]
                                  ).then_inc(prep_sb.sem, 1)
            nc.vector.tensor_tensor(b_o[:, :], ps[:, 5, 0:D], b_o_in, ALU.add).then_inc(prep_sb.sem, 1)
            nc.vector.tensor_scalar(b_up[:, :], b_up[:, :], 1.0, None, ALU.add).then_inc(prep_sb.sem, 1)
            dve.wait_ge(prep_sb.sem, H0 + 5)

            with dve.Fori(0, BATCH) as index:
                b = Sequence(dve, index)
                count = [0]

                def link(ins, aggregates_next=False):
                    count[0] += 1
                    ins.then_inc(dve_step.sem, 1)
                    dve.wait_ge(dve_step.sem, dve_step.at(b, count[0]))
                    if aggregates_next:
                        nc.vector.memset(spare[:, 0:1], 0.0)

                def layer_norm(l, x):
                    for n in range(NT):
                        last = nc.vector.bn_stats(stats[:, n, :], x[:, n, :])
                    link(last, aggregates_next=True)
                    for n in range(NT):
                        last = nc.vector.bn_aggr(mean_var[:, n, :], stats[:, n, :])
                    link(last)
                    nc.vector.tensor_scalar(var_eps[:, :], mean_var[:, :, 1], LN_EPS, None, ALU.add
                                            ).then_inc(var_ready.sem, 1)
                    dve.wait_ge(rstd_ready.sem, rstd_ready.at(b, l + 1))
                    for n in range(NT):
                        nc.vector.tensor_scalar(x_norm[:, n, :], x[:, n, :], mean_var[:, n, 0:1], rstd[:, n:n + 1],
                                                ALU.subtract, ALU.mult).then_inc(norm_ready.sem, 1)

                def wide(v):
                    return v.unsqueeze(2).to_broadcast([P, NT, E])

                def ranks():
                    by_j = logits[:, :, :].unsqueeze(2).to_broadcast([P, NT, E, E])
                    by_e = logits[:, :, :].unsqueeze(3).to_broadcast([P, NT, E, E])
                    nc.vector.tensor_tensor(pair_a, by_j, by_e, ALU.is_gt)
                    link(nc.vector.tensor_tensor(pair_b, by_j, by_e, ALU.is_equal))
                    yield
                    link(nc.vector.tensor_tensor(pair_b, pair_b,
                                                 earlier[:, :, :].unsqueeze(1).to_broadcast([P, NT, E, E]), ALU.mult))
                    yield
                    link(nc.vector.tensor_tensor(pair_a, pair_a, pair_b, ALU.add))
                    yield
                    link(nc.vector.tensor_reduce(rank[:, :, :], pair_a, X, ALU.add))
                    yield

                def route_two():
                    dve.wait_ge(logits_mm.sem, logits_mm.at(b, 1))
                    link(nc.vector.tensor_copy(logits[:, :, :].rearrange("p n e -> p (n e)"), ps[:, 7, 256:256 + NT * E]))
                    yield
                    link(nc.vector.tensor_reduce(top1[:, :], logits[:, :, :], X, ALU.max))
                    yield
                    nc.vector.tensor_tensor(r_a[:, :, :], logits[:, :, :], wide(top1[:, :]), ALU.subtract
                                            ).then_inc(shift_ready.sem, 1)
                    yield
                    yield from ranks()
                    link(nc.vector.tensor_scalar(r_b[:, :, :], rank[:, :, :], 0.0, MINUS_INF, ALU.is_equal, ALU.mult))
                    yield
                    link(nc.vector.tensor_tensor(r_b[:, :, :], r_b[:, :, :], logits[:, :, :], ALU.add))
                    yield
                    link(nc.vector.tensor_reduce(top2[:, :], r_b[:, :, :], X, ALU.max))
                    yield
                    nc.vector.tensor_tensor(r_c[:, :, :], r_b[:, :, :], wide(top2[:, :]), ALU.subtract
                                            ).then_inc(shift_ready.sem, 1)
                    yield
                    link(nc.vector.scalar_tensor_tensor(r_d[:, :, :], logits[:, :, :], -1.0, logits[:, :, :],
                                                        ALU.mult, ALU.max))
                    yield
                    for k, (top, total) in enumerate(((top1, r_s1), (top2, r_s2))):
                        link(nc.vector.tensor_tensor(r_e[:, :, :], r_d[:, :, :], wide(top[:, :]), ALU.max))
                        yield
                        link(nc.vector.tensor_tensor(gate_w[:, :, :], logits[:, :, :], wide(top[:, :]), ALU.subtract))
                        yield
                        link(nc.vector.scalar_tensor_tensor(r_e[:, :, :], r_e[:, :, :], JITTER2, gate_w[:, :, :],
                                                            ALU.mult, ALU.add))
                        yield
                        dve.wait_ge(r_exp_done.sem, r_exp_done.at(b, k + 1))
                        link(nc.vector.scalar_tensor_tensor(r_e[:, :, :], r_e[:, :, :], 0.0, r_exp[:, k, :, :],
                                                            ALU.is_ge, ALU.mult))
                        yield
                        link(nc.vector.tensor_reduce(total[:, :], r_e[:, :, :], X, ALU.add))
                        yield
                        link(nc.vector.reciprocal(total[:, :], total[:, :]))
                        yield
                    link(nc.vector.scalar_tensor_tensor(r_e[:, :, :], rank[:, :, :], 0.0, wide(r_s1[:, :]),
                                                        ALU.is_equal, ALU.mult))
                    yield
                    link(nc.vector.scalar_tensor_tensor(r_d[:, :, :], rank[:, :, :], 1.0, wide(r_s2[:, :]),
                                                        ALU.is_equal, ALU.mult))
                    yield
                    nc.vector.tensor_tensor(gate_w[:, :, :], r_e[:, :, :], r_d[:, :, :], ALU.add
                                            ).then_inc(gate_ready.sem, 1)
                    yield

                def route_four():
                    dve.wait_ge(logits_mm.sem, logits_mm.at(b, 2))
                    link(nc.vector.tensor_tensor(
                        logits[:, :, :], ps[:, 7, 256:256 + NT * E].rearrange("p (n e) -> p n e", e=E),
                        b_router[:, :].unsqueeze(1).to_broadcast([P, NT, E]), ALU.add))
                    link(nc.vector.tensor_reduce(top1[:, :], logits[:, :, :], X, ALU.max))
                    nc.vector.tensor_tensor(r_a[:, :, :], logits[:, :, :], wide(top1[:, :]), ALU.subtract
                                            ).then_inc(shift_ready.sem, 1)
                    for _ in ranks():
                        pass
                    dve.wait_ge(r_exp_done.sem, r_exp_done.at(b, 3))
                    link(nc.vector.scalar_tensor_tensor(r_e[:, :, :], rank[:, :, :], TOP_K - 0.5, r_exp[:, 0, :, :],
                                                        ALU.is_lt, ALU.mult))
                    link(nc.vector.tensor_reduce(r_s1[:, :], r_e[:, :, :], X, ALU.add))
                    link(nc.vector.reciprocal(r_s1[:, :], r_s1[:, :]))
                    nc.vector.tensor_tensor(gate_w[:, :, :], r_e[:, :, :], wide(r_s1[:, :]), ALU.mult
                                            ).then_inc(gate_ready.sem, 1)

                def experts_add(l):
                    for c in range(2):
                        dve.wait_ge(y_mm.sem, y_mm.at(b, 2 * l + c + 1))
                        link(nc.vector.tensor_tensor(
                            x_mid[:, 4 * c:4 * c + 4, :], x_mid[:, 4 * c:4 * c + 4, :],
                            ps[:, c, :].rearrange("p (n d) -> p n d", d=D), ALU.add))

                dve.wait_ge(x_loaded.sem, x_loaded.at(b, 16))
                layer_norm(0, x_in)
                route = route_two()
                dve.wait_ge(y_stored.sem, y_stored.at(b, 0))
                count[0] += 1
                nc.vector.tensor_tensor(x_mid[:, :, :], x_in[:, :, :],
                                        b_o[:, :].unsqueeze(1).to_broadcast([P, NT, D]), ALU.add
                                        ).then_inc(dve_step.sem, 1)
                dve.wait_ge(dve_step.sem, dve_step.at(b, count[0]))
                dve.wait_ge(norm_ready.sem, norm_ready.at(b, NT))
                nc.vector.tensor_copy(var_eps[:, 0:1], var_eps[:, 0:1]).then_inc(x_taken.sem, 1)

                dve.wait_ge(k_proj.sem, k_proj.at(b, 1))
                nc.vector.tensor_scalar(keys[0:KD, :], banks(0)[0:KD, :], b_k[0:KD, :], None, ALU.add)
                high = probs[KD:P, 1, :]
                link(nc.vector.tensor_scalar(high.bitcast(F32R), banks(0)[KD:P, :], b_k[KD:P, :], None, ALU.add))
                nc.vector.scalar_tensor_tensor(keys[KD:P, :], banks(0)[KD:P, :], b_k[KD:P, :], high,
                                               ALU.add, ALU.subtract).then_inc(keys_ready.sem, 1)
                dve.wait_ge(latent_mm.sem, latent_mm.at(b, 1))
                next(route)
                nc.vector.tensor_tensor(latent[:, :, :], ps[:, 7, 0:NT * DC].rearrange("p (n c) -> p n c", c=DC),
                                        b_dkv[:, :].unsqueeze(1).to_broadcast([P, NT, DC]), ALU.add
                                        ).then_inc(latent_ready.sem, 1)

                def attention_step(w):
                    h, t = use_of(w)
                    if h is not None:
                        dve.wait_ge(q_high.sem, q_high.at(b, h + 1))
                        nc.vector.scalar_tensor_tensor(
                            q_parts[:, h % QUAD, 1, :], banks(2 * (h % 2)), b_q[:, h:h + 1],
                            q_parts[:, h % QUAD, 0, :].bitcast(F32), ALU.add, ALU.subtract).then_inc(q_ready.sem, 1)
                    if t is not None:
                        dve.wait_ge(scores_ready.sem, scores_ready.at(b, t + 1))
                        if t >= 4:
                            dve.wait_ge(exp_done.sem, exp_done.at(b, t - 3))
                        nc.vector.tensor_reduce(neg_max[:, t % 4:t % 4 + 1], banks(2 * (t % 2)), X, ALU.max,
                                                negate=True).then_inc(max_ready.sem, 1)
                    if ROUTER_STEP <= w < GATES_STEP:
                        next(route, None)
                    t = use_of(w - T_LAG)[1]
                    if t is not None:
                        dve.wait_ge(pT_high.sem, pT_high.at(b, t + 1))
                        if t >= 2 * QUAD:
                            dve.wait_ge(u_ready.sem, u_ready.at(b, t // QUAD - 1))
                        nc.vector.tensor_copy(probsT[:, t % (2 * QUAD), BANK:SEQ], ps[:, 5, :]
                                              ).then_inc(high_copied.sem, 1)
                    g = group_at(w, INV_LAG)
                    if g is not None:
                        dve.wait_ge(exp_done.sem, exp_done.at(b, (g + 1) * QUAD))
                        if g >= 2:
                            dve.wait_ge(u_ready.sem, u_ready.at(b, g - 1))
                        nc.vector.reciprocal(inv_sum[:, g % 2, :], row_sum[:, g % 2, :]).then_inc(inv_ready.sem, 1)
                    g = group_at(w, SCALED_LAG)
                    if g is not None:
                        dve.wait_ge(scale_ready.sem, scale_ready.at(b, g + 1))
                        if g >= 2:
                            dve.wait_ge(o_ready.sem, o_ready.at(b, g - 1))
                        nc.vector.tensor_tensor(o_latent[:, g % 2, :], ps[:, 6 + g % 2, 0:P],
                                                scale_sb[:, g % 2, :], ALU.mult).then_inc(u_scaled.sem, 1)
                    g = group_at(w, ADDED_LAG)
                    if g is not None:
                        n = g % NT
                        dve.wait_ge(o_ready.sem, o_ready.at(b, g + 1))
                        if g >= NT:
                            dve.wait_ge(o_added.sem, o_added.at(b, g - NT + 1))
                        nc.vector.tensor_tensor(x_mid[:, n, :], x_mid[:, n, :],
                                                ps[:, 6 + g % 2, 2 * P:3 * P], ALU.add
                                                ).then_inc(o_added.sem, 1)

                for w in range(UNIT_STEP):
                    attention_step(w)
                    if w == GATES_STEP:
                        assert next(route, "end") == "end"

                for u in range(UNITS):
                    dve.wait_ge(tanh_done.sem, tanh_done.at(b, u + 1))
                    nc.vector.scalar_tensor_tensor(ffn_g[:, u % 2, :], ffn_t[:, u % 2, :], 1.0, ps[:, u % 2, :],
                                                   ALU.add, ALU.mult).then_inc(g_free.sem, 1)
                    dve.wait_ge(g_free.sem, g_free.at(b, u + 1))
                    if u >= 2:
                        dve.wait_ge(h_ready.sem, h_ready.at(b, u - 1))
                    nc.vector.tensor_tensor(ffn_gu[:, u % 2, :], ffn_g[:, u % 2, :], ps[:, 2 + u % 2, :], ALU.mult
                                            ).then_inc(gu_done.sem, 1)
                    attention_step(UNIT_STEP + u)
                dve.wait_ge(o_added.sem, o_added.at(b, GROUPS))
                experts_add(0)
                layer_norm(1, x_mid)
                dve.wait_ge(norm_ready.sem, norm_ready.at(b, 2 * NT))
                link(nc.vector.tensor_tensor(x_mid[:, :, :], x_mid[:, :, :],
                                             b_proj[:, :].unsqueeze(1).to_broadcast([P, NT, D]), ALU.add))
                route_four()
                q, k, v = qkv[:, :, 0:D], qkv[:, :, D:2 * D], qkv[:, :, 2 * D:3 * D]

                def heads(x):
                    return x.rearrange("p n (h d) -> p n h d", d=D1)

                def per_head(x):
                    return x.rearrange("p (n h) -> p n h", n=NT).unsqueeze(3).to_broadcast([P, NT, H1, D1])

                def flow(dst, x, total):
                    link(nc.vector.scalar_tensor_tensor(tmp, x, EPS1, total.unsqueeze(1).to_broadcast([P, NT, D]),
                                                        ALU.add, ALU.mult))
                    link(nc.vector.tensor_reduce(dst, tmp.rearrange("p n (h d) -> p (n h) d", d=D1), X, ALU.add))

                def flow_step(u):
                    if u < FLOW_TANH:
                        for n in (2 * u, 2 * u + 1):
                            dve.wait_ge(qkv_mm.sem, qkv_mm.at(b, n + 1))
                            nc.vector.tensor_tensor(qkv[:, n, :], ps[:, 6 + n % 2, 0:3 * D], b_qkv[:, :], ALU.add
                                                    ).then_inc(z_ready.sem, 1)
                    if u == FLOW_TANH + 1:
                        dve.wait_ge(sig_tanh.sem, sig_tanh.at(b, 1))
                        nc.vector.tensor_scalar(qkv[:, :, 0:2 * D], qkv[:, :, 0:2 * D], 0.5, 0.5, ALU.mult, ALU.add
                                                ).then_inc(qk_ready.sem, 1)
                    if u == FLOW_WEIGHTS:
                        dve.wait_ge(sums_mm.sem, sums_mm.at(b, 1))
                        link(nc.vector.tensor_scalar(sums_eps[:, :], ps[:, 6, 0:2 * D], EPS1, None, ALU.add))
                        flow(inv_flow[:, 0, :], q, sums_eps[:, D:2 * D])
                    if u == FLOW_WEIGHTS + 1:
                        flow(inv_flow[:, 1, :], k, sums_eps[:, 0:D])
                    if u == FLOW_WEIGHTS + 2:
                        link(nc.vector.reciprocal(inv_flow[:, :, :], inv_flow[:, :, :]))
                        nc.vector.tensor_tensor(heads(weighted[:, :, 0:D]), heads(q), per_head(inv_flow[:, 0, :]),
                                                ALU.mult)
                    if u == FLOW_WEIGHTS + 3:
                        nc.vector.tensor_tensor(heads(weighted[:, :, D:2 * D]), heads(k), per_head(inv_flow[:, 1, :]),
                                                ALU.mult).then_inc(weighted_ready.sem, 1)
                    if u == FLOW_CONSERVED:
                        dve.wait_ge(sums_mm.sem, sums_mm.at(b, 2))
                        link(nc.vector.tensor_scalar(sums2_eps[:, :], ps[:, 7, 0:2 * D], EPS1, None, ALU.add))
                        flow(conserved[:, 0, :], q, sums2_eps[:, D:2 * D])
                    if u == FLOW_CONSERVED + 1:
                        flow(conserved[:, 1, :], k, sums2_eps[:, 0:D])
                        link(nc.vector.tensor_scalar(conserved[:, :, :], conserved[:, :, :], EPS1, None, ALU.add))
                        nc.vector.tensor_scalar(conserved[:, 1, :], conserved[:, 1, :], 1.0, -1.0, ALU.min, ALU.max
                                                ).then_inc(conserved_ready.sem, 1)
                    if u == FLOW_VALUES:
                        dve.wait_ge(flow_act.sem, flow_act.at(b, 1))
                        link(nc.vector.tensor_scalar(sink_alloc[:, :], sink_alloc[:, :], 0.5, 0.5, ALU.mult, ALU.add))
                        dve.wait_ge(flow_act.sem, flow_act.at(b, 2))
                        nc.vector.tensor_tensor(heads(v_comp), heads(v), per_head(source_exp[:, :]), ALU.mult
                                                ).then_inc(v_ready.sem, 1)
                    if u == FLOW_KV + 1:
                        dve.wait_ge(kv_mm.sem, kv_mm.at(b, 1))
                        link(nc.vector.tensor_reduce(
                            source_inv[:, :], ps[:, 7, 0:NT * H1].rearrange("p (n h) -> p h n", n=NT), X, ALU.add))
                        nc.vector.reciprocal(source_inv[:, :], source_inv[:, :])
                        link(nc.vector.scalar_tensor_tensor(kv[:, :], ps[:, 6, 0:D], float(SEQ),
                                                            same_head[:, :, :].rearrange("p h d -> p (h d)"),
                                                            ALU.mult, ALU.mult))
                        nc.vector.tensor_tensor(kv[:, :].rearrange("p (h d) -> p h d", d=D1),
                                                kv[:, :].rearrange("p (h d) -> p h d", d=D1),
                                                source_inv[:, :].unsqueeze(2).to_broadcast([P, H1, D1]), ALU.mult
                                                ).then_inc(kv_ready.sem, 1)
                    if u == FLOW_OUT + 1:
                        for c in range(2):
                            dve.wait_ge(heads_mm.sem, heads_mm.at(b, c + 1))
                            half = slice(4 * c, 4 * c + 4)
                            nc.vector.tensor_tensor(heads(heads_out[:, half, :]),
                                                    ps[:, 6 + c, :].rearrange("p (n h d) -> p n h d", n=4, d=D1),
                                                    per_head(sink_alloc[:, :])[:, half, :, :], ALU.mult
                                                    ).then_inc(heads_ready.sem, 1)
                    if u == FLOW_PROJ + 1:
                        for c in range(2):
                            dve.wait_ge(proj_mm.sem, proj_mm.at(b, c + 1))
                            link(nc.vector.tensor_tensor(
                                x_mid[:, 4 * c:4 * c + 4, :], x_mid[:, 4 * c:4 * c + 4, :],
                                ps[:, 6 + c, :].rearrange("p (n d) -> p n d", d=D), ALU.add))

                for u in range(UNITS):
                    f = u // HALVES
                    dve.wait_ge(gu_ready.sem, gu_ready.at(b, UNITS + u + 1))
                    nc.vector.tensor_scalar(ffn_g[:, u % 2, :], ps[:, u % 2, :], b_gate[:, f:f + 1], LIMIT,
                                            ALU.add, ALU.min).then_inc(gate_lim.sem, 1)
                    dve.wait_ge(up_copied.sem, up_copied.at(b, u + 1))
                    nc.vector.tensor_scalar(ffn_u[:, u % 2, :], ffn_u[:, u % 2, :], 1.0 + LIMIT, 1.0 - LIMIT,
                                            ALU.min, ALU.max)
                    dve.wait_ge(tanh_done.sem, tanh_done.at(b, UNITS + u + 1))
                    nc.vector.scalar_tensor_tensor(ffn_g[:, u % 2, :], ffn_t[:, u % 2, :], 1.0, ffn_g[:, u % 2, :],
                                                   ALU.add, ALU.mult).then_inc(g_free.sem, 1)
                    dve.wait_ge(g_free.sem, g_free.at(b, UNITS + u + 1))
                    if u >= 2:
                        dve.wait_ge(h_ready.sem, h_ready.at(b, UNITS + u - 1))
                    nc.vector.tensor_tensor(ffn_gu[:, u % 2, :], ffn_g[:, u % 2, :], ffn_u[:, u % 2, :], ALU.mult
                                            ).then_inc(gu_done.sem, 1)
                    flow_step(u)
                experts_add(1)
                nc.vector.tensor_copy(var_eps[:, 0:1], var_eps[:, 0:1]).then_inc(y_done.sem, 1)
                assert count[0] == DVE_STEPS, count[0]

        @block.tensor
        def _(pe):
            pe.wait_ge(weights_in.sem, ALL_WEIGHTS)
            pe.wait_ge(pool_consts.sem, 9)
            for h in range(H0):
                mm = nc.tensor.matmul(ps[0:DC + 1, 0, h * DC:(h + 1) * DC], uq_T[:, h, :], uk_T[:, h, :],
                                      start=True, stop=True)
            mm.then_inc(prep_mm.sem, 1)
            for h in range(H0):
                nc.tensor.matmul(ps[DC * (h % QUAD):DC * (h % QUAD + 1), 4, (h // QUAD) * D:(h // QUAD + 1) * D],
                                 uv_T[:, h, :], wo_heads[:, h, :], start=True, stop=True)
            for h in range(H0):
                nc.tensor.matmul(ps[:, 5, 0:D], b_uv[:, h:h + 1].to_broadcast([P, P]), wo_heads[:, h, :],
                                 start=(h == 0), stop=(h == H0 - 1))
            pe.wait_ge(prep_sb.sem, H0)
            for h in range(H0):
                nc.tensor.matmul(ps[:, 1, h:h + 1], absorbed[:, h, :], b_dq1, start=True, stop=True)
            for c in range(2):
                last = nc.tensor.matmul(ps[:, 2 + c, :], dq_T,
                                        absorbed[0:DC, 4 * c:4 * c + 4, :].rearrange("p a b -> p (a b)"),
                                        start=True, stop=True)
            last.then_inc(prep_mm.sem, 1)
            pe.wait_ge(prep_sb.sem, H0 + 5)
            pe.wait_ge(prep_act.sem, 2)

            def transpose_norm(b, l):
                for n in range(NT):
                    pe.wait_ge(norm_ready.sem, norm_ready.at(b, l * NT + n + 1))
                    mm = nc.tensor.transpose(ps[:, 4 + n // 4, (n % 4) * P:(n % 4 + 1) * P], x_norm[:, n, :],
                                             ident[:, :])
                    if n % 4 == 3:
                        mm.then_inc(normT_ready.sem, 1)

            def router(b, l):
                for n in range(NT):
                    mm = nc.tensor.matmul(ps[:, 7, 256 + n * E:256 + (n + 1) * E], xT[:, n * P:(n + 1) * P], w_router[l][:, :],
                                          start=True, stop=True)
                mm.then_inc(logits_mm.sem, 1)

            def gates_transpose(b, l):
                pe.wait_ge(gate_ready.sem, gate_ready.at(b, l + 1))
                for n in range(NT):
                    mm = nc.tensor.transpose(ps[0:E, 4 + n // 4, (n % 4) * P:(n % 4 + 1) * P], gate_w[:, n, :],
                                             ident[:, :])
                mm.then_inc(gateT_mm.sem, 1)

            def experts(b, l, beside=None):
                def gate_up(u):
                    f, c = u // HALVES, u % HALVES
                    if u >= 2:
                        pe.wait_ge(gu_done.sem, gu_done.at(b, l * UNITS + u - 1))
                    tokens = xT[:, c * BANK:(c + 1) * BANK]
                    nc.tensor.matmul(ps[:, u % 2, :], w_gate[l][:, f * P:(f + 1) * P], tokens, start=True, stop=True)
                    nc.tensor.matmul(ps[:, 2 + u % 2, :], w_up[l][:, f * P:(f + 1) * P], tokens, start=True, stop=True
                                     ).then_inc(gu_ready.sem, 1)

                def down(u):
                    f, c = u // HALVES, u % HALVES
                    pe.wait_ge(h_ready.sem, h_ready.at(b, l * UNITS + u + 1))
                    nc.tensor.matmul(ps[:, 4 + c, :], w_down[l][:, f, :], ffn_h[:, u % 2, :], start=(l == 0 and f == 0),
                                     stop=(f == E * FH - 1)).then_inc(down_done.sem, 1)

                if l == 0:
                    pe.wait_ge(low_copied.sem, low_copied.at(b, TILES))
                    pe.wait_ge(high_copied.sem, high_copied.at(b, TILES))
                else:
                    pe.wait_ge(gateT_ready.sem, gateT_ready.at(b, 2))
                    for c in range(HALVES):
                        nc.tensor.matmul(ps[:, 4 + c, :], b_down[:, :], gate_wT[:, c * BANK:(c + 1) * BANK],
                                         start=True, stop=False)
                for u in range(UNITS + 2):
                    if u < UNITS:
                        gate_up(u)
                    if beside and u < UNITS:
                        beside(u)
                    if u >= 2:
                        down(u - 2)
                for n in range(NT):
                    if n % 4 == 0:
                        pe.wait_ge(yT_ready.sem, yT_ready.at(b, 2 * l + n // 4 + 1))
                    mm = nc.tensor.transpose(ps[:, n // 4, (n % 4) * P:(n % 4 + 1) * P], y_T[:, n * P:(n + 1) * P],
                                             ident[:, :])
                    if n % 4 == 3:
                        mm.then_inc(y_mm.sem, 1)

            with pe.Fori(0, BATCH) as index:
                b = Sequence(pe, index)
                transpose_norm(b, 0)
                pe.wait_ge(xT_ready.sem, xT_ready.at(b, 2))
                for c in range(HALVES):
                    mm = nc.tensor.matmul(ps[:, c, :], w_k[:, :], xT[:, c * BANK:(c + 1) * BANK], start=True, stop=True)
                mm.then_inc(k_proj.sem, 1)
                for n in range(NT):
                    mm = nc.tensor.matmul(ps[:, 7, n * DC:(n + 1) * DC], xT[:, n * P:(n + 1) * P], w_dkv[:, :],
                                          start=True, stop=True)
                mm.then_inc(latent_mm.sem, 1)
                router(b, 0)

                def scores(t):
                    j, n = t % QUAD, (t // QUAD) % NT
                    if n == 0:
                        pe.wait_ge(q_ready.sem, q_ready.at(b, (t // (NT * QUAD)) * QUAD + j + 1))
                    for c in range(HALVES):
                        for part in range(2):
                            mm = nc.tensor.matmul(ps[:, 2 * (t % 2) + c, :], q_parts[:, j, part, n * P:(n + 1) * P],
                                                  keys[:, c * BANK:(c + 1) * BANK], start=(part == 0),
                                                  stop=(part == 1))
                    mm.then_inc(scores_ready.sem, 1)

                def transpose_probs(t):
                    pe.wait_ge(exp_done.sem, exp_done.at(b, t + 1))
                    for c, (copied, done) in enumerate(((low_copied, pT_low), (high_copied, pT_high))):
                        if t >= 1:
                            pe.wait_ge(copied.sem, copied.at(b, t))
                        if t == NT * QUAD:
                            pe.wait_ge(gateT_ready.sem, gateT_ready.at(b, 1))
                        for i in range(4):
                            k = 4 * c + i
                            mm = nc.tensor.transpose(ps[:, 4 + c, i * P:(i + 1) * P],
                                                     probs[:, t % 3, k * P:(k + 1) * P], ident[:, :])
                        mm.then_inc(done.sem, 1)

                def values(g, i):
                    if i == 0:
                        pe.wait_ge(low_copied.sem, low_copied.at(b, (g + 1) * QUAD))
                        pe.wait_ge(high_copied.sem, high_copied.at(b, (g + 1) * QUAD))
                        if g == 0:
                            pe.wait_ge(latent_ready.sem, latent_ready.at(b, 1))
                        if g >= 2:
                            pe.wait_ge(o_added.sem, o_added.at(b, g - 1))
                    for k in (2 * i, 2 * i + 1):
                        for j in range(QUAD):
                            nc.tensor.matmul(ps[DC * j:DC * (j + 1), 6 + g % 2, 0:P], latent[:, k, :],
                                             probsT[:, (g % 2) * QUAD + j, k * P:(k + 1) * P],
                                             start=(k == 0), stop=(k == NT - 1))
                    if i == 3:
                        pe.wait_ge(inv_ready.sem, inv_ready.at(b, g + 1))
                        for j in range(QUAD):
                            mm = nc.tensor.matmul(ps[DC * j:DC * (j + 1), 6 + g % 2, P:2 * P],
                                                  inv_sum[:, g % 2, j:j + 1].to_broadcast([P, DC]), ident[:, :],
                                                  start=True, stop=True)
                        mm.then_inc(u_ready.sem, 1)

                def output(g):
                    pe.wait_ge(u_scaled.sem, u_scaled.at(b, g + 1))
                    nc.tensor.matmul(ps[:, 6 + g % 2, 2 * P:3 * P], o_latent[:, g % 2, :], w_o[:, g // NT, :],
                                     start=True, stop=True).then_inc(o_ready.sem, 1)

                def queries(h):
                    for c in range(HALVES):
                        mm = nc.tensor.matmul(ps[:, 2 * (h % 2) + c, :], w_q[:, h, :],
                                              xT[:, c * BANK:(c + 1) * BANK], start=True, stop=True)
                    mm.then_inc(q_proj.sem, 1)

                def attention_step(w):
                    before_h, before_t = use_of(w - 2)
                    if w < 2:
                        pe.wait_ge(keys_ready.sem, keys_ready.at(b, 1))
                    elif w < STEPS and before_h is not None:
                        pe.wait_ge(q_ready.sem, q_ready.at(b, before_h + 1))
                    elif w < STEPS:
                        pe.wait_ge(exp_done.sem, exp_done.at(b, before_t + 1))
                    h, t = use_of(w)
                    if h is not None:
                        queries(h)
                    if t is not None:
                        scores(t)
                    t = use_of(w - T_LAG)[1]
                    if t is not None:
                        transpose_probs(t)
                    if w == GATES_STEP:
                        pe.wait_ge(low_copied.sem, low_copied.at(b, NT * QUAD))
                        pe.wait_ge(high_copied.sem, high_copied.at(b, NT * QUAD))
                        gates_transpose(b, 0)
                    g = group_at(w, OUTPUT_LAG)
                    if g is not None:
                        output(g)
                    for i in range(4):
                        g = group_at(w, VALUES_LAG + i)
                        if g is not None:
                            values(g, i)

                for w in range(UNIT_STEP):
                    attention_step(w)
                pe.wait_ge(exp_done.sem, exp_done.at(b, TILES))
                experts(b, 0, lambda u: attention_step(UNIT_STEP + u))

                transpose_norm(b, 1)
                pe.wait_ge(xT_ready.sem, xT_ready.at(b, 4))
                router(b, 1)
                gates_transpose(b, 1)

                def flow_step(u):
                    if u < FLOW_TANH:
                        for n in (2 * u, 2 * u + 1):
                            if n >= 2:
                                pe.wait_ge(z_ready.sem, z_ready.at(b, n - 1))
                            nc.tensor.matmul(ps[:, 6 + n % 2, 0:3 * D], xT[:, n * P:(n + 1) * P], w_qkv[:, :],
                                             start=True, stop=True).then_inc(qkv_mm.sem, 1)
                    if u == FLOW_SUMS:
                        pe.wait_ge(qk_ready.sem, qk_ready.at(b, 1))
                        for n in range(NT):
                            mm = nc.tensor.matmul(ps[:, 6, 0:2 * D], ones[:, :], qkv[:, n, 0:2 * D], start=(n == 0),
                                                  stop=(n == NT - 1))
                        mm.then_inc(sums_mm.sem, 1)
                    if u == FLOW_SUMS2:
                        pe.wait_ge(weighted_ready.sem, weighted_ready.at(b, 1))
                        for n in range(NT):
                            mm = nc.tensor.matmul(ps[:, 7, 0:2 * D], ones[:, :], weighted[:, n, :], start=(n == 0),
                                                  stop=(n == NT - 1))
                        mm.then_inc(sums_mm.sem, 1)
                    if u in (FLOW_SUMS2, FLOW_SUMS2 + 1):
                        c = u - FLOW_SUMS2
                        if c == 1:
                            pe.wait_ge(qnT_ready.sem, qnT_ready.at(b, 1))
                        for i in range(4):
                            mm = nc.tensor.transpose(ps[:, 6, i * P:(i + 1) * P], weighted[:, 4 * c + i, 0:D],
                                                     ident[:, :])
                        mm.then_inc(qnT_mm.sem, 1)
                    if u == FLOW_KV:
                        pe.wait_ge(v_ready.sem, v_ready.at(b, 1))
                        for n in range(NT):
                            nc.tensor.matmul(ps[:, 6, 0:D], qkv[:, n, D:2 * D], v_comp[:, n, :], start=(n == 0),
                                             stop=(n == NT - 1))
                        nc.tensor.matmul(ps[:, 7, 0:NT * H1], ones[:, :], source_exp[:, :], start=True, stop=True
                                         ).then_inc(kv_mm.sem, 1)
                    if u == FLOW_OUT:
                        pe.wait_ge(kv_ready.sem, kv_ready.at(b, 1))
                        pe.wait_ge(qnT_ready.sem, qnT_ready.at(b, 2))
                        for n in range(NT):
                            mm = nc.tensor.matmul(ps[:, 6 + n // 4, (n % 4) * D:(n % 4 + 1) * D],
                                                  q_normT[:, n * P:(n + 1) * P], kv[:, :], start=True, stop=True)
                            if n % 4 == 3:
                                mm.then_inc(heads_mm.sem, 1)
                    if u == FLOW_OUT + 2:
                        for n in range(NT):
                            if n % 4 == 0:
                                pe.wait_ge(heads_ready.sem, heads_ready.at(b, n // 4 + 1))
                            mm = nc.tensor.transpose(ps[:, 6 + n // 4, (n % 4) * P:(n % 4 + 1) * P],
                                                     heads_out[:, n, :], ident[:, :])
                            if n % 4 == 3:
                                mm.then_inc(headsT_mm.sem, 1)
                    if u == FLOW_PROJ:
                        pe.wait_ge(headsT_ready.sem, headsT_ready.at(b, 2))
                        for n in range(NT):
                            mm = nc.tensor.matmul(ps[:, 6 + n // 4, (n % 4) * D:(n % 4 + 1) * D],
                                                  heads_outT[:, n * P:(n + 1) * P], w_proj[:, :], start=True, stop=True)
                            if n % 4 == 3:
                                mm.then_inc(proj_mm.sem, 1)

                experts(b, 1, flow_step)


def kernel(**inputs):
    import concourse.bacc as _bacc
    from concourse.bass_utils import run_bass_kernel_spmd as _run

    def get(name):
        return np.asarray(inputs[name])

    def head_T(w, heads):
        return w.reshape(w.shape[0], heads, -1).transpose(2, 1, 0)

    def stack(w, bias):
        return np.concatenate([w, bias[None, :]], axis=0)

    a0, a1, f0, f1 = "L0_attn_", "L1_attn_", "L0_ffn_", "L1_ffn_"
    key_w = np.concatenate([get(a0 + "W_DKV"), get(a0 + "W_KR")], axis=1)
    key_b = np.concatenate([get(a0 + "b_DKV"), get(a0 + "b_KR")])
    gu = get(f1 + "gate_up_proj")
    gu_b = get(f1 + "gate_up_proj_bias")

    def up(w):
        return w.transpose(2, 0, 1).reshape(D, E * F)

    def down(w):
        return w.transpose(2, 0, 1).reshape(FH, P, E, D).transpose(1, 2, 0, 3).reshape(P, E * FH, D)

    def column(bias):
        return bias.reshape(E * FH, P).T

    arrays = {
        "x": get(a0 + "h_t"),
        "UQ_T": head_T(stack(get(a0 + "W_UQ"), get(a0 + "b_UQ")), H0),
        "UK_T": head_T(get(a0 + "W_UK"), H0),
        "UV_T": head_T(get(a0 + "W_UV"), H0),
        "W_O": get(a0 + "W_O").reshape(H0, DK, D).transpose(1, 0, 2),
        "b_UV": get(a0 + "b_UV").reshape(H0, DK).T,
        "DQ_T": get(a0 + "W_DQ").T,
        "b_DQ1": np.concatenate([get(a0 + "b_DQ"), np.ones(1, np.float32)])[:, None],
        "Q_rope": stack(get(a0 + "W_QR"), get(a0 + "b_QR")).reshape(DC + 1, H0, DR),
        "W_K": np.concatenate([key_w, key_w], axis=1),
        "b_K": np.concatenate([key_b, key_b])[:, None],
        "W_DKV": get(a0 + "W_DKV"),
        "gate0": up(get(f0 + "w_gate")),
        "up0": up(get(f0 + "w_up")),
        "down0": down(get(f0 + "w_down")),
        "router0": get(f0 + "router_w").T,
        "W_QKV": get(a1 + "qkv_w").T,
        "W_PROJ": get(a1 + "proj_w").T,
        "gate1": up(gu[:, 0:F, :]),
        "up1": up(gu[:, F:2 * F, :]),
        "down1": down(get(f1 + "down_proj")),
        "router1": get(f1 + "router_weight").T,
        "b_gate": column(gu_b[:, 0:F]),
        "b_up": column(gu_b[:, F:2 * F]),
        "b_down": get(f1 + "down_proj_bias"),
        "b_DKV": get(a0 + "b_DKV"),
        "b_O": get(a0 + "b_O"),
        "b_QKV": get(a1 + "qkv_b"),
        "b_PROJ": get(a1 + "proj_b"),
        "b_ROUTER": get(f1 + "router_bias"),
    }
    nc = _bacc.Bacc("TRN2", target_bir_lowering=False, num_devices=1)
    arrays = {f"in_{k}": np.ascontiguousarray(v) for k, v in arrays.items()}
    ins = {k[3:]: nc.dram_tensor(k, v.shape, mybir.dt.from_np(v.dtype), kind="ExternalInput").ap()
           for k, v in arrays.items()}
    out = nc.dram_tensor("out", (BATCH, SEQ, D), F32, kind="ExternalOutput").ap()
    nc.disable_value_cache = True
    two_layer_kernel(nc, ins, out)
    r = _run(nc, [arrays], core_ids=[0])
    return r.results[0]["out"]
```

```python
from contextlib import ExitStack

import numpy as np

import concourse.bass as bass
from concourse import mybir

F32 = mybir.dt.float32
F32R = mybir.dt.float32r
ALU = mybir.AluOpType
ACT = mybir.ActivationFunctionType
X = mybir.AxisListType.X

P = 128
BATCH = 8
SEQ = 1024
NT = SEQ // P
D = 128
BANK = 512
HALVES = SEQ // BANK
LN_EPS = 1e-5

H0, DK, DC, DR = 8, 128, 32, 32
KD = DC + DR
SCALE = 1.0 / float(np.sqrt(DK + DR))
QUAD = P // DC
QUADS = H0 // QUAD
GROUPS = QUADS * NT
TILES = GROUPS * QUAD

STEPS = H0 + TILES
T_LAG = 2
INV_LAG = 1
VALUES_LAG = 3
SCALES_LAG = 7
SCALED_LAG = 8
OUTPUT_LAG = 9
ADDED_LAG = 10
ROUTER_STEP = 8
ROUTER_EXP_STEPS = (18, 20)
GATES_STEP = QUAD + NT * QUAD + 3
UNIT_STEP = STEPS + T_LAG

NORM_STATS = 8
NORM_VAR = 13
NORM_APPLY = 17
NEXT_TRANSPOSE = 14

H1, D1 = 16, 8
EPS1 = 1e-6

E, F = 8, 256
FH = F // P
UNITS = E * FH * HALVES
JITTER2 = 0.02
TOP_K = 4
ALPHA, LIMIT = 1.702, 7.0
MINUS_INF = -3.0e38

EARLY_UNITS = 4

FLOW_SIGMOID = 0
FLOW_SUMS = 4
FLOW_WEIGHTS = (3, 4, 5, 6, 7, 8)
FLOW_BIAS = 22
FLOW_SUMS2 = 11
FLOW_CONSERVED = (10, 11, 12, 13)
FLOW_ALLOC = 14
FLOW_VALUES = 15
FLOW_KV = 19
FLOW_OUT = 22
FLOW_HEADS = 25
FLOW_PROJ = 28

DOWN_LAG = 4

DVE_STEPS = 50
DVE_STEPS_BEFORE = 2
POOL_STEPS = 2 * E + UNITS // 2


def step_of(t):
    return t + (t // (NT * QUAD) + 1) * QUAD


def use_of(w):
    quad, s = divmod(w, QUAD + NT * QUAD)
    if not 0 <= w < STEPS:
        return None, None
    return (quad * QUAD + s, None) if s < QUAD else (None, quad * NT * QUAD + s - QUAD)


def group_at(w, lag):
    t = use_of(w - lag)[1]
    return t // QUAD if t is not None and t % QUAD == QUAD - 1 else None


class Signal:

    def __init__(self, sem, per, start):
        self.sem, self.per, self.start = sem, per, start

    def at(self, b, k):
        return k if b is None else b.times(self.per) + (self.start + k)


class Sequence:

    def __init__(self, engine, index):
        self.engine, self.index, self.products = engine, index, {}

    def times(self, n):
        if n not in self.products:
            self.products[n] = self.engine.snap(self.index * n)
        return self.products[n]


def two_layer_kernel(nc, ins, out):
    with ExitStack() as ctx:
        def sb(name, shape, dt=F32):
            return ctx.enter_context(nc.sbuf_tensor(name, shape, dt))

        def signal(name, per=0, start=0):
            return Signal(ctx.enter_context(nc.semaphore(name)), per, start)

        x_in = sb("x_in", [P, NT, D])
        x_mid = sb("x_mid", [P, NT, D])
        xT = [sb(f"xT{l}", [P, SEQ]) for l in range(2)]
        stats = sb("stats", [P, NT, 6])
        mean_var = sb("mean_var", [P, NT, 2])
        var_eps = sb("var_eps", [P, NT])
        rstd = sb("rstd", [P, NT])
        spare = sb("spare", [P, 2])
        minus_half = sb("minus_half", [P, NT])

        keys = sb("keys", [P, SEQ], F32R)
        q_parts = sb("q_parts", [P, QUAD, 2, SEQ], F32R)
        probs = sb("probs", [P, 3, SEQ])
        probsT = sb("probsT", [P, 2 * QUAD, SEQ])
        latent = sb("latent", [P, NT, DC])
        neg_max = sb("neg_max", [P, 4])
        row_sum = sb("row_sum", [P, 2, QUAD])
        inv_sum = sb("inv_sum", [P, 2, QUAD])
        out_room = sb("out_room", [P, 2, 2, P])
        scale_sb, o_latent = out_room[:, 0, :, :], out_room[:, 1, :, :]

        x_high, x_low = q_parts[:, 0, 0, :], q_parts[:, 0, 1, :]
        w_split = q_parts[:, 1, :, :].rearrange("p a b -> p (a b)").rearrange("p (s h c) -> p s h c", s=4, h=2)

        room = probsT[:, :, :].rearrange("p a b -> p (a b)")
        qkv = room[:, 0:NT * 3 * D].rearrange("p (n c) -> p n c", n=NT)
        weighted = room[:, 3 * SEQ:5 * SEQ].rearrange("p (n c) -> p n c", n=NT)
        tmp = room[:, 5 * SEQ:6 * SEQ].rearrange("p (n c) -> p n c", n=NT)
        v_comp = room[:, 6 * SEQ:7 * SEQ].rearrange("p (n c) -> p n c", n=NT)
        q_normT = room[:, 7 * SEQ:8 * SEQ]
        heads_out, heads_outT = tmp, room[:, 6 * SEQ:7 * SEQ]
        flow_q, flow_k, flow_v = qkv[:, :, 0:D], qkv[:, :, D:2 * D], qkv[:, :, 2 * D:3 * D]

        def heads(x):
            return x.rearrange("p n (h d) -> p n h d", d=D1)

        def per_head(x):
            return x.rearrange("p (n h) -> p n h", n=NT).unsqueeze(3).to_broadcast([P, NT, H1, D1])

        sums_eps = latent[:, :, :].rearrange("p n c -> p (n c)")
        inv_flow = sb("inv_flow", [P, 2, NT * H1])
        conserved = weighted[:, 0:2, D:2 * D]
        sink_alloc = weighted[:, 2, D:2 * D]
        source_exp = weighted[:, 3, D:2 * D]
        kv = weighted[:, 4, D:2 * D]
        source_inv = sb("source_inv", [P, H1])

        logits = sb("logits", [P, NT, E])
        gate_w = sb("gate_w", [P, NT, E])
        r_a, r_b, r_c, r_d, r_e = (sb(f"r_{c}", [P, NT, E]) for c in "abcde")
        rank = sb("rank", [P, NT, E])
        top1, top2, r_s1, r_s2 = (sb(f"top_{c}", [P, NT]) for c in "abcd")
        r_exp = sb("r_exp", [P, 2, NT, E])
        gate_wT = sb("gate_wT", [E, SEQ])
        gate_rows = sb("gate_rows", [P, E // 4, SEQ])
        gate_bc = sb("gate_bc", [P, 2, SEQ])
        ffn_t = sb("ffn_t", [P, 2, BANK])
        ffn_g3, ffn_u4 = sb("ffn_g3", [P, 3, BANK]), sb("ffn_u4", [P, 4, BANK])
        ffn_g = [ffn_g3[:, i, :] for i in range(3)] + [out_room[:, :, :, :].rearrange("p a b c -> p (a b c)")]
        ffn_u = [ffn_u4[:, i, :] for i in range(4)]
        ffn_h4 = sb("ffn_h4", [P, BANK])
        ffn_gu = sb("ffn_gu", [P, 2, BANK])
        pair_a, pair_b = (t[:, 0, :].rearrange("p (n e j) -> p n e j", n=NT, e=E) for t in (ffn_t, ffn_gu))
        y_T = probs[:, 0, :]
        ffn_h = [probs[:, slot, c * BANK:(c + 1) * BANK] for slot in (0, 2) for c in range(2)] + [ffn_h4[:, :]]
        x_norm = [probs[:, l + 1, :].rearrange("p (n d) -> p n d", d=D) for l in range(2)]

        ident = sb("ident", [P, P])
        ones_column = sb("ones", [P, 1])
        ones = ones_column[:, :].to_broadcast([P, P])
        same_head = sb("same_head", [P, H1, D1])
        earlier = sb("earlier", [P, E, E])
        w_q = sb("w_q", [P, H0, P])
        b_q = sb("b_q", [P, H0])
        w_k = sb("w_k", [P, P])
        b_k = sb("b_k", [P, 1])
        w_dkv = sb("w_dkv", [P, DC])
        b_dkv = sb("b_dkv", [P, DC])
        w_o = sb("w_o", [P, QUADS, D])
        b_o = sb("b_o", [P, D])
        w_gate_up = [sb(f"w_gate_up{l}", [P, E * FH, 2, P]) for l in range(2)]
        w_down = [sb(f"w_down{l}", [P, E * FH, D]) for l in range(2)]
        w_router = [sb(f"w_router{l}", [P, E]) for l in range(2)]
        b_router = sb("b_router", [P, E])
        b_gate = sb("b_gate", [P, E * FH])
        b_up = sb("b_up", [P, E * FH])
        b_down = sb("b_down", [E, D])
        w_qkv = sb("w_qkv", [P, 3 * D])
        b_qkv = sb("b_qkv", [P, 3 * D])
        w_proj = sb("w_proj", [P, D])
        b_proj = sb("b_proj", [P, D])

        take = [0]

        def prep(parts, *shape):
            n = int(np.prod(shape))
            v = room[0:parts, take[0]:take[0] + n]
            take[0] += n
            return v.rearrange("p (a b) -> p a b", a=shape[0]) if len(shape) > 1 else v

        uq_T = prep(P, H0, DC + 1)
        uk_T = prep(P, H0, DC)
        uv_T = prep(P, H0, DC)
        wo_heads = prep(P, H0, D)
        b_uv = prep(P, H0)
        dq_T = prep(DC, D)
        b_dq1 = prep(DC + 1, 1)
        q_rope = prep(DC + 1, H0, DR)
        absorbed = prep(DC + 1, H0, P)
        b_o_in = prep(P, D)

        ps = ctx.enter_context(nc.psum_tensor("ps", [P, 8, BANK], F32))

        def banks(a, n=2):
            return ps[:, a:a + n, :].rearrange("p a b -> p (a b)")

        weights_in = signal("weights_in")
        pool_consts = signal("pool_consts")
        prep_mm = signal("prep_mm")
        prep_sb = signal("prep_sb")
        prep_act = signal("prep_act")
        x_loaded = signal("x_loaded", 16, start=16)
        x_taken = signal("x_taken", 1)
        y_stored = signal("y_stored", 16, start=1)
        dve_step = signal("dve_step", DVE_STEPS, start=DVE_STEPS_BEFORE)
        pool_step = signal("pool_step", POOL_STEPS)
        pool_carrier = signal("pool_carrier")
        var_ready = signal("var_ready", 2, start=1)
        rstd_ready = signal("rstd_ready", 2, start=1)
        norm_ready = signal("norm_ready", 2 * NT, start=NT)
        normT_ready = signal("normT_ready", 4, start=2)
        xT_ready = signal("xT_ready", 4, start=2)
        k_proj = signal("k_proj", 1, start=1)
        keys_high = signal("keys_high", 1, start=1)
        keys_ready = signal("keys_ready", 1, start=1)
        latent_mm = signal("latent_mm", 1)
        latent_ready = signal("latent_ready", 1)
        q_proj = signal("q_proj", H0)
        q_high = signal("q_high", H0)
        q_ready = signal("q_ready", H0)
        scores_ready = signal("scores_ready", TILES)
        max_ready = signal("max_ready", TILES)
        exp_done = signal("exp_done", TILES)
        pT_low = signal("pT_low", TILES)
        pT_high = signal("pT_high", TILES)
        low_copied = signal("low_copied", TILES)
        high_copied = signal("high_copied", TILES)
        inv_ready = signal("inv_ready", GROUPS)
        u_ready = signal("u_ready", GROUPS)
        scale_ready = signal("scale_ready", GROUPS)
        u_scaled = signal("u_scaled", GROUPS)
        o_ready = signal("o_ready", GROUPS)
        o_added = signal("o_added", GROUPS)
        x_high_ready = signal("x_high_ready", 2)
        x_low_ready = signal("x_low_ready", 2)
        w_high_ready = signal("w_high_ready", 2 * E * FH)
        w_low_ready = signal("w_low_ready", 2 * E * FH)
        logits_mm = signal("logits_mm", 2)
        shift_ready = signal("shift_ready", 3)
        r_exp_done = signal("r_exp_done", 3)
        gate_ready = signal("gate_ready", 2)
        gateT_mm = signal("gateT_mm", 2)
        gateT_ready = signal("gateT_ready", 2)
        rows_ready = signal("rows_ready", 64)
        gu_ready = signal("gu_ready", 2 * UNITS)
        gate_lim = signal("gate_lim", UNITS)
        tanh_done = signal("tanh_done", 2 * UNITS)
        gate_copied = signal("gate_copied", UNITS)
        up_copied = signal("up_copied", UNITS)
        g_free = signal("g_free", 2 * UNITS)
        gu_done = signal("gu_done", UNITS + UNITS // 2)
        h_ready = signal("h_ready", 2 * UNITS)
        down_done = signal("down_done", 2 * UNITS)
        yT_ready = signal("yT_ready", 4)
        y_mm = signal("y_mm", 4)
        y_added = signal("y_added", 4, start=1)
        qkv_mm = signal("qkv_mm", NT)
        z_ready = signal("z_ready", NT)
        sig_tanh = signal("sig_tanh", 1)
        qk_ready = signal("qk_ready", 1)
        sums_mm = signal("sums_mm", 2)
        sums2_taken = signal("sums2_taken", 1)
        inv_flow_ready = signal("inv_flow_ready", 1)
        weighted_q = signal("weighted_q", 1)
        weighted_k = signal("weighted_k", 1)
        bias_added = signal("bias_added", 1)
        qnT_mm = signal("qnT_mm", 2)
        qnT_ready = signal("qnT_ready", 2)
        conserved_ready = signal("conserved_ready", 1)
        flow_act = signal("flow_act", 2)
        v_ready = signal("v_ready", 1)
        kv_mm = signal("kv_mm", 1)
        kv_ready = signal("kv_ready", 1)
        heads_mm = signal("heads_mm", 2)
        heads_ready = signal("heads_ready", 2)
        headsT_mm = signal("headsT_mm", 2)
        headsT_ready = signal("headsT_ready", 2)
        proj_mm = signal("proj_mm", 2)
        proj_added = signal("proj_added", 2)

        loads = [
            (uq_T, "UQ_T"), (uk_T, "UK_T"), (uv_T, "UV_T"), (wo_heads, "W_O"), (b_uv, "b_UV"), (dq_T, "DQ_T"),
            (b_dq1, "b_DQ1"), (q_rope, "Q_rope"), (w_k[:, :], "W_K"), (b_k[:, :], "b_K"), (w_dkv[:, :], "W_DKV"),
            (w_gate_up[0][:, :, :, :], "gate_up0"), (w_down[0][:, :, :], "down0"),
            (w_router[0][:, :], "router0"), (w_qkv[:, :], "W_QKV"), (w_proj[:, :], "W_PROJ"),
            (w_gate_up[1][:, :, :, :], "gate_up1"), (w_down[1][:, :, :], "down1"),
            (w_router[1][:, :], "router1"), (b_gate[:, :], "b_gate"), (b_up[:, :], "b_up"), (b_down[:, :], "b_down"),
        ]
        rows = [(b_dkv, "b_DKV", DC), (b_o_in, "b_O", D), (b_qkv, "b_QKV", 3 * D), (b_proj, "b_PROJ", D),
                (b_router, "b_ROUTER", E)]
        ALL_WEIGHTS = 16 * (len(loads) + len(rows))

        block = ctx.enter_context(nc.Block())

        @block.sync
        def _(sp):
            for dst, name in loads:
                sp.dma_start(dst, ins[name]).then_inc(weights_in.sem, 16)
            for dst, name, n in rows:
                sp.dma_start(dst[:, 0:n], ins[name].partition_broadcast(P)).then_inc(weights_in.sem, 16)
            sp.dma_start(x_in[:, :, :], ins["x"][0, :, :].rearrange("(n p) d -> p n d", p=P)
                         ).then_inc(x_loaded.sem, 16)
            sp.sem_inc(y_stored.sem, 1)
            with sp.Fori(0, BATCH) as index:
                b = Sequence(sp, index)
                sp.wait_ge(x_taken.sem, x_taken.at(b, 1))
                sp.dma_start(x_in[:, :, :], ins["x"][bass.ds(sp.snap((index + 1) % BATCH), 1), :, :].rearrange("a (n p) d -> p (a n) d", p=P)
                             ).then_inc(x_loaded.sem, 16)
                for l in range(2):
                    sp.wait_ge(gateT_ready.sem, gateT_ready.at(b, l + 1))
                    for g in range(E // 4):
                        sp.dma_start(gate_rows[0:97:32, g, :], gate_wT[4 * g:4 * g + 4, :]).then_inc(rows_ready.sem, 16)
                sp.wait_ge(y_added.sem, y_added.at(b, 4))
                sp.dma_start(out[bass.ds(index, 1), :, :].rearrange("a (n p) d -> p (a n) d", p=P), x_mid[:, :, :]
                             ).then_inc(y_stored.sem, 16)
            sp.wait_ge(y_stored.sem, y_stored.per * BATCH + 1)

        @block.gpsimd
        def _(pool):
            nc.gpsimd.memset(minus_half[:, :], -0.5).then_inc(pool_consts.sem, 1)
            nc.gpsimd.memset(ident[:, :], 0.0).then_inc(pool_consts.sem, 1)
            nc.gpsimd.memset(ones_column[:, :], 1.0).then_inc(pool_consts.sem, 1)
            nc.gpsimd.memset(same_head[:, :, :], 1.0).then_inc(pool_consts.sem, 1)
            nc.gpsimd.memset(earlier[:, :, :], 1.0).then_inc(pool_consts.sem, 1)
            pool.wait_ge(pool_consts.sem, 5)
            nc.gpsimd.affine_select(out=ident[:, :], in_=ident[:, :], compare_op=ALU.not_equal, fill=1.0, base=0,
                                    pattern=[[-1, P]], channel_multiplier=1).then_inc(pool_consts.sem, 1)
            nc.gpsimd.affine_select(out=same_head[:, :, :], in_=same_head[:, :, :], compare_op=ALU.is_ge, fill=0.0,
                                    base=0, pattern=[[-D1, H1], [0, D1]], channel_multiplier=1
                                    ).then_inc(pool_consts.sem, 1)
            pool.wait_ge(pool_consts.sem, 7)
            nc.gpsimd.affine_select(out=same_head[:, :, :], in_=same_head[:, :, :], compare_op=ALU.is_ge, fill=0.0,
                                    base=D1 - 1, pattern=[[D1, H1], [0, D1]], channel_multiplier=-1
                                    ).then_inc(pool_consts.sem, 1)
            nc.gpsimd.affine_select(out=earlier[:, :, :], in_=earlier[:, :, :], compare_op=ALU.is_ge, fill=0.0,
                                    base=-1, pattern=[[1, E], [-1, E]], channel_multiplier=0
                                    ).then_inc(pool_consts.sem, 1)

            def inverse_deviation(b, k):
                pool.wait_ge(var_ready.sem, var_ready.at(b, k))
                nc.gpsimd.tensor_tensor(rstd[:, :], var_eps[:, :], minus_half[:, :], ALU.pow
                                        ).then_inc(rstd_ready.sem, 1)

            inverse_deviation(None, 1)
            with pool.Fori(0, BATCH) as index:
                b = Sequence(pool, index)
                steps = 0
                for l in range(2):
                    if l == 1:
                        inverse_deviation(b, 2)
                    for u in range(UNITS):
                        e, c = u // (FH * HALVES), u % HALVES
                        if u == 0 or (u % (FH * HALVES) == 2 and e + 1 < E):
                            to = 0 if u == 0 else e + 1
                            if u == 0:
                                pool.wait_ge(rows_ready.sem, rows_ready.at(b, 32 * (l + 1)))
                            else:
                                pool.wait_ge(h_ready.sem, h_ready.at(b, l * UNITS + u))
                            pool.sem_inc(pool_carrier.sem, 1)
                            nc.gpsimd.partition_broadcast(
                                gate_bc[:, to % 2, :], gate_rows[32 * (to % 4):32 * (to % 4) + 1, to // 4, :]
                            ).then_inc(pool_step.sem, 1)
                            steps += 1
                            pool.wait_ge(pool_step.sem, pool_step.at(b, steps))
                        if l == 1 and u % 2 == 1:
                            if u >= 3:
                                pool.wait_ge(h_ready.sem, h_ready.at(b, UNITS + u - 1))
                            pool.wait_ge(g_free.sem, g_free.at(b, UNITS + u + 1))
                            nc.gpsimd.tensor_tensor(ffn_gu[:, 1, :], ffn_g[u % 4], ffn_u[u % 4], ALU.mult
                                                    ).then_inc(pool_step.sem, 1)
                            steps += 1
                            pool.wait_ge(pool_step.sem, pool_step.at(b, steps))
                        else:
                            pool.wait_ge(gu_done.sem, gu_done.at(b, u + 1 if l == 0 else UNITS + u // 2 + 1))
                        if u >= 5:
                            pool.wait_ge(down_done.sem, down_done.at(b, l * UNITS + u - 4))
                        nc.gpsimd.tensor_tensor(ffn_h[u % 5], ffn_gu[:, u % 2, :],
                                                gate_bc[:, e % 2, c * BANK:(c + 1) * BANK], ALU.mult
                                                ).then_inc(h_ready.sem, 1)
                        if l == 0 and u == NORM_VAR + 1:
                            inverse_deviation(b, 1)
                        if l == 1 and u == FLOW_WEIGHTS[4]:
                            pool.wait_ge(inv_flow_ready.sem, inv_flow_ready.at(b, 1))
                            nc.gpsimd.tensor_tensor(heads(weighted[:, :, D:2 * D]), heads(flow_k),
                                                    per_head(inv_flow[:, 1, :]), ALU.mult).then_inc(weighted_k.sem, 1)
                        if l == 1 and u == FLOW_BIAS:
                            pool.wait_ge(norm_ready.sem, norm_ready.at(b, 2 * NT))
                            nc.gpsimd.tensor_tensor(x_mid[:, :, :], x_mid[:, :, :],
                                                    b_proj[:, :].unsqueeze(1).to_broadcast([P, NT, D]), ALU.add
                                                    ).then_inc(bias_added.sem, 1)
                        if l == 1 and u == FLOW_VALUES:
                            pool.wait_ge(flow_act.sem, flow_act.at(b, 2))
                            nc.gpsimd.tensor_tensor(heads(v_comp), heads(flow_v), per_head(source_exp), ALU.mult
                                                    ).then_inc(v_ready.sem, 1)
                assert steps == POOL_STEPS, steps

        @block.scalar
        def _(act):
            act.wait_ge(weights_in.sem, ALL_WEIGHTS)
            for l in range(2):
                nc.scalar.mul(w_down[l][:, :, :], w_down[l][:, :, :], 0.5).then_inc(prep_act.sem, 1)

            def copy_xT(b, l, before, bank):
                for c in range(2):
                    act.wait_ge(normT_ready.sem, normT_ready.at(b, before + c + 1))
                    nc.scalar.copy(xT[l][:, c * BANK:(c + 1) * BANK], ps[:, bank + c, :]).then_inc(xT_ready.sem, 1)

            def router_exp(b, k):
                act.wait_ge(shift_ready.sem, shift_ready.at(b, k + 1))
                src = r_c if k == 1 else r_a
                nc.scalar.activation(r_exp[:, k % 2, :, :], src[:, :, :], ACT.Exp).then_inc(r_exp_done.sem, 1)

            def copy_gatesT(b, l):
                act.wait_ge(gateT_mm.sem, gateT_mm.at(b, l + 1))
                nc.scalar.copy(gate_wT[:, :], banks(4)[0:E, :]).then_inc(gateT_ready.sem, 1)

            def experts_out(b, l):
                for c in range(HALVES):
                    act.wait_ge(down_done.sem, down_done.at(b, (l + 1) * UNITS))
                    nc.scalar.copy(y_T[:, c * BANK:(c + 1) * BANK], ps[:, 4 + c, :]).then_inc(yT_ready.sem, 1)

            def make_keys_high(b):
                act.wait_ge(k_proj.sem, k_proj.at(b, 1))
                nc.scalar.activation(probs[KD:P, 1, :].bitcast(F32R), banks(6)[KD:P, :], ACT.Identity,
                                     bias=b_k[KD:P, :])
                nc.scalar.activation(keys[0:KD, :], banks(6)[0:KD, :], ACT.Identity, bias=b_k[0:KD, :]
                                     ).then_inc(keys_high.sem, 1)

            copy_xT(None, 0, 0, 6)
            make_keys_high(None)
            with act.Fori(0, BATCH) as index:
                b = Sequence(act, index)

                def query_high(h):
                    act.wait_ge(q_proj.sem, q_proj.at(b, h + 1))
                    nc.scalar.activation(q_parts[:, h % QUAD, 0, :], banks(2 * (h % 2)), ACT.Identity,
                                         bias=b_q[:, h:h + 1]).then_inc(q_high.sem, 1)

                def split_high(l):
                    if l == 0:
                        act.wait_ge(scores_ready.sem, scores_ready.at(b, TILES - 2))
                    else:
                        act.wait_ge(xT_ready.sem, xT_ready.at(b, 2))
                    nc.scalar.copy(x_high, xT[l][:, :]).then_inc(x_high_ready.sem, 1)

                def split_weights_high(l, f):
                    if l == 1 or f >= 4:
                        act.wait_ge(gu_ready.sem, gu_ready.at(b, l * UNITS + (f - 3) * HALVES))
                    nc.scalar.copy(w_split[:, f % 4, 0, :], w_gate_up[l][:, f, :, :].rearrange("p a b -> p (a b)")
                                   ).then_inc(w_high_ready.sem, 1)

                def attention_step(w):
                    t = use_of(w - T_LAG)[1]
                    if t is not None:
                        act.wait_ge(pT_low.sem, pT_low.at(b, t + 1))
                        if t >= 2 * QUAD:
                            act.wait_ge(u_ready.sem, u_ready.at(b, t // QUAD - 1))
                        nc.scalar.copy(probsT[:, t % (2 * QUAD), 0:BANK], ps[:, 4, :]).then_inc(low_copied.sem, 1)
                    h, t = use_of(w)
                    if h is not None:
                        query_high(h)
                    if t is not None:
                        act.wait_ge(max_ready.sem, max_ready.at(b, t + 1))
                        if t >= 3:
                            act.wait_ge(pT_high.sem, pT_high.at(b, t - 2))
                        g = t // QUAD
                        if g >= 2 and t % QUAD == 0:
                            act.wait_ge(inv_ready.sem, inv_ready.at(b, g - 1))
                        nc.scalar.activation(probs[:, t % 3, :], banks(2 * (t % 2)), ACT.Exp,
                                             bias=neg_max[:, t % 4:t % 4 + 1],
                                             accum_out=row_sum[:, g % 2, t % QUAD:t % QUAD + 1]
                                             ).then_inc(exp_done.sem, 1)
                    if w in ROUTER_EXP_STEPS:
                        router_exp(b, ROUTER_EXP_STEPS.index(w))
                    if w == GATES_STEP + 1:
                        copy_gatesT(b, 0)
                    g = group_at(w, SCALES_LAG)
                    if g is not None:
                        act.wait_ge(u_ready.sem, u_ready.at(b, g + 1))
                        if g >= 2:
                            act.wait_ge(u_scaled.sem, u_scaled.at(b, g - 1))
                        nc.scalar.copy(scale_sb[:, g % 2, :], ps[:, 6 + g % 2, P:2 * P]).then_inc(scale_ready.sem, 1)

                for w in range(UNIT_STEP):
                    attention_step(w)
                    if w == STEPS - 1:
                        split_high(0)
                        split_weights_high(0, 0)
                    if w == STEPS:
                        split_weights_high(0, 1)

                for u in range(UNITS):
                    if u % HALVES == 0 and u // HALVES + 2 < E * FH:
                        split_weights_high(0, u // HALVES + 2)
                    act.wait_ge(gu_ready.sem, gu_ready.at(b, u + 1))
                    if u >= 2:
                        act.wait_ge(g_free.sem, g_free.at(b, u - 1))
                    nc.scalar.activation(ffn_t[:, u % 2, :], ps[:, u % 2, :], ACT.Tanh, scale=0.5
                                         ).then_inc(tanh_done.sem, 1)
                    attention_step(UNIT_STEP + u)
                    if u in (UNITS - 3, UNITS - 1):
                        split_weights_high(1, (u - UNITS + 3) // 2)
                experts_out(b, 0)

                copy_xT(b, 1, 0, 4)
                split_high(1)
                split_weights_high(1, 2)
                router_exp(b, 2)
                def copies(u):
                    if u >= 4 and u % 2 == 0:
                        act.wait_ge(gu_done.sem, gu_done.at(b, UNITS + (u - 4) // 2 + 1))
                    elif u >= 4:
                        act.wait_ge(h_ready.sem, h_ready.at(b, UNITS + u - 3))
                    act.wait_ge(gu_ready.sem, gu_ready.at(b, UNITS + u + 1))
                    f = u // HALVES
                    nc.scalar.activation(ffn_g[u % 4], ps[:, u % 2, :], ACT.Identity,
                                         bias=b_gate[:, f:f + 1]).then_inc(gate_copied.sem, 1)
                    nc.scalar.activation(ffn_u[u % 4], ps[:, 2 + u % 2, :], ACT.Identity,
                                         bias=b_up[:, f:f + 1]).then_inc(up_copied.sem, 1)

                for u in range(EARLY_UNITS):
                    copies(u)
                copy_gatesT(b, 1)
                act.wait_ge(z_ready.sem, z_ready.at(b, NT))
                nc.scalar.activation(qkv[:, :, 0:2 * D], qkv[:, :, 0:2 * D], ACT.Tanh, scale=0.5
                                     ).then_inc(sig_tanh.sem, 1)
                for u in range(UNITS):
                    if u % HALVES == 0 and u // HALVES + 3 < E * FH:
                        split_weights_high(1, u // HALVES + 3)
                    if u >= EARLY_UNITS:
                        copies(u)
                    act.wait_ge(gate_lim.sem, gate_lim.at(b, u + 1))
                    if u >= 2:
                        act.wait_ge(g_free.sem, g_free.at(b, UNITS + u - 1))
                    nc.scalar.activation(ffn_t[:, u % 2, :], ffn_g[u % 4], ACT.Tanh, scale=0.5 * ALPHA
                                         ).then_inc(tanh_done.sem, 1)
                    if u in (FLOW_SUMS2, FLOW_SUMS2 + 1):
                        c = u - FLOW_SUMS2
                        act.wait_ge(qnT_mm.sem, qnT_mm.at(b, c + 1))
                        nc.scalar.copy(q_normT[:, c * BANK:(c + 1) * BANK], ps[:, 6, :]).then_inc(qnT_ready.sem, 1)
                    if u == FLOW_ALLOC:
                        act.wait_ge(conserved_ready.sem, conserved_ready.at(b, 1))
                        nc.scalar.activation(sink_alloc, conserved[:, 0, :], ACT.Tanh, scale=0.5
                                             ).then_inc(flow_act.sem, 1)
                        nc.scalar.activation(source_exp, conserved[:, 1, :], ACT.Exp).then_inc(flow_act.sem, 1)
                    if u == FLOW_HEADS - 1:
                        for c in range(2):
                            act.wait_ge(headsT_mm.sem, headsT_mm.at(b, c + 1))
                            nc.scalar.copy(heads_outT[:, c * BANK:(c + 1) * BANK], ps[:, 6 + c, :]
                                           ).then_inc(headsT_ready.sem, 1)
                    if u == NEXT_TRANSPOSE + 1:
                        copy_xT(b, 0, 2, 6)
                experts_out(b, 1)
                make_keys_high(b)

        @block.vector
        def _(dve):
            dve.wait_ge(weights_in.sem, ALL_WEIGHTS)
            dve.wait_ge(prep_mm.sem, 1)
            for h in range(H0):
                for half in range(2):
                    nc.vector.tensor_scalar(absorbed[:, h, half * KD:half * KD + DC],
                                            ps[0:DC + 1, 0, h * DC:(h + 1) * DC], SCALE, None, ALU.mult)
                    last = nc.vector.tensor_scalar(absorbed[:, h, half * KD + DC:(half + 1) * KD], q_rope[:, h, :],
                                                   SCALE, None, ALU.mult)
                last.then_inc(prep_sb.sem, 1)
            dve.wait_ge(prep_mm.sem, 2)
            nc.vector.tensor_copy(w_q[:, :, :].rearrange("p a b -> p (a b)"), banks(2)).then_inc(prep_sb.sem, 1)
            nc.vector.tensor_copy(b_q[:, :], ps[:, 1, 0:H0]).then_inc(prep_sb.sem, 1)
            nc.vector.tensor_copy(w_o[:, :, :].rearrange("p a b -> p (a b)"), ps[:, 4, 0:QUADS * D]
                                  ).then_inc(prep_sb.sem, 1)
            nc.vector.tensor_tensor(b_o[:, :], ps[:, 5, 0:D], b_o_in, ALU.add).then_inc(prep_sb.sem, 1)
            nc.vector.tensor_scalar(b_up[:, :], b_up[:, :], 1.0, None, ALU.add).then_inc(prep_sb.sem, 1)
            dve.wait_ge(prep_sb.sem, H0 + 5)

            b, count = None, [0]

            def link(ins, aggregates_next=False):
                count[0] += 1
                ins.then_inc(dve_step.sem, 1)
                dve.wait_ge(dve_step.sem, dve_step.at(b, count[0]))
                if aggregates_next:
                    nc.vector.memset(spare[:, 0:1], 0.0)

            def norm_stats(x, tiles):
                for n in tiles:
                    last = nc.vector.bn_stats(stats[:, n, :], x[:, n, :])
                return last

            def norm_variance():
                for n in range(NT):
                    last = nc.vector.bn_aggr(mean_var[:, n, :], stats[:, n, :])
                link(last)
                nc.vector.tensor_scalar(var_eps[:, :], mean_var[:, :, 1], LN_EPS, None, ALU.add
                                        ).then_inc(var_ready.sem, 1)

            def norm_apply(l, x, tiles):
                for n in tiles:
                    nc.vector.tensor_scalar(x_norm[l][:, n, :], x[:, n, :], mean_var[:, n, 0:1], rstd[:, n:n + 1],
                                            ALU.subtract, ALU.mult).then_inc(norm_ready.sem, 1)

            def make_keys():
                dve.wait_ge(keys_high.sem, keys_high.at(b, 1))
                nc.vector.scalar_tensor_tensor(keys[KD:P, :], banks(6)[KD:P, :], b_k[KD:P, :], probs[KD:P, 1, :],
                                               ALU.add, ALU.subtract).then_inc(keys_ready.sem, 1)

            nc.vector.memset(spare[:, 1:2], 0.0).then_inc(y_added.sem, 1)
            dve.wait_ge(x_loaded.sem, 16)
            link(norm_stats(x_in, range(NT)), aggregates_next=True)
            norm_variance()
            dve.wait_ge(rstd_ready.sem, 1)
            norm_apply(0, x_in, range(NT))
            make_keys()
            assert count[0] == DVE_STEPS_BEFORE, count[0]

            with dve.Fori(0, BATCH) as index:
                b, count[0] = Sequence(dve, index), 0

                def wide(v):
                    return v.unsqueeze(2).to_broadcast([P, NT, E])

                def ranks():
                    by_j = logits[:, :, :].unsqueeze(2).to_broadcast([P, NT, E, E])
                    by_e = logits[:, :, :].unsqueeze(3).to_broadcast([P, NT, E, E])
                    nc.vector.tensor_tensor(pair_a, by_j, by_e, ALU.is_gt)
                    link(nc.vector.tensor_tensor(pair_b, by_j, by_e, ALU.is_equal))
                    yield
                    link(nc.vector.tensor_tensor(pair_b, pair_b,
                                                 earlier[:, :, :].unsqueeze(1).to_broadcast([P, NT, E, E]), ALU.mult))
                    yield
                    link(nc.vector.tensor_tensor(pair_a, pair_a, pair_b, ALU.add))
                    yield
                    link(nc.vector.tensor_reduce(rank[:, :, :], pair_a, X, ALU.add))
                    yield

                def route_two():
                    dve.wait_ge(logits_mm.sem, logits_mm.at(b, 1))
                    link(nc.vector.tensor_copy(logits[:, :, :].rearrange("p n e -> p (n e)"),
                                               ps[:, 5, NT * DC:NT * (DC + E)]))
                    yield
                    link(nc.vector.tensor_reduce(top1[:, :], logits[:, :, :], X, ALU.max))
                    yield
                    nc.vector.tensor_tensor(r_a[:, :, :], logits[:, :, :], wide(top1[:, :]), ALU.subtract
                                            ).then_inc(shift_ready.sem, 1)
                    yield
                    yield from ranks()
                    link(nc.vector.tensor_scalar(r_b[:, :, :], rank[:, :, :], 0.0, MINUS_INF, ALU.is_equal, ALU.mult))
                    yield
                    link(nc.vector.tensor_tensor(r_b[:, :, :], r_b[:, :, :], logits[:, :, :], ALU.add))
                    yield
                    link(nc.vector.tensor_reduce(top2[:, :], r_b[:, :, :], X, ALU.max))
                    yield
                    nc.vector.tensor_tensor(r_c[:, :, :], r_b[:, :, :], wide(top2[:, :]), ALU.subtract
                                            ).then_inc(shift_ready.sem, 1)
                    yield
                    link(nc.vector.scalar_tensor_tensor(r_d[:, :, :], logits[:, :, :], -1.0, logits[:, :, :],
                                                        ALU.mult, ALU.max))
                    yield
                    for k, (top, total) in enumerate(((top1, r_s1), (top2, r_s2))):
                        link(nc.vector.tensor_tensor(r_e[:, :, :], r_d[:, :, :], wide(top[:, :]), ALU.max))
                        yield
                        link(nc.vector.tensor_tensor(gate_w[:, :, :], logits[:, :, :], wide(top[:, :]), ALU.subtract))
                        yield
                        link(nc.vector.scalar_tensor_tensor(r_e[:, :, :], r_e[:, :, :], JITTER2, gate_w[:, :, :],
                                                            ALU.mult, ALU.add))
                        yield
                        dve.wait_ge(r_exp_done.sem, r_exp_done.at(b, k + 1))
                        link(nc.vector.scalar_tensor_tensor(r_e[:, :, :], r_e[:, :, :], 0.0, r_exp[:, k, :, :],
                                                            ALU.is_ge, ALU.mult))
                        yield
                        link(nc.vector.tensor_reduce(total[:, :], r_e[:, :, :], X, ALU.add))
                        yield
                        link(nc.vector.reciprocal(total[:, :], total[:, :]))
                        yield
                    link(nc.vector.scalar_tensor_tensor(r_e[:, :, :], rank[:, :, :], 0.0, wide(r_s1[:, :]),
                                                        ALU.is_equal, ALU.mult))
                    yield
                    link(nc.vector.scalar_tensor_tensor(r_d[:, :, :], rank[:, :, :], 1.0, wide(r_s2[:, :]),
                                                        ALU.is_equal, ALU.mult))
                    yield
                    nc.vector.tensor_tensor(gate_w[:, :, :], r_e[:, :, :], r_d[:, :, :], ALU.add
                                            ).then_inc(gate_ready.sem, 1)
                    yield

                def route_four():
                    dve.wait_ge(logits_mm.sem, logits_mm.at(b, 2))
                    link(nc.vector.tensor_tensor(
                        logits[:, :, :], ps[:, 4, 0:NT * E].rearrange("p (n e) -> p n e", e=E),
                        b_router[:, :].unsqueeze(1).to_broadcast([P, NT, E]), ALU.add))
                    yield
                    link(nc.vector.tensor_reduce(top1[:, :], logits[:, :, :], X, ALU.max))
                    nc.vector.tensor_tensor(r_a[:, :, :], logits[:, :, :], wide(top1[:, :]), ALU.subtract
                                            ).then_inc(shift_ready.sem, 1)
                    yield
                    yield from ranks()
                    dve.wait_ge(r_exp_done.sem, r_exp_done.at(b, 3))
                    link(nc.vector.scalar_tensor_tensor(r_e[:, :, :], rank[:, :, :], TOP_K - 0.5, r_exp[:, 0, :, :],
                                                        ALU.is_lt, ALU.mult))
                    yield
                    link(nc.vector.tensor_reduce(r_s1[:, :], r_e[:, :, :], X, ALU.add))
                    link(nc.vector.reciprocal(r_s1[:, :], r_s1[:, :]))
                    nc.vector.tensor_tensor(gate_w[:, :, :], r_e[:, :, :], wide(r_s1[:, :]), ALU.mult
                                            ).then_inc(gate_ready.sem, 1)
                    yield

                def experts_add(l):
                    for c in range(2):
                        dve.wait_ge(y_mm.sem, y_mm.at(b, 2 * l + c + 1))
                        nc.vector.tensor_tensor(
                            x_mid[:, 4 * c:4 * c + 4, :], x_mid[:, 4 * c:4 * c + 4, :],
                            ps[:, c, :].rearrange("p (n d) -> p n d", d=D), ALU.add).then_inc(y_added.sem, 1)

                route = route_two()

                def split_low(l):
                    dve.wait_ge(x_high_ready.sem, x_high_ready.at(b, l + 1))
                    nc.vector.tensor_tensor(x_low, xT[l][:, :], x_high.bitcast(F32), ALU.subtract
                                            ).then_inc(x_low_ready.sem, 1)

                def split_weights_low(l, f):
                    dve.wait_ge(w_high_ready.sem, w_high_ready.at(b, l * E * FH + f + 1))
                    nc.vector.tensor_tensor(w_split[:, f % 4, 1, :],
                                            w_gate_up[l][:, f, :, :].rearrange("p a b -> p (a b)"),
                                            w_split[:, f % 4, 0, :].bitcast(F32), ALU.subtract
                                            ).then_inc(w_low_ready.sem, 1)

                def attention_step(w):
                    h, t = use_of(w)
                    if h is not None:
                        dve.wait_ge(q_high.sem, q_high.at(b, h + 1))
                        nc.vector.scalar_tensor_tensor(
                            q_parts[:, h % QUAD, 1, :], banks(2 * (h % 2)), b_q[:, h:h + 1],
                            q_parts[:, h % QUAD, 0, :].bitcast(F32), ALU.add, ALU.subtract).then_inc(q_ready.sem, 1)
                    if t is not None:
                        dve.wait_ge(scores_ready.sem, scores_ready.at(b, t + 1))
                        if t >= 4:
                            dve.wait_ge(exp_done.sem, exp_done.at(b, t - 3))
                        nc.vector.tensor_reduce(neg_max[:, t % 4:t % 4 + 1], banks(2 * (t % 2)), X, ALU.max,
                                                negate=True).then_inc(max_ready.sem, 1)
                    if ROUTER_STEP <= w < GATES_STEP:
                        next(route, None)
                    t = use_of(w - T_LAG)[1]
                    if t is not None:
                        dve.wait_ge(pT_high.sem, pT_high.at(b, t + 1))
                        if t >= 2 * QUAD:
                            dve.wait_ge(u_ready.sem, u_ready.at(b, t // QUAD - 1))
                        nc.vector.tensor_copy(probsT[:, t % (2 * QUAD), BANK:SEQ], ps[:, 5, :]
                                              ).then_inc(high_copied.sem, 1)
                    g = group_at(w, INV_LAG)
                    if g is not None:
                        dve.wait_ge(exp_done.sem, exp_done.at(b, (g + 1) * QUAD))
                        if g >= 2:
                            dve.wait_ge(u_ready.sem, u_ready.at(b, g - 1))
                        nc.vector.reciprocal(inv_sum[:, g % 2, :], row_sum[:, g % 2, :]).then_inc(inv_ready.sem, 1)
                    g = group_at(w, SCALED_LAG)
                    if g is not None:
                        dve.wait_ge(scale_ready.sem, scale_ready.at(b, g + 1))
                        if g >= 2:
                            dve.wait_ge(o_ready.sem, o_ready.at(b, g - 1))
                        nc.vector.tensor_tensor(o_latent[:, g % 2, :], ps[:, 6 + g % 2, 0:P],
                                                scale_sb[:, g % 2, :], ALU.mult).then_inc(u_scaled.sem, 1)
                    g = group_at(w, ADDED_LAG)
                    if g is not None:
                        n = g % NT
                        dve.wait_ge(o_ready.sem, o_ready.at(b, g + 1))
                        if g >= NT:
                            dve.wait_ge(o_added.sem, o_added.at(b, g - NT + 1))
                        nc.vector.tensor_tensor(x_mid[:, n, :], x_mid[:, n, :],
                                                ps[:, 6 + g % 2, 2 * P:3 * P], ALU.add
                                                ).then_inc(o_added.sem, 1)

                for w in range(UNIT_STEP):
                    attention_step(w)
                    if w == STEPS:
                        split_low(0)
                    if w == STEPS + 1:
                        split_weights_low(0, 0)
                        split_weights_low(0, 1)
                    if w == 0:
                        dve.wait_ge(latent_mm.sem, latent_mm.at(b, 1))
                        next(route)
                        nc.vector.tensor_tensor(latent[:, :, :],
                                                ps[:, 5, 0:NT * DC].rearrange("p (n c) -> p n c", c=DC),
                                                b_dkv[:, :].unsqueeze(1).to_broadcast([P, NT, DC]), ALU.add
                                                ).then_inc(latent_ready.sem, 1)
                    if w == 10:
                        dve.wait_ge(y_stored.sem, y_stored.at(b, 0))
                        nc.vector.tensor_tensor(x_mid[:, :, :], x_in[:, :, :],
                                                b_o[:, :].unsqueeze(1).to_broadcast([P, NT, D]), ALU.add
                                                ).then_inc(x_taken.sem, 1)
                        dve.wait_ge(x_taken.sem, x_taken.at(b, 1))
                    if w == GATES_STEP:
                        assert next(route, "end") == "end"

                for u in range(UNITS):
                    if u % HALVES == 1 and u // HALVES + 2 < E * FH:
                        split_weights_low(0, u // HALVES + 2)
                    dve.wait_ge(tanh_done.sem, tanh_done.at(b, u + 1))
                    nc.vector.scalar_tensor_tensor(ffn_g[u % 3], ffn_t[:, u % 2, :], 1.0, ps[:, u % 2, :],
                                                   ALU.add, ALU.mult).then_inc(g_free.sem, 1)
                    dve.wait_ge(g_free.sem, g_free.at(b, u + 1))
                    if u >= 2:
                        dve.wait_ge(h_ready.sem, h_ready.at(b, u - 1))
                    nc.vector.tensor_tensor(ffn_gu[:, u % 2, :], ffn_g[u % 3], ps[:, 2 + u % 2, :], ALU.mult
                                            ).then_inc(gu_done.sem, 1)
                    attention_step(UNIT_STEP + u)
                    if NORM_STATS <= u < NORM_STATS + NT // 2:
                        k = u - NORM_STATS
                        if k == 0:
                            dve.wait_ge(x_loaded.sem, x_loaded.at(b, 16))
                        last = norm_stats(x_in, (2 * k, 2 * k + 1))
                        if k == NT // 2 - 1:
                            link(last, aggregates_next=True)
                    if u == NORM_VAR:
                        norm_variance()
                    if NORM_APPLY <= u < NORM_APPLY + NT // 2:
                        k = u - NORM_APPLY
                        if k == 0:
                            dve.wait_ge(rstd_ready.sem, rstd_ready.at(b, 1))
                        norm_apply(0, x_in, (2 * k, 2 * k + 1))
                split_weights_low(1, 0)
                split_weights_low(1, 1)
                dve.wait_ge(o_added.sem, o_added.at(b, GROUPS))
                experts_add(0)
                for c in range(2):
                    dve.wait_ge(y_added.sem, y_added.at(b, c + 1))
                    last = norm_stats(x_mid, range(4 * c, 4 * c + 4))
                link(last, aggregates_next=True)
                norm_variance()
                dve.wait_ge(rstd_ready.sem, rstd_ready.at(b, 2))
                norm_apply(1, x_mid, range(NT))
                route = route_four()
                for n in range(NT):
                    next(route, None)
                    if n == 1:
                        split_low(1)
                    dve.wait_ge(qkv_mm.sem, qkv_mm.at(b, n + 1))
                    nc.vector.tensor_tensor(qkv[:, n, :], ps[:, 6 + n % 2, 0:3 * D], b_qkv[:, :], ALU.add
                                            ).then_inc(z_ready.sem, 1)
                assert next(route, "end") == "end"
                split_weights_low(1, 2)

                def flow_products(x, total):
                    link(nc.vector.scalar_tensor_tensor(tmp, x, EPS1, total.unsqueeze(1).to_broadcast([P, NT, D]),
                                                        ALU.add, ALU.mult))

                def flow_sums(dst):
                    link(nc.vector.tensor_reduce(dst, tmp.rearrange("p n (h d) -> p (n h) d", d=D1), X, ALU.add))

                def flow_step(u):
                    if u == FLOW_SIGMOID:
                        dve.wait_ge(sig_tanh.sem, sig_tanh.at(b, 1))
                        nc.vector.tensor_scalar(qkv[:, :, 0:2 * D], qkv[:, :, 0:2 * D], 0.5, 0.5, ALU.mult, ALU.add
                                                ).then_inc(qk_ready.sem, 1)
                    if u == FLOW_WEIGHTS[0]:
                        dve.wait_ge(sums_mm.sem, sums_mm.at(b, 1))
                        link(nc.vector.tensor_scalar(sums_eps, ps[:, 6, 0:2 * D], EPS1, None, ALU.add))
                        flow_products(flow_q, sums_eps[:, D:2 * D])
                    if u == FLOW_WEIGHTS[1]:
                        flow_sums(inv_flow[:, 0, :])
                    if u == FLOW_WEIGHTS[2]:
                        flow_products(flow_k, sums_eps[:, 0:D])
                    if u == FLOW_WEIGHTS[3]:
                        flow_sums(inv_flow[:, 1, :])
                    if u == FLOW_WEIGHTS[4]:
                        nc.vector.reciprocal(inv_flow[:, :, :], inv_flow[:, :, :]).then_inc(inv_flow_ready.sem, 1)
                        dve.wait_ge(inv_flow_ready.sem, inv_flow_ready.at(b, 1))
                    if u == FLOW_WEIGHTS[5]:
                        nc.vector.tensor_tensor(heads(weighted[:, :, 0:D]), heads(flow_q), per_head(inv_flow[:, 0, :]),
                                                ALU.mult).then_inc(weighted_q.sem, 1)
                    if u == FLOW_CONSERVED[0]:
                        dve.wait_ge(sums_mm.sem, sums_mm.at(b, 2))
                        nc.vector.tensor_scalar(sums_eps, ps[:, 7, 0:2 * D], EPS1, None, ALU.add
                                                ).then_inc(sums2_taken.sem, 1)
                        dve.wait_ge(sums2_taken.sem, sums2_taken.at(b, 1))
                        flow_products(flow_q, sums_eps[:, D:2 * D])
                    if u == FLOW_CONSERVED[1]:
                        flow_sums(conserved[:, 0, :])
                    if u == FLOW_CONSERVED[2]:
                        flow_products(flow_k, sums_eps[:, 0:D])
                    if u == FLOW_CONSERVED[3]:
                        flow_sums(conserved[:, 1, :])
                        link(nc.vector.tensor_scalar(conserved[:, :, :], conserved[:, :, :], EPS1, None, ALU.add))
                        nc.vector.tensor_scalar(conserved[:, 1, :], conserved[:, 1, :], 1.0, -1.0, ALU.min, ALU.max
                                                ).then_inc(conserved_ready.sem, 1)
                    if u == FLOW_VALUES:
                        dve.wait_ge(flow_act.sem, flow_act.at(b, 1))
                        link(nc.vector.tensor_scalar(sink_alloc, sink_alloc, 0.5, 0.5, ALU.mult, ALU.add))
                    if u == FLOW_KV - 1:
                        dve.wait_ge(kv_mm.sem, kv_mm.at(b, 1))
                        link(nc.vector.tensor_reduce(
                            source_inv[:, :], ps[:, 7, 0:NT * H1].rearrange("p (n h) -> p h n", n=NT), X, ALU.add))
                        nc.vector.reciprocal(source_inv[:, :], source_inv[:, :])
                        link(nc.vector.scalar_tensor_tensor(kv, ps[:, 6, 0:D], float(SEQ),
                                                            same_head[:, :, :].rearrange("p h d -> p (h d)"),
                                                            ALU.mult, ALU.mult))
                        nc.vector.tensor_tensor(kv.rearrange("p (h d) -> p h d", d=D1),
                                                kv.rearrange("p (h d) -> p h d", d=D1),
                                                source_inv[:, :].unsqueeze(2).to_broadcast([P, H1, D1]), ALU.mult
                                                ).then_inc(kv_ready.sem, 1)
                    if u == FLOW_OUT - 1:
                        for c in range(2):
                            dve.wait_ge(heads_mm.sem, heads_mm.at(b, c + 1))
                            half = slice(4 * c, 4 * c + 4)
                            nc.vector.tensor_tensor(heads(heads_out[:, half, :]),
                                                    ps[:, 6 + c, :].rearrange("p (n h d) -> p n h d", n=4, d=D1),
                                                    per_head(sink_alloc)[:, half, :, :], ALU.mult
                                                    ).then_inc(heads_ready.sem, 1)
                    if u == FLOW_PROJ - 1:
                        dve.wait_ge(bias_added.sem, bias_added.at(b, 1))
                        for c in range(2):
                            dve.wait_ge(proj_mm.sem, proj_mm.at(b, c + 1))
                            nc.vector.tensor_tensor(
                                x_mid[:, 4 * c:4 * c + 4, :], x_mid[:, 4 * c:4 * c + 4, :],
                                ps[:, 6 + c, :].rearrange("p (n d) -> p n d", d=D), ALU.add
                            ).then_inc(proj_added.sem, 1)

                for u in range(UNITS):
                    f = u // HALVES
                    if u % HALVES == 1 and f + 3 < E * FH:
                        split_weights_low(1, f + 3)
                    dve.wait_ge(gate_copied.sem, gate_copied.at(b, u + 1))
                    nc.vector.tensor_scalar(ffn_g[u % 4], ffn_g[u % 4], LIMIT, None, ALU.min
                                            ).then_inc(gate_lim.sem, 1)
                    dve.wait_ge(up_copied.sem, up_copied.at(b, u + 1))
                    nc.vector.tensor_scalar(ffn_u[u % 4], ffn_u[u % 4], 1.0 + LIMIT, 1.0 - LIMIT,
                                            ALU.min, ALU.max)
                    dve.wait_ge(tanh_done.sem, tanh_done.at(b, UNITS + u + 1))
                    nc.vector.scalar_tensor_tensor(ffn_g[u % 4], ffn_t[:, u % 2, :], 1.0, ffn_g[u % 4],
                                                   ALU.add, ALU.mult).then_inc(g_free.sem, 1)
                    if u % 2 == 0:
                        dve.wait_ge(g_free.sem, g_free.at(b, UNITS + u + 1))
                        if u >= 2:
                            dve.wait_ge(h_ready.sem, h_ready.at(b, UNITS + u - 1))
                        nc.vector.tensor_tensor(ffn_gu[:, 0, :], ffn_g[u % 4], ffn_u[u % 4], ALU.mult
                                                ).then_inc(gu_done.sem, 1)
                    flow_step(u)
                dve.wait_ge(proj_added.sem, proj_added.at(b, 2))
                experts_add(1)
                make_keys()
                assert count[0] == DVE_STEPS, count[0]

        @block.tensor
        def _(pe):
            pe.wait_ge(weights_in.sem, ALL_WEIGHTS)
            pe.wait_ge(pool_consts.sem, 9)
            for h in range(H0):
                mm = nc.tensor.matmul(ps[0:DC + 1, 0, h * DC:(h + 1) * DC], uq_T[:, h, :], uk_T[:, h, :],
                                      start=True, stop=True)
            mm.then_inc(prep_mm.sem, 1)
            for h in range(H0):
                nc.tensor.matmul(ps[DC * (h % QUAD):DC * (h % QUAD + 1), 4, (h // QUAD) * D:(h // QUAD + 1) * D],
                                 uv_T[:, h, :], wo_heads[:, h, :], start=True, stop=True)
            for h in range(H0):
                nc.tensor.matmul(ps[:, 5, 0:D], b_uv[:, h:h + 1].to_broadcast([P, P]), wo_heads[:, h, :],
                                 start=(h == 0), stop=(h == H0 - 1))
            pe.wait_ge(prep_sb.sem, H0)
            for h in range(H0):
                nc.tensor.matmul(ps[:, 1, h:h + 1], absorbed[:, h, :], b_dq1, start=True, stop=True)
            for c in range(2):
                last = nc.tensor.matmul(ps[:, 2 + c, :], dq_T,
                                        absorbed[0:DC, 4 * c:4 * c + 4, :].rearrange("p a b -> p (a b)"),
                                        start=True, stop=True)
            last.then_inc(prep_mm.sem, 1)
            pe.wait_ge(prep_sb.sem, H0 + 5)
            pe.wait_ge(prep_act.sem, 2)

            def transpose_norm(b, l, bank):
                for n in range(NT):
                    pe.wait_ge(norm_ready.sem, norm_ready.at(b, l * NT + n + 1))
                    mm = nc.tensor.transpose(ps[:, bank + n // 4, (n % 4) * P:(n % 4 + 1) * P], x_norm[l][:, n, :],
                                             ident[:, :])
                    if n % 4 == 3:
                        mm.then_inc(normT_ready.sem, 1)

            def key_projection(b, before):
                pe.wait_ge(xT_ready.sem, xT_ready.at(b, before + 2))
                for c in range(HALVES):
                    mm = nc.tensor.matmul(ps[:, 6 + c, :], w_k[:, :], xT[0][:, c * BANK:(c + 1) * BANK],
                                          start=True, stop=True)
                mm.then_inc(k_proj.sem, 1)

            def router(b, l, bank, column):
                for n in range(NT):
                    mm = nc.tensor.matmul(ps[:, bank, column + n * E:column + (n + 1) * E],
                                          xT[l][:, n * P:(n + 1) * P], w_router[l][:, :], start=True, stop=True)
                mm.then_inc(logits_mm.sem, 1)

            def gates_transpose(b, l):
                pe.wait_ge(gate_ready.sem, gate_ready.at(b, l + 1))
                for n in range(NT):
                    mm = nc.tensor.transpose(ps[0:E, 4 + n // 4, (n % 4) * P:(n % 4 + 1) * P], gate_w[:, n, :],
                                             ident[:, :])
                mm.then_inc(gateT_mm.sem, 1)

            def experts(b, l, beside):
                def gate_up(u):
                    f, c = u // HALVES, u % HALVES
                    if u >= 2:
                        if l == 0:
                            pe.wait_ge(gu_done.sem, gu_done.at(b, u - 1))
                        else:
                            pe.wait_ge(gate_copied.sem, gate_copied.at(b, u - 1))
                            pe.wait_ge(up_copied.sem, up_copied.at(b, u - 1))
                    if u == 0:
                        pe.wait_ge(x_low_ready.sem, x_low_ready.at(b, l + 1))
                    if c == 0:
                        pe.wait_ge(w_low_ready.sem, w_low_ready.at(b, l * E * FH + f + 1))
                    half = slice(c * BANK, (c + 1) * BANK)
                    for k, bank in enumerate((u % 2, 2 + u % 2)):
                        for part, (h, tokens) in enumerate(((0, x_high), (0, x_low), (1, x_high))):
                            mm = nc.tensor.matmul(ps[:, bank, :], w_split[:, f % 4, h, k * P:(k + 1) * P],
                                                  tokens[:, half], start=(part == 0), stop=(part == 2))
                    mm.then_inc(gu_ready.sem, 1)

                def down(u):
                    f, c = u // HALVES, u % HALVES
                    pe.wait_ge(h_ready.sem, h_ready.at(b, l * UNITS + u + 1))
                    nc.tensor.matmul(ps[:, 4 + c, :], w_down[l][:, f, :], ffn_h[u % 5], start=(l == 0 and f == 0),
                                     stop=(f == E * FH - 1)).then_inc(down_done.sem, 1)

                def down_biases():
                    pe.wait_ge(gateT_ready.sem, gateT_ready.at(b, 2))
                    for c in range(HALVES):
                        nc.tensor.matmul(ps[:, 4 + c, :], b_down[:, :], gate_wT[:, c * BANK:(c + 1) * BANK],
                                         start=True, stop=False)

                if l == 0:
                    pe.wait_ge(low_copied.sem, low_copied.at(b, TILES))
                    pe.wait_ge(high_copied.sem, high_copied.at(b, TILES))
                if l == 1:
                    for n in range(NT):
                        if n >= 2:
                            pe.wait_ge(z_ready.sem, z_ready.at(b, n - 1))
                        nc.tensor.matmul(ps[:, 6 + n % 2, 0:3 * D], xT[1][:, n * P:(n + 1) * P], w_qkv[:, :],
                                         start=True, stop=True).then_inc(qkv_mm.sem, 1)
                        if 3 <= n < 3 + EARLY_UNITS:
                            gate_up(n - 3)
                    gates_transpose(b, 1)
                for u in range(UNITS + DOWN_LAG):
                    if u < UNITS and not (l == 1 and u < EARLY_UNITS):
                        gate_up(u)
                    if l == 1 and u == DOWN_LAG:
                        down_biases()
                    if u >= DOWN_LAG:
                        down(u - DOWN_LAG)
                    if u < UNITS:
                        beside(u)
                for n in range(NT):
                    if n % 4 == 0:
                        pe.wait_ge(yT_ready.sem, yT_ready.at(b, 2 * l + n // 4 + 1))
                    mm = nc.tensor.transpose(ps[:, n // 4, (n % 4) * P:(n % 4 + 1) * P], y_T[:, n * P:(n + 1) * P],
                                             ident[:, :])
                    if n % 4 == 3:
                        mm.then_inc(y_mm.sem, 1)

            transpose_norm(None, 0, 6)
            key_projection(None, 0)
            with pe.Fori(0, BATCH) as index:
                b = Sequence(pe, index)
                def scores(t):
                    j, n = t % QUAD, (t // QUAD) % NT
                    if t == 0:
                        pe.wait_ge(keys_ready.sem, keys_ready.at(b, 0))
                    if n == 0:
                        pe.wait_ge(q_ready.sem, q_ready.at(b, (t // (NT * QUAD)) * QUAD + j + 1))
                    for c in range(HALVES):
                        for part in range(2):
                            mm = nc.tensor.matmul(ps[:, 2 * (t % 2) + c, :], q_parts[:, j, part, n * P:(n + 1) * P],
                                                  keys[:, c * BANK:(c + 1) * BANK], start=(part == 0),
                                                  stop=(part == 1))
                    mm.then_inc(scores_ready.sem, 1)

                def transpose_probs(t):
                    pe.wait_ge(exp_done.sem, exp_done.at(b, t + 1))
                    for c, (copied, done) in enumerate(((low_copied, pT_low), (high_copied, pT_high))):
                        if t >= 1:
                            pe.wait_ge(copied.sem, copied.at(b, t))
                        if t == 0 and c == 1:
                            pe.wait_ge(latent_ready.sem, latent_ready.at(b, 1))
                        if t == NT * QUAD:
                            pe.wait_ge(gateT_ready.sem, gateT_ready.at(b, 1))
                        for i in range(4):
                            k = 4 * c + i
                            mm = nc.tensor.transpose(ps[:, 4 + c, i * P:(i + 1) * P],
                                                     probs[:, t % 3, k * P:(k + 1) * P], ident[:, :])
                        mm.then_inc(done.sem, 1)

                def values(g, i):
                    if i == 0:
                        pe.wait_ge(low_copied.sem, low_copied.at(b, (g + 1) * QUAD))
                        pe.wait_ge(high_copied.sem, high_copied.at(b, (g + 1) * QUAD))
                        if g >= 2:
                            pe.wait_ge(o_added.sem, o_added.at(b, g - 1))
                    for k in (2 * i, 2 * i + 1):
                        for j in range(QUAD):
                            nc.tensor.matmul(ps[DC * j:DC * (j + 1), 6 + g % 2, 0:P], latent[:, k, :],
                                             probsT[:, (g % 2) * QUAD + j, k * P:(k + 1) * P],
                                             start=(k == 0), stop=(k == NT - 1))
                    if i == 3:
                        pe.wait_ge(inv_ready.sem, inv_ready.at(b, g + 1))
                        for j in range(QUAD):
                            mm = nc.tensor.matmul(ps[DC * j:DC * (j + 1), 6 + g % 2, P:2 * P],
                                                  inv_sum[:, g % 2, j:j + 1].to_broadcast([P, DC]), ident[:, :],
                                                  start=True, stop=True)
                        mm.then_inc(u_ready.sem, 1)

                def output(g):
                    pe.wait_ge(u_scaled.sem, u_scaled.at(b, g + 1))
                    nc.tensor.matmul(ps[:, 6 + g % 2, 2 * P:3 * P], o_latent[:, g % 2, :], w_o[:, g // NT, :],
                                     start=True, stop=True).then_inc(o_ready.sem, 1)

                def queries(h):
                    for c in range(HALVES):
                        mm = nc.tensor.matmul(ps[:, 2 * (h % 2) + c, :], w_q[:, h, :],
                                              xT[0][:, c * BANK:(c + 1) * BANK], start=True, stop=True)
                    mm.then_inc(q_proj.sem, 1)

                def attention_step(w):
                    before_h, before_t = use_of(w - 2)
                    if w == 0:
                        pe.wait_ge(y_added.sem, y_added.at(b, 0))
                    elif w == 1:
                        pass
                    elif w < STEPS and before_h is not None:
                        pe.wait_ge(q_ready.sem, q_ready.at(b, before_h + 1))
                    elif w < STEPS:
                        pe.wait_ge(exp_done.sem, exp_done.at(b, before_t + 1))
                    h, t = use_of(w)
                    if h is not None:
                        queries(h)
                    if w == 0:
                        for n in range(NT):
                            mm = nc.tensor.matmul(ps[:, 5, n * DC:(n + 1) * DC], xT[0][:, n * P:(n + 1) * P],
                                                  w_dkv[:, :], start=True, stop=True)
                        mm.then_inc(latent_mm.sem, 1)
                        router(b, 0, 5, NT * DC)
                    if t is not None:
                        scores(t)
                    t = use_of(w - T_LAG)[1]
                    if t is not None:
                        transpose_probs(t)
                    if w == GATES_STEP:
                        pe.wait_ge(low_copied.sem, low_copied.at(b, NT * QUAD))
                        pe.wait_ge(high_copied.sem, high_copied.at(b, NT * QUAD))
                        gates_transpose(b, 0)
                    g = group_at(w, OUTPUT_LAG)
                    if g is not None:
                        output(g)
                    for i in range(4):
                        g = group_at(w, VALUES_LAG + i)
                        if g is not None:
                            values(g, i)

                for w in range(UNIT_STEP):
                    attention_step(w)
                pe.wait_ge(exp_done.sem, exp_done.at(b, TILES))
                experts(b, 0, lambda u: attention_step(UNIT_STEP + u))

                transpose_norm(b, 1, 4)
                pe.wait_ge(xT_ready.sem, xT_ready.at(b, 2))
                router(b, 1, 4, 0)

                def flow_step(u):
                    if u == FLOW_SUMS:
                        pe.wait_ge(qk_ready.sem, qk_ready.at(b, 1))
                        for n in range(NT):
                            mm = nc.tensor.matmul(ps[:, 6, 0:2 * D], ones, qkv[:, n, 0:2 * D], start=(n == 0),
                                                  stop=(n == NT - 1))
                        mm.then_inc(sums_mm.sem, 1)
                    if u == FLOW_SUMS2:
                        pe.wait_ge(weighted_q.sem, weighted_q.at(b, 1))
                        pe.wait_ge(weighted_k.sem, weighted_k.at(b, 1))
                        for n in range(NT):
                            mm = nc.tensor.matmul(ps[:, 7, 0:2 * D], ones, weighted[:, n, :], start=(n == 0),
                                                  stop=(n == NT - 1))
                        mm.then_inc(sums_mm.sem, 1)
                    if u in (FLOW_SUMS2, FLOW_SUMS2 + 1):
                        c = u - FLOW_SUMS2
                        if c == 1:
                            pe.wait_ge(qnT_ready.sem, qnT_ready.at(b, 1))
                        for i in range(4):
                            mm = nc.tensor.transpose(ps[:, 6, i * P:(i + 1) * P], weighted[:, 4 * c + i, 0:D],
                                                     ident[:, :])
                        mm.then_inc(qnT_mm.sem, 1)
                    if u == FLOW_KV:
                        pe.wait_ge(xT_ready.sem, xT_ready.at(b, 4))
                        pe.wait_ge(v_ready.sem, v_ready.at(b, 1))
                        for n in range(NT):
                            nc.tensor.matmul(ps[:, 6, 0:D], qkv[:, n, D:2 * D], v_comp[:, n, :], start=(n == 0),
                                             stop=(n == NT - 1))
                        nc.tensor.matmul(ps[:, 7, 0:NT * H1], ones, source_exp, start=True, stop=True
                                         ).then_inc(kv_mm.sem, 1)
                    if u == FLOW_OUT:
                        pe.wait_ge(kv_ready.sem, kv_ready.at(b, 1))
                        pe.wait_ge(qnT_ready.sem, qnT_ready.at(b, 2))
                        for n in range(NT):
                            mm = nc.tensor.matmul(ps[:, 6 + n // 4, (n % 4) * D:(n % 4 + 1) * D],
                                                  q_normT[:, n * P:(n + 1) * P], kv, start=True, stop=True)
                            if n % 4 == 3:
                                mm.then_inc(heads_mm.sem, 1)
                    if u == FLOW_HEADS:
                        for n in range(NT):
                            if n % 4 == 0:
                                pe.wait_ge(heads_ready.sem, heads_ready.at(b, n // 4 + 1))
                            mm = nc.tensor.transpose(ps[:, 6 + n // 4, (n % 4) * P:(n % 4 + 1) * P],
                                                     heads_out[:, n, :], ident[:, :])
                            if n % 4 == 3:
                                mm.then_inc(headsT_mm.sem, 1)
                    if u == FLOW_PROJ:
                        pe.wait_ge(headsT_ready.sem, headsT_ready.at(b, 2))
                        for n in range(NT):
                            mm = nc.tensor.matmul(ps[:, 6 + n // 4, (n % 4) * D:(n % 4 + 1) * D],
                                                  heads_outT[:, n * P:(n + 1) * P], w_proj[:, :], start=True, stop=True)
                            if n % 4 == 3:
                                mm.then_inc(proj_mm.sem, 1)

                    if u == NEXT_TRANSPOSE:
                        pe.wait_ge(qnT_ready.sem, qnT_ready.at(b, 2))
                        pe.wait_ge(sums2_taken.sem, sums2_taken.at(b, 1))
                        transpose_norm(b, 0, 6)

                experts(b, 1, flow_step)
                pe.wait_ge(proj_added.sem, proj_added.at(b, 2))
                key_projection(b, 2)


def kernel(**inputs):
    import concourse.bacc as _bacc
    from concourse.bass_utils import run_bass_kernel_spmd as _run

    def get(name):
        return np.asarray(inputs[name])

    def head_T(w, heads):
        return w.reshape(w.shape[0], heads, -1).transpose(2, 1, 0)

    def stack(w, bias):
        return np.concatenate([w, bias[None, :]], axis=0)

    a0, a1, f0, f1 = "L0_attn_", "L1_attn_", "L0_ffn_", "L1_ffn_"
    key_w = np.concatenate([get(a0 + "W_DKV"), get(a0 + "W_KR")], axis=1)
    key_b = np.concatenate([get(a0 + "b_DKV"), get(a0 + "b_KR")])
    gu = get(f1 + "gate_up_proj")
    gu_b = get(f1 + "gate_up_proj_bias")

    def gate_up(gate, up):
        return np.stack([w.transpose(2, 0, 1).reshape(D, E * FH, P) for w in (gate, up)], axis=2)

    def down(w):
        return w.transpose(2, 0, 1).reshape(FH, P, E, D).transpose(1, 2, 0, 3).reshape(P, E * FH, D)

    def column(bias):
        return bias.reshape(E * FH, P).T

    arrays = {
        "x": get(a0 + "h_t"),
        "UQ_T": head_T(stack(get(a0 + "W_UQ"), get(a0 + "b_UQ")), H0),
        "UK_T": head_T(get(a0 + "W_UK"), H0),
        "UV_T": head_T(get(a0 + "W_UV"), H0),
        "W_O": get(a0 + "W_O").reshape(H0, DK, D).transpose(1, 0, 2),
        "b_UV": get(a0 + "b_UV").reshape(H0, DK).T,
        "DQ_T": get(a0 + "W_DQ").T,
        "b_DQ1": np.concatenate([get(a0 + "b_DQ"), np.ones(1, np.float32)])[:, None],
        "Q_rope": stack(get(a0 + "W_QR"), get(a0 + "b_QR")).reshape(DC + 1, H0, DR),
        "W_K": np.concatenate([key_w, key_w], axis=1),
        "b_K": np.concatenate([key_b, key_b])[:, None],
        "W_DKV": get(a0 + "W_DKV"),
        "gate_up0": gate_up(get(f0 + "w_gate"), get(f0 + "w_up")),
        "down0": down(get(f0 + "w_down")),
        "router0": get(f0 + "router_w").T,
        "W_QKV": get(a1 + "qkv_w").T,
        "W_PROJ": get(a1 + "proj_w").T,
        "gate_up1": gate_up(gu[:, 0:F, :], gu[:, F:2 * F, :]),
        "down1": down(get(f1 + "down_proj")),
        "router1": get(f1 + "router_weight").T,
        "b_gate": column(gu_b[:, 0:F]),
        "b_up": column(gu_b[:, F:2 * F]),
        "b_down": get(f1 + "down_proj_bias"),
        "b_DKV": get(a0 + "b_DKV"),
        "b_O": get(a0 + "b_O"),
        "b_QKV": get(a1 + "qkv_b"),
        "b_PROJ": get(a1 + "proj_b"),
        "b_ROUTER": get(f1 + "router_bias"),
    }
    nc = _bacc.Bacc("TRN2", target_bir_lowering=False, num_devices=1)
    arrays = {f"in_{k}": np.ascontiguousarray(v) for k, v in arrays.items()}
    ins = {k[3:]: nc.dram_tensor(k, v.shape, mybir.dt.from_np(v.dtype), kind="ExternalInput").ap()
           for k, v in arrays.items()}
    out = nc.dram_tensor("out", (BATCH, SEQ, D), F32, kind="ExternalOutput").ap()
    nc.disable_value_cache = True
    two_layer_kernel(nc, ins, out)
    r = _run(nc, [arrays], core_ids=[0])
    return r.results[0]["out"]
```
